# Optimizing a Trainium2 kernel written in Bass

```python
import numpy as np
import jax
import jax.numpy as jnp

def _softmax(x, axis=-1):
    return jax.nn.softmax(x, axis=axis)

def _gelu(x):
    return jax.nn.gelu(x, approximate=True)

def _silu(x):
    return jax.nn.silu(x)

def _sigmoid(x):
    return jax.nn.sigmoid(x)

def _layernorm(x, axis=-1, eps=1e-05):
    m = jnp.mean(x, axis=axis, keepdims=True)
    v = jnp.var(x, axis=axis, keepdims=True)
    return (x - m) / jnp.sqrt(v + eps)

def _scatter_add(tgt, idx, src, axis=0):
    return tgt.at[idx].add(src)

def _segment_sum(src, seg, n):
    return jax.ops.segment_sum(src, seg, n)
kernel_name = 'mk_flamingo_gated_d2_seqx_r4_d476da'

def setup_inputs(seed: int=0):
    np.random.seed(seed)
    _w = jnp.asarray

    def _rec_inputs():
        import jax
        import jax.numpy as jnp
        _rk = jax.random.key(seed)
        x = -0.0002928 + 1 * jax.random.normal(jax.random.fold_in(_rk, 1), (16, 112, 256), jnp.float32)
        _lenS = 112 - jax.random.randint(jax.random.fold_in(_rk, 7), (16,), 0, max(1, 112 // 4) + 1, jnp.int32)
        _lenS2 = 375 - jax.random.randint(jax.random.fold_in(_rk, 8), (16,), 0, max(1, 375 // 4) + 1, jnp.int32)
        _ctx_1024P = jax.random.normal(jax.random.fold_in(_rk, 11), (16, 16, 256), jnp.float32)
        _ctx_1024c = jax.random.dirichlet(jax.random.fold_in(_rk, 511), 0.3 * jnp.ones((16,), jnp.float32), (16, 375))
        _ctx_1024t = jnp.einsum('bsk,bkd->bsd', _ctx_1024c, _ctx_1024P)
        _ctx_1024t = _ctx_1024t * jax.lax.rsqrt(jnp.mean(jnp.square(_ctx_1024t)) + 1e-12) * 0.953939
        ctx_1024 = -1.39393e-06 + 0.999914 * (_ctx_1024t + 0.3 * jax.random.normal(jax.random.fold_in(_rk, 611), (16, 375, 256), jnp.float32))
        _validS = jnp.arange(112)[None, :] < _lenS[:, None]
        _validS2 = jnp.arange(375)[None, :] < _lenS2[:, None]
        _causal = jnp.tril(jnp.ones((112, 112), dtype=bool))
        mask_Bx1xSxS2_ff1 = jnp.where(jnp.ones((16, 1, 112, 375), dtype=bool), 1.0, 0.0).astype(jnp.float32)
        _g = jax.random.normal(jax.random.fold_in(_rk, 9001), (2, 2), jnp.float32)
        _g = jnp.sign(_g) * jnp.maximum(jnp.abs(_g), 1.0) + (_g == 0) * 1.0
        g_xattn = _g[0]
        g_ffn = _g[1]
        return (x, ctx_1024, mask_Bx1xSxS2_ff1, g_xattn, g_ffn)
    x, ctx_1024, mask_Bx1xSxS2_ff1, g_xattn, g_ffn = _rec_inputs()

    def _L0_xattn_setup():
        import jax, jax.numpy as jnp
        import numpy as np
        B, N, D_MODEL, H, DH = (2, 512, 256, 16, 64)
        SCALE = DH ** (-0.5)
        key = jax.random.key(seed)
        ks = jax.random.split(key, 6)

        def lin(k, fan_in, shape):
            return jax.random.normal(k, shape, dtype=jnp.float32) / np.sqrt(fan_in)
        return {'x': jax.random.normal(ks[0], (B, N, D_MODEL), dtype=jnp.float32), 'context': jax.random.normal(ks[1], (B, N, D_MODEL), dtype=jnp.float32), 'Wq': lin(ks[2], D_MODEL, (D_MODEL, H * DH)), 'Wk': lin(ks[3], D_MODEL, (D_MODEL, H * DH)), 'Wv': lin(ks[4], D_MODEL, (D_MODEL, H * DH)), 'Wo': lin(ks[5], H * DH, (H * DH, D_MODEL)), 'bo': jnp.zeros((D_MODEL,), dtype=jnp.float32)}
    _L0_xattn_all = _L0_xattn_setup()
    _L0_xattn_in = {k: v for k, v in _L0_xattn_all.items() if k in ('Wq', 'Wk', 'Wv', 'Wo', 'bo')}
    del _L0_xattn_all

    def _L0_ffn_setup():
        import jax, jax.numpy as jnp
        import numpy as np
        BLOCK = 32
        W_BITS = 4
        ACT_BITS = 16

        def act_qdq(x):
            qmax = 2.0 ** (ACT_BITS - 1) - 1.0
            scale = jnp.maximum(jnp.max(jnp.abs(x)) / qmax, 1e-12)
            return jnp.clip(jnp.round(x / scale), -qmax - 1.0, qmax) * scale

        def fixed_qdq_u16(x):
            scale = 1.0 / 65536.0
            return jnp.clip(jnp.round(x / scale), 0.0, 65535.0) * scale

        def lpbq_dequant(w):
            O, I = w.shape
            qmax = 2.0 ** (W_BITS - 1) - 1.0
            wb = w.reshape(O, I // BLOCK, BLOCK)
            s = jnp.maximum(jnp.max(jnp.abs(wb), axis=-1, keepdims=True) / qmax, 1e-12)
            wq = jnp.clip(jnp.round(wb / s), -qmax - 1.0, qmax) * s
            return wq.reshape(O, I)
        key = jax.random.key(seed)
        k1, k2, k3, k4 = jax.random.split(key, 4)
        B, S, H, I = (2, 1024, 256, 768)
        x = jax.random.normal(k1, (B, S, H), jnp.float32)
        w_gate = jax.random.normal(k2, (I, H), jnp.float32) * 0.02
        w_up = jax.random.normal(k3, (I, H), jnp.float32) * 0.02
        w_down = jax.random.normal(k4, (H, I), jnp.float32) * 0.02
        return {'x': x, 'w_gate': w_gate, 'w_up': w_up, 'w_down': w_down}
    _L0_ffn_all = _L0_ffn_setup()
    _L0_ffn_in = {k: v for k, v in _L0_ffn_all.items() if k in ('w_gate', 'w_up', 'w_down')}
    del _L0_ffn_all

    def _L1_xattn_setup():
        import jax, jax.numpy as jnp
        import numpy as np
        MODEL_SIZE = 256
        H = 16
        KEY_SIZE = MODEL_SIZE // H
        B, LQ, LK = (2, 512, 512)
        NEG_INF = -1000000000.0
        key = jax.random.key(seed)
        ks = jax.random.split(key, 10)
        s = 0.02
        return {'decoder_output': jax.random.normal(ks[0], (B, LQ, MODEL_SIZE), dtype=jnp.float32), 'encoder_output': jax.random.normal(ks[1], (B, LK, MODEL_SIZE), dtype=jnp.float32), 'mask': jnp.ones((B, 1, LQ, LK), dtype=jnp.float32), 'wq_w': jax.random.normal(ks[2], (MODEL_SIZE, MODEL_SIZE), dtype=jnp.float32) * s, 'wq_b': jnp.zeros((MODEL_SIZE,), dtype=jnp.float32), 'wk_w': jax.random.normal(ks[3], (MODEL_SIZE, MODEL_SIZE), dtype=jnp.float32) * s, 'wk_b': jnp.zeros((MODEL_SIZE,), dtype=jnp.float32), 'wv_w': jax.random.normal(ks[4], (MODEL_SIZE, MODEL_SIZE), dtype=jnp.float32) * s, 'wv_b': jnp.zeros((MODEL_SIZE,), dtype=jnp.float32), 'wo_w': jax.random.normal(ks[5], (MODEL_SIZE, MODEL_SIZE), dtype=jnp.float32) * s, 'wo_b': jnp.zeros((MODEL_SIZE,), dtype=jnp.float32)}
    _L1_xattn_all = _L1_xattn_setup()
    _L1_xattn_in = {k: v for k, v in _L1_xattn_all.items() if k in ('wq_w', 'wq_b', 'wk_w', 'wk_b', 'wv_w', 'wv_b', 'wo_w', 'wo_b')}
    del _L1_xattn_all

    def _L1_ffn_setup():
        import jax, jax.numpy as jnp
        import numpy as np
        D, H, O, E, TOPK = (256, 1024, 256, 8, 2)
        B, S = (4, 256)
        key = jax.random.key(seed)
        ks = jax.random.split(key, 12)
        std = 0.02
        return {'hidden_states': jax.random.normal(ks[0], (B, S, D), dtype=jnp.float32), 'norm_weight': jnp.ones((D,), dtype=jnp.float32), 'router_w': jax.random.normal(ks[1], (E, D), dtype=jnp.float32) * std, 'sw1': jax.random.normal(ks[2], (D, H), dtype=jnp.float32) * (1.0 / np.sqrt(D)), 'sb1': jnp.zeros((H,), dtype=jnp.float32), 'sw2': jax.random.normal(ks[3], (H, O), dtype=jnp.float32) * (1.0 / np.sqrt(H)), 'sb2': jnp.zeros((O,), dtype=jnp.float32), 'ew1': jax.random.normal(ks[4], (E, D, H), dtype=jnp.float32) * (1.0 / np.sqrt(D)), 'eb1': jnp.zeros((E, H), dtype=jnp.float32), 'ew2': jax.random.normal(ks[5], (E, H, O), dtype=jnp.float32) * (1.0 / np.sqrt(H)), 'eb2': jnp.zeros((E, O), dtype=jnp.float32)}
    _L1_ffn_all = _L1_ffn_setup()
    _L1_ffn_in = {k: v for k, v in _L1_ffn_all.items() if k in ('norm_weight', 'router_w', 'sw1', 'sb1', 'sw2', 'sb2', 'ew1', 'eb1', 'ew2', 'eb2')}
    del _L1_ffn_all
    return {'x': x, 'ctx_1024': ctx_1024, 'mask_Bx1xSxS2_ff1': mask_Bx1xSxS2_ff1, 'g_xattn': g_xattn, 'g_ffn': g_ffn, 'L0_xattn_Wq': _L0_xattn_in['Wq'], 'L0_xattn_Wk': _L0_xattn_in['Wk'], 'L0_xattn_Wv': _L0_xattn_in['Wv'], 'L0_xattn_Wo': _L0_xattn_in['Wo'], 'L0_xattn_bo': _L0_xattn_in['bo'], 'L0_ffn_w_gate': _L0_ffn_in['w_gate'], 'L0_ffn_w_up': _L0_ffn_in['w_up'], 'L0_ffn_w_down': _L0_ffn_in['w_down'], 'L1_xattn_wq_w': _L1_xattn_in['wq_w'], 'L1_xattn_wq_b': _L1_xattn_in['wq_b'], 'L1_xattn_wk_w': _L1_xattn_in['wk_w'], 'L1_xattn_wk_b': _L1_xattn_in['wk_b'], 'L1_xattn_wv_w': _L1_xattn_in['wv_w'], 'L1_xattn_wv_b': _L1_xattn_in['wv_b'], 'L1_xattn_wo_w': _L1_xattn_in['wo_w'], 'L1_xattn_wo_b': _L1_xattn_in['wo_b'], 'L1_ffn_norm_weight': _L1_ffn_in['norm_weight'], 'L1_ffn_router_w': _L1_ffn_in['router_w'], 'L1_ffn_sw1': _L1_ffn_in['sw1'], 'L1_ffn_sb1': _L1_ffn_in['sb1'], 'L1_ffn_sw2': _L1_ffn_in['sw2'], 'L1_ffn_sb2': _L1_ffn_in['sb2'], 'L1_ffn_ew1': _L1_ffn_in['ew1'], 'L1_ffn_eb1': _L1_ffn_in['eb1'], 'L1_ffn_ew2': _L1_ffn_in['ew2'], 'L1_ffn_eb2': _L1_ffn_in['eb2']}

def reference(x, ctx_1024, mask_Bx1xSxS2_ff1, g_xattn, g_ffn, L0_xattn_Wq, L0_xattn_Wk, L0_xattn_Wv, L0_xattn_Wo, L0_xattn_bo, L0_ffn_w_gate, L0_ffn_w_up, L0_ffn_w_down, L1_xattn_wq_w, L1_xattn_wq_b, L1_xattn_wk_w, L1_xattn_wk_b, L1_xattn_wv_w, L1_xattn_wv_b, L1_xattn_wo_w, L1_xattn_wo_b, L1_ffn_norm_weight, L1_ffn_router_w, L1_ffn_sw1, L1_ffn_sb1, L1_ffn_sw2, L1_ffn_sb2, L1_ffn_ew1, L1_ffn_eb1, L1_ffn_ew2, L1_ffn_eb2):
    import jax
    import jax.numpy as jnp

    def _L0_xattn_ref(x, context, Wq, Wk, Wv, Wo, bo):
        import jax, jax.numpy as jnp
        import numpy as np
        B, N, D_MODEL, H, DH = (2, 512, 256, 16, 64)
        SCALE = DH ** (-0.5)
        b, n, _ = x.shape
        m = context.shape[1]
        q = (x @ Wq).reshape(b, n, H, DH)
        k = (context @ Wk * SCALE).reshape(b, m, H, DH)
        v = (context @ Wv).reshape(b, m, H, DH)
        scores = jnp.einsum('bihd,bjhd->bhij', q, k)
        attn = jax.nn.softmax(scores, axis=-1)
        out = jnp.einsum('bhij,bjhd->bihd', attn, v)
        out = out.reshape(b, n, H * DH)
        return out @ Wo + bo

    def _L0_ffn_ref(x, w_gate, w_up, w_down):
        import jax, jax.numpy as jnp
        import numpy as np
        BLOCK = 32
        W_BITS = 4
        ACT_BITS = 16

        def act_qdq(x):
            qmax = 2.0 ** (ACT_BITS - 1) - 1.0
            scale = jnp.maximum(jnp.max(jnp.abs(x)) / qmax, 1e-12)
            return jnp.clip(jnp.round(x / scale), -qmax - 1.0, qmax) * scale

        def fixed_qdq_u16(x):
            scale = 1.0 / 65536.0
            return jnp.clip(jnp.round(x / scale), 0.0, 65535.0) * scale

        def lpbq_dequant(w):
            O, I = w.shape
            qmax = 2.0 ** (W_BITS - 1) - 1.0
            wb = w.reshape(O, I // BLOCK, BLOCK)
            s = jnp.maximum(jnp.max(jnp.abs(wb), axis=-1, keepdims=True) / qmax, 1e-12)
            wq = jnp.clip(jnp.round(wb / s), -qmax - 1.0, qmax) * s
            return wq.reshape(O, I)
        x = act_qdq(x)
        up = act_qdq(x @ lpbq_dequant(w_up).T)
        gate = act_qdq(x @ lpbq_dequant(w_gate).T)
        sig = fixed_qdq_u16(jax.nn.sigmoid(gate))
        gate = act_qdq(gate * sig)
        o = act_qdq(gate * up)
        return o @ lpbq_dequant(w_down).T

    def _L1_xattn_ref(decoder_output, encoder_output, mask, wq_w, wq_b, wk_w, wk_b, wv_w, wv_b, wo_w, wo_b):
        import jax, jax.numpy as jnp
        import numpy as np
        MODEL_SIZE = 256
        H = 16
        KEY_SIZE = MODEL_SIZE // H
        B, LQ, LK = (2, 512, 512)
        NEG_INF = -1000000000.0
        b = decoder_output.shape[0]
        q = decoder_output @ wq_w + wq_b
        k = encoder_output @ wk_w + wk_b
        v = encoder_output @ wv_w + wv_b
        q = q.reshape(b, -1, H, KEY_SIZE).transpose(0, 2, 1, 3)
        k = k.reshape(b, -1, H, KEY_SIZE).transpose(0, 2, 1, 3)
        v = v.reshape(b, -1, H, KEY_SIZE).transpose(0, 2, 1, 3)
        score = jnp.einsum('bhqd,bhkd->bhqk', q, k) / jnp.sqrt(jnp.asarray(KEY_SIZE, dtype=jnp.float32))
        score = score * mask
        score = jnp.where(score == 0, jnp.float32(NEG_INF), score)
        alignment = jax.nn.softmax(score, axis=-1)
        context = jnp.einsum('bhqk,bhkd->bhqd', alignment, v)
        context = context.transpose(0, 2, 1, 3).reshape(b, -1, H * KEY_SIZE)
        heads = context @ wo_w + wo_b
        return heads

    def _L1_ffn_ref(hidden_states, norm_weight, router_w, sw1, sb1, sw2, sb2, ew1, eb1, ew2, eb2):
        import jax, jax.numpy as jnp
        import numpy as np
        D, H, O, E, TOPK = (256, 1024, 256, 8, 2)
        B, S = (4, 256)
        b, s, d = hidden_states.shape
        var = jnp.mean(jnp.square(hidden_states), axis=-1, keepdims=True)
        normed = hidden_states * jax.lax.rsqrt(var + 1e-08) * norm_weight
        shared = jnp.maximum(normed @ sw1 + sb1, 0.0) @ sw2 + sb2
        flat = normed.reshape(-1, d)
        T = flat.shape[0]
        probs = jax.nn.sigmoid(flat @ router_w.T)
        scores, idx = jax.lax.top_k(probs, TOPK)
        w = scores / (jnp.sum(scores, axis=-1, keepdims=True) + 1e-06)
        comb = jnp.zeros((T, E), dtype=flat.dtype)
        comb = comb.at[jnp.arange(T)[:, None], idx].add(w)
        h = jnp.maximum(jnp.einsum('td,edh->teh', flat, ew1) + eb1[None, :, :], 0.0)
        eo = jnp.einsum('teh,eho->teo', h, ew2) + eb2[None, :, :]
        routed = jnp.einsum('teo,te->to', eo, comb)
        return shared + routed.reshape(b, s, -1)
    x = x + jnp.tanh(g_xattn[0]) * _L0_xattn_ref(_layernorm(x, axis=-1), ctx_1024, L0_xattn_Wq, L0_xattn_Wk, L0_xattn_Wv, L0_xattn_Wo, L0_xattn_bo)
    x = x + jnp.tanh(g_ffn[0]) * _L0_ffn_ref(_layernorm(x, axis=-1), L0_ffn_w_gate, L0_ffn_w_up, L0_ffn_w_down)
    x = x + jnp.tanh(g_xattn[1]) * _L1_xattn_ref(_layernorm(x, axis=-1), ctx_1024, mask_Bx1xSxS2_ff1, L1_xattn_wq_w, L1_xattn_wq_b, L1_xattn_wk_w, L1_xattn_wk_b, L1_xattn_wv_w, L1_xattn_wv_b, L1_xattn_wo_w, L1_xattn_wo_b)
    x = x + jnp.tanh(g_ffn[1]) * _L1_ffn_ref(_layernorm(x, axis=-1), L1_ffn_norm_weight, L1_ffn_router_w, L1_ffn_sw1, L1_ffn_sb1, L1_ffn_sw2, L1_ffn_sb2, L1_ffn_ew1, L1_ffn_eb1, L1_ffn_ew2, L1_ffn_eb2)
    return x

_drawn_inputs = setup_inputs


def setup_inputs(seed=0):
    import zlib

    import numpy as np

    out = dict(_drawn_inputs(seed))
    spreads = {'g_ffn': (-1.0, 0.2),
     'L0_xattn_bo': (0.0, 0.1),
     'L1_xattn_wq_b': (0.0, 0.8),
     'L1_xattn_wk_b': (0.0, 0.8),
     'L1_xattn_wv_b': (0.0, 0.1),
     'L1_xattn_wo_b': (0.0, 0.1),
     'L1_ffn_norm_weight': (1.0, 0.2),
     'L1_ffn_sb1': (0.0, 0.1),
     'L1_ffn_sb2': (0.0, 0.1),
     'L1_ffn_eb1': (0.0, 0.271),
     'L1_ffn_eb2': (0.0, 0.1)}
    factors = {'L1_xattn_wq_w': 6.138, 'L1_xattn_wk_w': 8.0}
    for name, (base, spread) in spreads.items():
        noise = np.random.default_rng([zlib.crc32(name.encode()), seed]).standard_normal(out[name].shape)
        drawn = base * np.exp(spread * noise) if base else spread * noise
        out[name] = jnp.asarray(drawn.astype(out[name].dtype))
    for name, factor in factors.items():
        out[name] = (out[name] * factor).astype(out[name].dtype)
    return out
```

```python
import concourse.bass as bass
from concourse import mybir
from contextlib import ExitStack

F32 = mybir.dt.float32
F16 = mybir.dt.float16
U32 = mybir.dt.uint32
ALU = mybir.AluOpType
ACT = mybir.ActivationFunctionType
AX = mybir.AxisListType

B, S, D, NC = 16, 112, 256, 375
T = B * S
KD = D // 128
NKV, KV = 3, 125
H = 16
DH0, DH1 = 64, 16
IN0 = H * DH0
CK0 = IN0 // 128
FF0 = 768
OC0 = FF0 // 128
FF1 = 1024
HC1 = FF1 // 128
E = 8
QBLK = 32
TG = 4
NG = B // TG
GW = TG * S
NP = H // 2

WS = 32.0
MAGIC = 12582912.0
QMAX = 32767.0
UQ = 65536.0


def wait(eng, sem, n):
    if not (isinstance(n, int) and n <= 0):
        eng.wait_ge(sem, n)


class Chain:

    def __init__(self, eng, sem):
        self.eng, self.sem, self.n = eng, sem, 0

    def __call__(self, instruction):
        self.n += 1
        instruction.then_inc(self.sem, 1)
        self.eng.wait_ge(self.sem, self.n)


def make_allocators(nc, ctx):
    def sb(name, shape, dt=F32):
        return ctx.enter_context(nc.sbuf_tensor(name, shape, dt))

    def ps(name, shape, dt=F32):
        return ctx.enter_context(nc.psum_tensor(name, shape, dt))

    def sem(name):
        return ctx.enter_context(nc.semaphore(name))

    return sb, ps, sem


def setup_phase(nc, A, x_res, ident32, ident16, gates, tanh_g):
    with ExitStack() as ctx:
        sb, ps, sem = make_allocators(nc, ctx)
        x_in, g_in, zeroed, made = sem("x_in"), sem("g_in"), sem("id_zeroed"), sem("id_made")
        tanh_done = sem("tanh_done")
        block = ctx.enter_context(nc.Block())

        @block.sync
        def _(sp):
            sp.dma_start(x_res[:], A["x"].rearrange("(t p) d -> p t d", p=S)).then_inc(x_in, 16)
            for i, name in enumerate(("g_xattn", "g_ffn")):
                sp.dma_start(gates[:, 2 * i:2 * i + 2], A[name].partition_broadcast(128)).then_inc(g_in, 16)
            sp.wait_ge(x_in, 16)

        @block.gpsimd
        def _(pool):
            for m in (ident32, ident16):
                nc.gpsimd.memset(m[:], 0.0).then_inc(zeroed, 1)
            pool.wait_ge(zeroed, 2)
            for m in (ident32, ident16):
                nc.gpsimd.affine_select(out=m[:], in_=m[:], compare_op=ALU.not_equal, fill=1.0, base=0,
                                        pattern=[[-1, 128]], channel_multiplier=1).then_inc(made, 1)

        @block.scalar
        def _(act):
            act.wait_ge(g_in, 32)
            nc.scalar.activation(tanh_g[:], gates[:], ACT.Tanh).then_inc(tanh_done, 1)


def norm_phase(nc, tag, x_res, ident32, xh, xl, n_out=None, rms_w=None, quant=None):
    with ExitStack() as ctx:
        sb, ps, sem = make_allocators(nc, ctx)
        stats = sb(f"{tag}_stats", [S, B, 6])
        mv = sb(f"{tag}_mv", [S, B, 2])
        eps = sb(f"{tag}_eps", [S, 1])
        var = sb(f"{tag}_var", [S, B])
        std = sb(f"{tag}_std", [S, B])
        rstd = sb(f"{tag}_rstd", [S, B])
        tmp = sb(f"{tag}_tmp", [S, B])
        xn = n_out if n_out is not None else sb(f"{tag}_xn", [S, B, D])
        amax = sb(f"{tag}_amax", [128, 2])
        tp = ps(f"{tag}_tp", [128, 4, 512])
        chain, var_ready, std_ready = sem(f"{tag}_chain"), sem(f"{tag}_var_ready"), sem(f"{tag}_std_ready")
        xn_ready, transposed, hi_done, lo_done = (sem(f"{tag}_{n}") for n in
                                                  ("xn_ready", "transposed", "hi_done", "lo_done"))
        amax_part, amax_all = sem(f"{tag}_amax_part"), sem(f"{tag}_amax_all")
        norms = 1 if rms_w is None else 2
        block = ctx.enter_context(nc.Block())

        @block.vector
        def _(dve):
            link = Chain(dve, chain)

            def statistics(src, epsilon, ms):
                for t in range(B):
                    last = nc.vector.bn_stats(stats[:, t, :], src[:, t, :])
                link(last)
                for t in range(B):
                    last = nc.vector.bn_aggr(mv[:, t, :], stats[:, t, :])
                link(last)
                if ms:
                    link(nc.vector.tensor_tensor(tmp[:], mv[:, :, 0], mv[:, :, 0], ALU.mult))
                    link(nc.vector.tensor_tensor(tmp[:], tmp[:], mv[:, :, 1], ALU.add))
                    link(nc.vector.tensor_scalar(var[:], tmp[:], epsilon, None, ALU.add))
                else:
                    link(nc.vector.tensor_scalar(var[:], mv[:, :, 1], epsilon, None, ALU.add))
                nc.vector.tensor_copy(tmp[:], var[:]).then_inc(var_ready, 1)
                dve.wait_ge(std_ready, 2 if ms else 1)
                link(nc.vector.reciprocal(rstd[:], std[:]))
                link(nc.vector.tensor_tensor(tmp[:], rstd[:], rstd[:], ALU.mult))
                link(nc.vector.tensor_tensor(tmp[:], tmp[:], var[:], ALU.mult))
                link(nc.vector.tensor_scalar(tmp[:], tmp[:], -0.5, 1.5, ALU.mult, ALU.add))
                link(nc.vector.tensor_tensor(rstd[:], rstd[:], tmp[:], ALU.mult))

            nc.vector.memset(amax[:], 0.0)
            statistics(x_res, 1e-5, False)
            for t in range(B):
                last = nc.vector.tensor_scalar(xn[:, t, :], x_res[:, t, :], mv[:, t, 0:1], rstd[:, t:t + 1],
                                               ALU.subtract, ALU.mult)
                if norms == 1 and quant is None:
                    last.then_inc(xn_ready, 1)
            if norms == 2:
                link(last)
                statistics(xn, 1e-8, True)
                for t in range(B):
                    nc.vector.scalar_tensor_tensor(out=xn[:, t, :], in0=xn[:, t, :], scalar=rstd[:, t:t + 1],
                                                   in1=rms_w[:], op0=ALU.mult, op1=ALU.mult).then_inc(xn_ready, 1)
            if quant is not None:
                scale, inv = quant
                link(last)
                nc.vector.tensor_reduce(amax[0:S, 0:1], xn[:], AX.XY, ALU.max,
                                        apply_absolute_value=True).then_inc(amax_part, 1)
                dve.wait_ge(amax_all, 1)
                link(nc.vector.tensor_scalar(scale[:], amax[:, 1:2], 1.0 / QMAX, 1e-12, ALU.mult, ALU.max))
                link(nc.vector.reciprocal(inv[:], scale[:]))
                link(nc.vector.tensor_scalar(xn[:], xn[:], inv[0:S, :], MAGIC, ALU.mult, ALU.add))
                nc.vector.tensor_scalar(xn[:], xn[:], -MAGIC, None, ALU.add).then_inc(xn_ready, B)
            for j in range(NG * KD):
                g, k = j // KD, j % KD
                dve.wait_ge(hi_done, j + 1)
                nc.vector.tensor_tensor(xl[:, k, g * GW:(g + 1) * GW], tp[:, j % 4, 0:GW],
                                        xh[:, k, g * GW:(g + 1) * GW], ALU.subtract).then_inc(lo_done, 1)

        @block.gpsimd
        def _(pool):
            if quant is not None:
                pool.wait_ge(amax_part, 1)
                nc.gpsimd.partition_all_reduce(amax[:, 1:2], amax[:, 0:1], 128,
                                               bass.bass_isa.ReduceOp.max).then_inc(amax_all, 1)

        @block.scalar
        def _(act):
            for n in range(norms):
                act.wait_ge(var_ready, n + 1)
                nc.scalar.activation(std[:], var[:], ACT.Sqrt).then_inc(std_ready, 1)
            for j in range(NG * KD):
                g, k = j // KD, j % KD
                act.wait_ge(transposed, j + 1)
                nc.scalar.activation(xh[:, k, g * GW:(g + 1) * GW], tp[:, j % 4, 0:GW],
                                     ACT.Copy).then_inc(hi_done, 1)

        @block.tensor
        def _(pe):
            for j in range(NG * KD):
                g, k = j // KD, j % KD
                pe.wait_ge(xn_ready, TG * (g + 1))
                if j >= 4:
                    pe.wait_ge(lo_done, j - 3)
                for i in range(TG):
                    last = nc.tensor.transpose(tp[:, j % 4, i * S:(i + 1) * S],
                                               xn[:, g * TG + i, k * 128:(k + 1) * 128], ident32[0:S, 0:S])
                last.then_inc(transposed, 1)


def split_phase(nc, tag, loads, stage_cols):
    with ExitStack() as ctx:
        sb, ps, sem = make_allocators(nc, ctx)
        stage = sb(f"{tag}_stage", [128, 2, stage_cols])
        arrived = [sem(f"{tag}_arrived{i}") for i in range(2)]
        hi_done, lo_done = sem(f"{tag}_hi_done"), sem(f"{tag}_lo_done")
        block = ctx.enter_context(nc.Block())

        @block.sync
        def _(sp):
            for i, (src, hi, lo) in enumerate(loads):
                if i >= 2:
                    sp.wait_ge(lo_done, i - 1)
                sp.dma_start(stage[:, i % 2, 0:hi.free_size()].rearrange("p (a b) -> p a b", a=src.shape[1]),
                             src).then_inc(arrived[i % 2], 16)

        @block.scalar
        def _(act):
            for i, (src, hi, lo) in enumerate(loads):
                act.wait_ge(arrived[i % 2], 16 * (i // 2 + 1))
                nc.scalar.activation(hi, stage[:, i % 2, 0:hi.free_size()], ACT.Copy, scale=WS).then_inc(hi_done, 1)

        @block.vector
        def _(dve):
            for i, (src, hi, lo) in enumerate(loads):
                dve.wait_ge(hi_done, i + 1)
                nc.vector.scalar_tensor_tensor(out=lo, in0=stage[:, i % 2, 0:hi.free_size()], scalar=WS, in1=hi,
                                               op0=ALU.mult, op1=ALU.subtract).then_inc(lo_done, 1)


def flat(ap):
    return ap.rearrange("p a b -> p (a b)")


def products(nc, out, pairs):
    n = len(pairs)
    for i, (wh, wl, mh, ml) in enumerate(pairs):
        nc.tensor.matmul(out, wh, mh, start=(i == 0), stop=False)
        nc.tensor.matmul(out, wh, ml, start=False, stop=False)
        last = nc.tensor.matmul(out, wl, mh, start=False, stop=(i == n - 1))
    return last


def attention0_phase(nc, A, x_res, xh, xl, ident32, ident16, tanh_g):
    SC = float(DH0) ** -0.5 / (WS * WS)
    with ExitStack() as ctx:
        sb, ps, sem = make_allocators(nc, ctx)
        wq, wk, wv = (sb(f"a0_{n}", [128, 2, KD, IN0], F16) for n in ("wq", "wk", "wv"))
        wo = sb("a0_wo", [128, 2, CK0, D], F16)
        split_phase(nc, "a0w", [
            (A[n][k * 128:(k + 1) * 128, :].rearrange("p (a b) -> p a b", a=1), w[:, 0, k, :], w[:, 1, k, :])
            for n, w in (("L0_xattn_Wk", wk), ("L0_xattn_Wq", wq), ("L0_xattn_Wv", wv)) for k in range(KD)
        ] + [
            (A["L0_xattn_Wo"].rearrange("(k p) n -> p k n", p=128)[:, 4 * k:4 * k + 4, :],
             flat(wo[:, 0, 4 * k:4 * k + 4, :]), flat(wo[:, 1, 4 * k:4 * k + 4, :])) for k in range(CK0 // 4)
        ], IN0)

        bo = sb("a0_bo", [S, D])
        bo_g = sb("a0_bo_g", [S, D])
        gate = sb("a0_gate", [S, 1])
        ctx32 = sb("a0_ctx32", [128, KD, NC])
        ch, cl = sb("a0_ch", [128, KD, NC], F16), sb("a0_cl", [128, KD, NC], F16)
        ks = sb("a0_ks", [128, H, NC], F16)
        qs = sb("a0_qs", [128, H, 2, S], F16)
        vh, vl = sb("a0_vh", [KV, NKV, IN0], F16), sb("a0_vl", [KV, NKV, IN0], F16)
        p32 = sb("a0_p32", [S, 2, 2, NC])
        ph, pl = sb("a0_ph", [S, 4, 2, NC], F16), sb("a0_pl", [S, 4, 2, NC], F16)
        pt = sb("a0_pt", [KV, 4, 2, NKV, 128], F16)
        mx, nb = sb("a0_mx", [S, 2, 2]), sb("a0_nb", [S, 2, 2])
        rsum, rinv = sb("a0_rsum", [S, H]), sb("a0_rinv", [S, H])
        on = sb("a0_on", [S, IN0])
        oth, otl = sb("a0_oth", [128, CK0, S], F16), sb("a0_otl", [128, CK0, S], F16)
        ps_s = ps("a0_ps_s", [128, 2, 512])
        ps_t = ps("a0_ps_t", [128, 2, 1024], F16)
        ps_o = ps("a0_ps_o", [128, 2, 512])
        ps_j = ps("a0_ps_j", [128, 2, 512])

        names = ("ctx_in", "bo_in", "pt_zeroed", "ctx_hi", "ctx_lo", "scored", "max_ready", "exp_done", "ph_done",
                 "pl_done", "p_transposed", "pt_ready", "pv_done", "job_done", "job_hi", "job_lo", "o_ready",
                 "wo_done", "x_done", "chain", "p_chain")
        (ctx_in, bo_in, pt_zeroed, ctx_hi, ctx_lo, scored, max_ready, exp_done, ph_done, pl_done, p_transposed,
         pt_ready, pv_done, job_done, job_hi, job_lo, o_ready, wo_done, x_done, chain, p_chain) = (
            sem(f"a0_{n}") for n in names)

        FIRST = ["V00", "V01", "V02"] + [f"K{p}" for p in range(NP)] + ["Q0", "Q1"]
        BODY = ["V10", "V11", "V12", "K0", "K1", "K2", "K3", "Q0", "K4", "K5", "K6", "K7", "Q1",
                "V00", "V01", "OT0", "OT1", "V02"]
        LAST = ["V10", "V11", "V12", "OT0", "OT1"]
        block = ctx.enter_context(nc.Block())

        def order(engine, last):
            out, late = [], []
            for p in range(NP + 3):
                js = []
                if p == 0:
                    js = ["V10", "V11"]
                if p == 1:
                    js = ["V12"]
                if 2 <= p < NP + 2 and not last:
                    js = [f"K{p - 2}"] + ["Q0"] * (p == 5) + ["Q1"] * (p == 9)
                if p == NP + 2 and not last:
                    js = ["V00"]
                js = [("J", n) for n in js]
                if p < NP:
                    out.append(("S", p))
                if engine == "act":
                    out += js + [("H", p)] * (p < NP)
                if engine == "dve" and p < 2:
                    out += js
                if p == 1 and not last:
                    out += [("J", "V12"), ("C", None)] if engine == "pe" else [("C", None)]
                elif engine == "pe" and p < 2:
                    out += js
                if 2 <= p < NP + 2:
                    out.append(("T", p - 2))
                if engine == "pe" and p >= 2:
                    out += js
                if engine == "dve" and p >= 2:
                    out += late
                    late = js
                if p >= 3:
                    out.append(("P", p - 3))
                if p == 7:
                    out.append(("O", 0))
            if engine == "dve":
                out += late
            out.append(("O", 1))
            out += [("J", n) for n in (["OT0", "OT1"] if last else ["V01", "OT0", "OT1", "V02"])]
            out.append(("W", None))
            return out

        def batches(eng, body):
            body(0, False)
            with eng.Fori(1, B - 1) as b:
                body(b, False)
            body(B - 1, True)

        def job_number(b, last, name):
            return b * len(BODY) + (len(FIRST) + (LAST if last else BODY).index(name))

        def job_bank(last, name):
            n = len(FIRST) + (LAST if last else BODY).index(name)
            return ((B - 1) * len(BODY) + n if last else n) % 2

        @block.sync
        def _(sp):
            sp.dma_start(bo[:], A["L0_xattn_bo"].partition_broadcast(S)).then_inc(bo_in, 16)
            sp.dma_start(ctx32[:], A["ctxT"][:, :, 0:NC].rearrange("k p n -> p k n")).then_inc(ctx_in, 16)
            with sp.Fori(1, B) as b:
                sp.wait_ge(ctx_lo, b)
                sp.dma_start(ctx32[:], A["ctxT"][:, :, bass.ds(b * NC, NC)].rearrange("k p n -> p k n")
                             ).then_inc(ctx_in, 16)

        @block.tensor
        def _(pe):
            def project(name, bank, b_q):
                if name[0] == "V":
                    c, t = int(name[1]), int(name[2])
                    last = products(nc, ps_j[0:KV, bank, :], [
                        (ch[:, k, t * KV:(t + 1) * KV], cl[:, k, t * KV:(t + 1) * KV],
                         wv[:, 0, k, c * 512:(c + 1) * 512], wv[:, 1, k, c * 512:(c + 1) * 512])
                        for k in range(KD)])
                elif name[0] == "K":
                    p = int(name[1])
                    last = products(nc, ps_j[:, bank, 0:NC], [
                        (wk[:, 0, k, p * 128:(p + 1) * 128], wk[:, 1, k, p * 128:(p + 1) * 128],
                         ch[:, k, :], cl[:, k, :]) for k in range(KD)])
                elif name[0] == "Q":
                    for i in range(4):
                        p = 4 * int(name[1]) + i
                        last = products(nc, ps_j[:, bank, i * S:(i + 1) * S], [
                            (wq[:, 0, k, p * 128:(p + 1) * 128], wq[:, 1, k, p * 128:(p + 1) * 128],
                             xh[:, k, bass.ds(b_q * S, S)], xl[:, k, bass.ds(b_q * S, S)]) for k in range(KD)])
                else:
                    for i in range(4):
                        k = 4 * int(name[2]) + i
                        last = nc.tensor.transpose(ps_j[:, bank, i * S:(i + 1) * S], on[:, k * 128:(k + 1) * 128],
                                                   ident32[0:S, 0:S])
                last.then_inc(job_done, 1)

            for n, name in enumerate(FIRST):
                if n == 0:
                    wait(pe, ctx_lo, 1)
                if n >= 2:
                    wait(pe, job_lo, n - 1)
                project(name, n % 2, 0)
            wait(pe, job_lo, len(FIRST))

            def body(b, last):
                for what, arg in order("pe", last):
                    if what == "S":
                        for i in range(2):
                            h = 2 * arg + i
                            if arg == 0 and i == 0:
                                wait(pe, job_lo, b * len(BODY) + (len(FIRST) - (len(BODY) - BODY.index("V00"))))
                            wait(pe, exp_done, b * H + max(h - 1, 0))
                            for part in range(2):
                                mm = nc.tensor.matmul(ps_s[0:S, i, 0:NC], qs[:, h, part, :], ks[:, h, :],
                                                      start=(part == 0), stop=(part == 1))
                            mm.then_inc(scored, 1)
                    elif what == "T":
                        wait(pe, pl_done, b * NP + (arg + 1))
                        for i in range(2):
                            h = 2 * arg + i
                            wait(pe, pt_ready, b * H + max(h - 1, 0))
                            for part, src in enumerate((ph, pl)):
                                for t in range(NKV):
                                    c = (part * NKV + t) * S
                                    mm = nc.tensor.transpose(ps_t[0:KV, i, c:c + S],
                                                             src[:, arg % 4, i, t * KV:(t + 1) * KV],
                                                             ident16[0:S, 0:S])
                            mm.then_inc(p_transposed, 1)
                    elif what == "P":
                        for i in range(2):
                            h = 2 * arg + i
                            wait(pe, pt_ready, b * H + (h + 1))
                            if h == 0:
                                wait(pe, job_lo, b * len(BODY) + len(FIRST))
                                wait(pe, o_ready, b * 2)
                                wait(pe, x_done, b)
                            if h == 8:
                                wait(pe, job_lo, job_number(b, last, "V12") + 1)
                            c = (h % 8) * DH0
                            hc = slice(h * DH0, (h + 1) * DH0)
                            mm = products(nc, ps_o[:, h // 8, c:c + DH0], [
                                (pt[:, h % 4, 0, t, :], pt[:, h % 4, 1, t, :], vh[:, t, hc], vl[:, t, hc])
                                for t in range(NKV)])
                            mm.then_inc(pv_done, 1)
                    elif what == "J":
                        n = job_number(b, last, arg)
                        wait(pe, job_lo, n - 1)
                        if arg == "K0":
                            wait(pe, ctx_lo, b + 2)
                        if arg == "OT0":
                            wait(pe, o_ready, b * 2 + 2)
                        project(arg, job_bank(last, arg), b + 1)
                    elif what == "W":
                        wait(pe, job_lo, job_number(b, last, "OT1") + 1)
                        mm = products(nc, ps_o[0:S, 0, 0:D], [
                            (oth[:, k, :], otl[:, k, :], wo[:, 0, k, :], wo[:, 1, k, :]) for k in range(CK0)])
                        mm.then_inc(wo_done, 1)

            batches(pe, body)

        @block.scalar
        def _(act):
            def split_context(b):
                wait(act, ctx_in, 16 * b + 16)
                nc.scalar.activation(ch[:], ctx32[:], ACT.Copy).then_inc(ctx_hi, 1)

            def evacuate(name, bank, number):
                wait(act, job_done, number + 1)
                if name[0] == "V":
                    c, t = int(name[1]), int(name[2])
                    last = nc.scalar.activation(vh[:, t, c * 512:(c + 1) * 512], ps_j[0:KV, bank, :], ACT.Copy)
                elif name[0] == "K":
                    p = int(name[1])
                    for i in range(2):
                        r = slice(64 * i, 64 * i + 64)
                        last = nc.scalar.activation(ks[r, 2 * p + i, :], ps_j[r, bank, 0:NC], ACT.Copy)
                elif name[0] == "Q":
                    p = int(name[1])
                    for i in range(2):
                        r = slice(64 * i, 64 * i + 64)
                        last = nc.scalar.activation(
                            qs[r, 8 * p + i:8 * p + 8:2, 0, :],
                            ps_j[r, bank, 0:4 * S].rearrange("p (h s) -> p h s", h=4), ACT.Copy)
                else:
                    k = 4 * int(name[2])
                    last = nc.scalar.activation(flat(oth[:, k:k + 4, :]), ps_j[:, bank, 0:4 * S], ACT.Copy)
                last.then_inc(job_hi, 1)

            split_context(0)
            for n, name in enumerate(FIRST):
                evacuate(name, n % 2, n)

            def body(b, last):
                for what, arg in order("act", last):
                    if what == "S":
                        wait(act, max_ready, b * NP + (arg + 1))
                        wait(act, pl_done, b * NP + max(arg - 1, 0))
                        for i in range(2):
                            h = 2 * arg + i
                            nc.scalar.activation(p32[:, arg % 2, i, :], ps_s[0:S, i, 0:NC], ACT.Exp,
                                                 bias=nb[:, arg % 2, i:i + 1], scale=SC,
                                                 accum_out=rsum[:, h:h + 1]).then_inc(exp_done, 1)
                    elif what == "H":
                        wait(act, exp_done, b * H + (2 * arg + 2))
                        if arg >= 4:
                            wait(act, p_transposed, b * H + 2 * (arg - 3))
                        else:
                            wait(act, p_transposed, b * H)
                        nc.scalar.activation(ph[:, arg % 4, :, :], p32[:, arg % 2, :, :], ACT.Copy
                                             ).then_inc(ph_done, 1)
                    elif what == "C":
                        wait(act, job_done, job_number(b, last, "V12") + 1)
                        split_context(b + 1)
                    elif what == "J":
                        evacuate(arg, job_bank(last, arg), job_number(b, last, arg))

            batches(act, body)

        @block.gpsimd
        def _(pool):
            def low(b, p):
                pool.wait_ge(ph_done, b * NP + (p + 1))
                nc.gpsimd.tensor_tensor(pl[:, p % 4, :, :], p32[:, p % 2, :, :], ph[:, p % 4, :, :],
                                        ALU.subtract).then_inc(pl_done, 1)

            nc.gpsimd.memset(pt[:], 0.0).then_inc(pt_zeroed, 1)
            with pool.Fori(0, B) as b:
                for p in range(NP):
                    low(b, p)

        @block.vector
        def _(dve):
            link = Chain(dve, chain)
            wait(dve, bo_in, 16)
            nc.vector.tensor_copy(gate[:], tanh_g[0:S, 0:1])
            link(nc.vector.tensor_scalar(bo_g[:], bo[:], tanh_g[0:S, 0:1], None, ALU.mult))
            link(nc.vector.tensor_scalar(gate[:], tanh_g[0:S, 0:1], 1.0 / (WS * WS), None, ALU.mult))

            def split_context(b):
                wait(dve, ctx_hi, b + 1)
                nc.vector.tensor_tensor(cl[:], ctx32[:], ch[:], ALU.subtract).then_inc(ctx_lo, 1)

            def evacuate(name, bank, number, dup_wait):
                wait(dve, job_hi, number + 1)
                if name[0] == "V":
                    c, t = int(name[1]), int(name[2])
                    cc = slice(c * 512, (c + 1) * 512)
                    last = nc.vector.tensor_tensor(vl[:, t, cc], ps_j[0:KV, bank, :], vh[:, t, cc], ALU.subtract)
                elif name[0] == "K":
                    p = int(name[1])
                    for i in range(2):
                        r, o = slice(64 * i, 64 * i + 64), slice(64 - 64 * i, 128 - 64 * i)
                        last = nc.vector.tensor_tensor(ks[o, 2 * p + i, :], ps_j[r, bank, 0:NC],
                                                       ks[r, 2 * p + i, :], ALU.subtract)
                elif name[0] == "Q":
                    p = int(name[1])
                    for i in range(2):
                        r = slice(64 * i, 64 * i + 64)
                        hh = slice(8 * p + i, 8 * p + 8, 2)
                        last = nc.vector.tensor_tensor(
                            qs[r, hh, 1, :], ps_j[r, bank, 0:4 * S].rearrange("p (h s) -> p h s", h=4),
                            qs[r, hh, 0, :], ALU.subtract)
                    last.then_inc(p_chain, 1)
                    wait(dve, p_chain, dup_wait)
                    for i in range(2):
                        r, o = slice(64 * i, 64 * i + 64), slice(64 - 64 * i, 128 - 64 * i)
                        hh = slice(8 * p + i, 8 * p + 8, 2)
                        last = nc.vector.tensor_copy(qs[o, hh, :, :], qs[r, hh, :, :])
                else:
                    k = 4 * int(name[2])
                    last = nc.vector.tensor_tensor(flat(otl[:, k:k + 4, :]), ps_j[:, bank, 0:4 * S],
                                                   flat(oth[:, k:k + 4, :]), ALU.subtract)
                last.then_inc(job_lo, 1)

            split_context(0)
            for n, name in enumerate(FIRST):
                evacuate(name, n % 2, n, 1 + (name == "Q1"))
            wait(dve, pt_zeroed, 1)
            n0 = link.n

            def body(b, last):
                c = 0

                def chained(instruction):
                    nonlocal c
                    c += 1
                    instruction.then_inc(chain, 1)
                    wait(dve, chain, b * (NP + 3) + (n0 + c))

                for what, arg in order("dve", last):
                    if what == "S":
                        for i in range(2):
                            h = 2 * arg + i
                            wait(dve, scored, b * H + (h + 1))
                            ins = nc.vector.reduce_max(mx[:, arg % 2, i:i + 1], ps_s[0:S, i, 0:NC], AX.X)
                        chained(ins)
                        nc.vector.tensor_scalar(nb[:, arg % 2, :], mx[:, arg % 2, :], -SC, None, ALU.mult
                                                ).then_inc(max_ready, 1)
                    elif what == "T":
                        for i in range(2):
                            h = 2 * arg + i
                            wait(dve, p_transposed, b * H + (h + 1))
                            wait(dve, pv_done, b * H + max(h - 3, 0))
                            nc.vector.tensor_copy(
                                pt[:, h % 4, :, :, 0:S].rearrange("p a t s -> p (a t) s"),
                                ps_t[0:KV, i, 0:2 * NKV * S].rearrange("p (a s) -> p a s", a=2 * NKV)
                            ).then_inc(pt_ready, 1)
                    elif what == "C":
                        split_context(b + 1)
                    elif what == "O":
                        hh = slice(8 * arg, 8 * arg + 8)
                        wait(dve, exp_done, b * H + 8 * arg + 8)
                        chained(nc.vector.reciprocal(rinv[:, hh], rsum[:, hh]))
                        wait(dve, pv_done, b * H + (8 * arg + 8))
                        nc.vector.tensor_tensor(
                            on[:, 512 * arg:512 * arg + 512].rearrange("p (h d) -> p h d", h=8),
                            ps_o[0:S, arg, :].rearrange("p (h d) -> p h d", h=8),
                            rinv[:, hh].unsqueeze(2).to_broadcast([S, 8, DH0]), ALU.mult).then_inc(o_ready, 1)
                    elif what == "J":
                        evacuate(arg, job_bank(last, arg), job_number(b, last, arg),
                                 b * 2 + (3 + (arg == "Q1")))
                    elif what == "W":
                        xb = x_res[:, bass.ds(b, 1), :].rearrange("p a d -> p (a d)")
                        chained(nc.vector.tensor_tensor(xb, xb, bo_g[:], ALU.add))
                        wait(dve, wo_done, b + 1)
                        ins = nc.vector.scalar_tensor_tensor(out=xb, in0=ps_o[0:S, 0, 0:D], scalar=gate[:],
                                                             in1=xb, op0=ALU.mult, op1=ALU.add)
                        ins.then_inc(x_done, 1)

            batches(dve, body)


def feed_forward0_phase(nc, A, x_res, xh, xl, sx, ident32, tanh_g):
    with ExitStack() as ctx:
        sb, ps, sem = make_allocators(nc, ctx)
        wup, wgt = (sb(f"f0_{n}", [128, 2, KD, FF0], F16) for n in ("wup", "wgt"))
        wdn = sb("f0_wdn", [128, 2, OC0, D], F16)
        quantise_weights(nc, A, wup, wgt, wdn, ident32)

        U, G = sb("f0_U", [128, OC0, T]), sb("f0_G", [128, OC0, T])
        sg_t = sb("f0_sig", [128, 2, T])
        m_c = sb("f0_mc", [128, 1])
        mx = sb("f0_mx", [128, 8])
        am = sb("f0_am", [128, 8])
        sc = sb("f0_sc", [128, 16])
        oh, ol = sb("f0_oh", [128, 2, OC0, GW], F16), sb("f0_ol", [128, 2, OC0, GW], F16)
        pj = ps("f0_pj", [128, 6, 512])
        po = ps("f0_po", [128, 2, 512])
        names = ("job_done", "copied", "reduced", "mx_part", "mx_all", "chain", "scal", "g_rounded", "g_int", "sig_done",
                 "u_rounded", "t_done", "g2_rounded", "w_done", "o_rounded", "o_split", "down_done", "x_done")
        (job_done, copied, reduced, mx_part, mx_all, chain, scal, g_rounded, g_int, sig_done, u_rounded, t_done,
         g2_rounded, w_done, o_rounded, o_split, down_done, x_done) = (sem(f"f0_{n}") for n in names)
        NJ = 2 * OC0
        KU = 1.0 / WS
        block = ctx.enter_context(nc.Block())

        @block.tensor
        def _(pe):
            def group(g):
                for j in range(NJ):
                    w, o = (wup, wgt)[j // OC0], j % OC0
                    wait(pe, copied, g * NJ + (j - 5))
                    mm = products(nc, pj[:, j % 6, 0:GW], [
                        (w[:, 0, k, o * 128:(o + 1) * 128], w[:, 1, k, o * 128:(o + 1) * 128],
                         xh[:, k, bass.ds(g * GW, GW)], xl[:, k, bass.ds(g * GW, GW)]) for k in range(KD)])
                    mm.then_inc(job_done, 1)

            group(0)
            with pe.Fori(1, NG) as g:
                group(g)
            for t in range(B):
                g = t // TG
                pe.wait_ge(o_split, g + 1)
                if t >= 2:
                    pe.wait_ge(x_done, t - 1)
                i = t % TG
                mm = products(nc, po[0:S, t % 2, 0:D], [
                    (oh[:, g % 2, o, i * S:(i + 1) * S], ol[:, g % 2, o, i * S:(i + 1) * S],
                     wdn[:, 0, o, :], wdn[:, 1, o, :]) for o in range(OC0)])
                mm.then_inc(down_done, 1)

        def gate_sigmoid(act, o):
            act.wait_ge(g_int, o + 1)
            if o >= 2:
                act.wait_ge(t_done, o - 1)
            nc.scalar.activation(sg_t[:, o % 2, :], G[:, o, :], ACT.Sigmoid, scale=sc[:, 3:4]).then_inc(sig_done, 1)

        @block.scalar
        def _(act):
            with act.Fori(0, NG) as g:
                for j in range(NJ):
                    dst, o = (U, G)[j // OC0], j % OC0
                    act.wait_ge(job_done, g * NJ + (j + 1))
                    nc.scalar.activation(dst[:, o, bass.ds(g * GW, GW)], pj[:, j % 6, 0:GW], ACT.Copy
                                         ).then_inc(copied, 1)
            act.wait_ge(scal, 1)
            for o in range(OC0):
                nc.scalar.activation(G[:, o, :], G[:, o, :], ACT.Identity, bias=m_c[:], scale=sc[:, 2:3]
                                     ).then_inc(g_rounded, 1)
                if o >= 1:
                    gate_sigmoid(act, o - 1)
                nc.scalar.activation(U[:, o, :], U[:, o, :], ACT.Identity, bias=m_c[:], scale=sc[:, 1:2]
                                     ).then_inc(u_rounded, 1)
            gate_sigmoid(act, OC0 - 1)
            act.wait_ge(scal, 2)
            for o in range(OC0):
                nc.scalar.activation(G[:, o, :], G[:, o, :], ACT.Identity, bias=m_c[:], scale=sc[:, 5:6]
                                     ).then_inc(g2_rounded, 1)
            act.wait_ge(scal, 3)
            for g in range(NG):
                cc = slice(g * GW, (g + 1) * GW)
                nc.scalar.activation(G[:, :, cc], G[:, :, cc], ACT.Identity, bias=m_c[:], scale=sc[:, 7:8]
                                     ).then_inc(o_rounded, 1)

        @block.gpsimd
        def _(pool):
            for n in range(3):
                k = 2 if n == 0 else 1
                pool.wait_ge(mx_part, n + 1)
                c = (0, 2, 3)[n]
                nc.gpsimd.partition_all_reduce(am[:, c:c + k], mx[:, c:c + k], 128, bass.bass_isa.ReduceOp.max
                                               ).then_inc(mx_all, 1)

        def gated(dve, link, o, omx):
            dve.wait_ge(sig_done, o + 1)
            st = sg_t[:, o % 2, :]
            link(nc.vector.tensor_scalar(st, st, UQ, MAGIC, ALU.mult, ALU.add))
            link(nc.vector.tensor_scalar(st, st, -MAGIC, UQ - 1.0, ALU.add, ALU.min))
            nc.vector.tensor_tensor(G[:, o, :], st, G[:, o, :], ALU.mult).then_inc(t_done, 1)
            dve.wait_ge(t_done, o + 1)
            link(nc.vector.tensor_reduce(omx[:, 0, o:o + 1], G[:, o, :], AX.X, ALU.max, apply_absolute_value=True))

        def add_down(dve, g, gate):
            for t in range(g * TG, (g + 1) * TG):
                dve.wait_ge(down_done, t + 1)
                nc.vector.scalar_tensor_tensor(out=x_res[:, t, :], in0=po[0:S, t % 2, 0:D], scalar=gate[:],
                                               in1=x_res[:, t, :], op0=ALU.mult, op1=ALU.add).then_inc(x_done, 1)

        @block.vector
        def _(dve):
            link = Chain(dve, chain)
            gmx = sb("f0_gmx", [128, NG, 2])
            omx = sb("f0_omx", [128, 2, OC0])
            gate = sb("f0_gate", [S, 1])
            nc.vector.memset(m_c[:], MAGIC)
            with dve.Fori(0, NG) as g:
                for i, src in enumerate((U, G)):
                    dve.wait_ge(copied, g * NJ + (i + 1) * OC0)
                    nc.vector.tensor_reduce(gmx[:, bass.ds(g, 1), i:i + 1].rearrange("p a b -> p (a b)"),
                                            src[:, :, bass.ds(g * GW, GW)], AX.XY, ALU.max,
                                            apply_absolute_value=True).then_inc(reduced, 1)
            dve.wait_ge(reduced, 2 * NG)
            nc.vector.tensor_reduce(mx[:, 0:2], gmx[:].rearrange("p g i -> p i g"), AX.X, ALU.max
                                    ).then_inc(mx_part, 1)
            dve.wait_ge(mx_all, 1)

            def scale_of(raw_max, unit, scale, inv):
                link(nc.vector.tensor_tensor(sc[:, 15:16], raw_max, unit, ALU.mult))
                link(nc.vector.tensor_scalar(scale, sc[:, 15:16], 1.0 / QMAX, 1e-12, ALU.mult, ALU.max))
                link(nc.vector.reciprocal(sc[:, 14:15], scale))
                link(nc.vector.tensor_tensor(inv, sc[:, 14:15], unit, ALU.mult))

            link(nc.vector.tensor_scalar(sc[:, 0:1], sx[:], KU, None, ALU.mult))
            scale_of(am[:, 0:1], sc[:, 0:1], sc[:, 4:5], sc[:, 1:2])
            scale_of(am[:, 1:2], sc[:, 0:1], sc[:, 3:4], sc[:, 2:3])
            nc.vector.tensor_scalar(sc[:, 9:10], sc[:, 3:4], 1.0 / UQ, None, ALU.mult).then_inc(scal, 1)
            for o in range(OC0):
                dve.wait_ge(g_rounded, o + 1)
                nc.vector.tensor_scalar(G[:, o, :], G[:, o, :], -MAGIC, None, ALU.add).then_inc(g_int, 1)
                if o >= 1:
                    gated(dve, link, o - 1, omx)
            gated(dve, link, OC0 - 1, omx)
            nc.vector.tensor_reduce(mx[:, 2:3], omx[:, 0, :], AX.X, ALU.max).then_inc(mx_part, 1)
            dve.wait_ge(mx_all, 2)
            scale_of(am[:, 2:3], sc[:, 9:10], sc[:, 6:7], sc[:, 5:6])
            nc.vector.tensor_tensor(sc[:, 10:11], sc[:, 6:7], sc[:, 4:5], ALU.mult).then_inc(scal, 1)
            for o in range(OC0):
                dve.wait_ge(g2_rounded, o + 1)
                link(nc.vector.tensor_scalar(G[:, o, :], G[:, o, :], -MAGIC, None, ALU.add))
                dve.wait_ge(u_rounded, o + 1)
                nc.vector.scalar_tensor_tensor(out=G[:, o, :], in0=U[:, o, :], scalar=-MAGIC, in1=G[:, o, :],
                                               op0=ALU.add, op1=ALU.mult).then_inc(w_done, 1)
                dve.wait_ge(w_done, o + 1)
                last = nc.vector.tensor_reduce(omx[:, 1, o:o + 1], G[:, o, :], AX.X, ALU.max,
                                               apply_absolute_value=True)
            link(last)
            nc.vector.tensor_reduce(mx[:, 3:4], omx[:, 1, :], AX.X, ALU.max).then_inc(mx_part, 1)
            dve.wait_ge(mx_all, 3)
            scale_of(am[:, 3:4], sc[:, 10:11], sc[:, 8:9], sc[:, 7:8])
            link(nc.vector.tensor_scalar(gate[:], sc[0:S, 8:9], tanh_g[0:S, 2:3], KU, ALU.mult, ALU.mult))
            nc.vector.tensor_copy(sc[:, 11:12], sc[:, 10:11]).then_inc(scal, 1)
            for g in range(NG):
                cc = slice(g * GW, (g + 1) * GW)
                dve.wait_ge(o_rounded, g + 1)
                if g >= 2:
                    dve.wait_ge(down_done, TG * (g - 1))
                link(nc.vector.tensor_scalar(oh[:, g % 2, :, :], G[:, :, cc], -MAGIC, None, ALU.add))
                nc.vector.scalar_tensor_tensor(out=ol[:, g % 2, :, :], in0=G[:, :, cc], scalar=-MAGIC,
                                               in1=oh[:, g % 2, :, :], op0=ALU.add, op1=ALU.subtract
                                               ).then_inc(o_split, 1)
                if g >= 1:
                    add_down(dve, g - 1, gate)
            add_down(dve, NG - 1, gate)


def quantise_weights(nc, A, wup, wgt, wdn, ident32):
    NU, ND = OC0 * D, KD * FF0
    NW = 2 * NU + ND
    with ExitStack() as ctx:
        sb, ps, sem = make_allocators(nc, ctx)
        w = sb("qw_w", [128, NW])
        q = sb("qw_q", [128, NW])
        bmax, bscale, binv = (sb(f"qw_{n}", [128, NW // QBLK]) for n in ("bmax", "bscale", "binv"))
        tp = ps("qw_tp", [128, 4, 512])
        w_in, chain, ready, transposed, hi_done, lo_done = (sem(f"qw_{n}") for n in (
            "w_in", "chain", "ready", "transposed", "hi_done", "lo_done"))
        groups = []
        for m, dst in enumerate((wup, wgt)):
            for k in range(KD):
                for o0 in range(0, OC0, 3):
                    groups.append((dst, k, o0 * 128, [m * NU + o * D + k * 128 for o in range(o0, o0 + 3)]))
        for k in range(OC0):
            groups.append((wdn, k, 0, [2 * NU + o * FF0 + k * 128 for o in range(KD)]))
        block = ctx.enter_context(nc.Block())

        @block.sync
        def _(sp):
            sp.dma_start(w[:, 0:NU].rearrange("p (o d) -> p o d", o=OC0),
                         A["L0_ffn_w_up"].rearrange("(o p) d -> p o d", p=128)).then_inc(w_in, 16)
            sp.dma_start(w[:, NU:2 * NU].rearrange("p (o d) -> p o d", o=OC0),
                         A["L0_ffn_w_gate"].rearrange("(o p) d -> p o d", p=128)).then_inc(w_in, 16)
            sp.dma_start(w[:, 2 * NU:NW].rearrange("p (o d) -> p o d", o=KD),
                         A["L0_ffn_w_down"].rearrange("(o p) d -> p o d", p=128)).then_inc(w_in, 16)

        @block.vector
        def _(dve):
            link = Chain(dve, chain)
            blocks = lambda a: a[:].rearrange("p (n b) -> p n b", b=QBLK)
            spread = lambda a: a[:].unsqueeze(2).to_broadcast([128, NW // QBLK, QBLK])
            dve.wait_ge(w_in, 48)
            link(nc.vector.tensor_reduce(bmax[:], blocks(w), AX.X, ALU.max, apply_absolute_value=True))
            link(nc.vector.tensor_scalar(bscale[:], bmax[:], 1.0 / 7.0, 1e-12, ALU.mult, ALU.max))
            link(nc.vector.reciprocal(binv[:], bscale[:]))
            link(nc.vector.tensor_tensor(blocks(q), blocks(w), spread(binv), ALU.mult))
            link(nc.vector.tensor_scalar(q[:], q[:], MAGIC, None, ALU.add))
            link(nc.vector.tensor_scalar(q[:], q[:], -MAGIC, 7.0, ALU.add, ALU.min))
            nc.vector.tensor_tensor(blocks(q), blocks(q), spread(bscale), ALU.mult).then_inc(ready, 1)
            for n, (dst, k, c0, srcs) in enumerate(groups):
                dve.wait_ge(hi_done, n + 1)
                cc = slice(c0, c0 + 128 * len(srcs))
                nc.vector.scalar_tensor_tensor(out=dst[:, 1, k, cc], in0=tp[:, n % 4, 0:128 * len(srcs)], scalar=WS,
                                               in1=dst[:, 0, k, cc], op0=ALU.mult, op1=ALU.subtract
                                               ).then_inc(lo_done, 1)

        @block.tensor
        def _(pe):
            pe.wait_ge(ready, 1)
            for n, (dst, k, c0, srcs) in enumerate(groups):
                if n >= 4:
                    pe.wait_ge(lo_done, n - 3)
                for i, s in enumerate(srcs):
                    mm = nc.tensor.transpose(tp[:, n % 4, i * 128:(i + 1) * 128], q[:, s:s + 128], ident32[:])
                mm.then_inc(transposed, 1)

        @block.scalar
        def _(act):
            for n, (dst, k, c0, srcs) in enumerate(groups):
                act.wait_ge(transposed, n + 1)
                nc.scalar.activation(dst[:, 0, k, c0:c0 + 128 * len(srcs)], tp[:, n % 4, 0:128 * len(srcs)],
                                     ACT.Copy, scale=WS).then_inc(hi_done, 1)


def attention1_phase(nc, A, x_res, xh, xl, ident32, ident16, tanh_g):
    SC = float(DH1) ** -0.5 / (WS * WS)
    FILL = -1.0e9 / SC
    HG = 8
    with ExitStack() as ctx:
        sb, ps, sem = make_allocators(nc, ctx)
        wq, wk, wv, wo = (sb(f"a1_{n}", [128, 2, KD, D], F16) for n in ("wq", "wk", "wv", "wo"))
        split_phase(nc, "a1w", [
            (A[f"L1_xattn_{n}_w"].rearrange("(k p) n -> p k n", p=128), flat(w[:, 0]), flat(w[:, 1]))
            for n, w in (("wk", wk), ("wq", wq), ("wv", wv), ("wo", wo))], KD * D)

        maskt = sb("a1_mask", [S, B, NC])
        bias_in = sb("a1_bias_in", [128, 3, KD])
        bias = sb("a1_bias", [128, 3, KD])
        bo, bo_g = sb("a1_bo", [S, D]), sb("a1_bo_g", [S, D])
        gate = sb("a1_gate", [S, 1])
        own = sb("a1_own", [128, HG], F16)
        ctx32 = sb("a1_ctx32", [128, KD, NC])
        ch, cl = sb("a1_ch", [128, KD, NC], F16), sb("a1_cl", [128, KD, NC], F16)
        kh, kl = sb("a1_kh", [128, KD, NC], F16), sb("a1_kl", [128, KD, NC], F16)
        q2 = sb("a1_q2", [128, KD, 2, S], F16)
        qm = sb("a1_qm", [128, H, 2, S], F16)
        vh, vl = sb("a1_vh", [KV, NKV, D], F16), sb("a1_vl", [KV, NKV, D], F16)
        s1, fill = sb("a1_s1", [S, 2, NC]), sb("a1_fill", [S, 2, NC])
        s2 = sb("a1_s2", [S, 2, 2, NC])
        p32 = sb("a1_p32", [S, 2, 2, NC])
        ph, pl = sb("a1_ph", [S, 4, 2, NC], F16), sb("a1_pl", [S, 4, 2, NC], F16)
        pt = sb("a1_pt", [KV, 4, 2, NKV, 128], F16)
        mx, nb = sb("a1_mx", [S, 2, 2]), sb("a1_nb", [S, 2, 2])
        rsum, rinv = sb("a1_rsum", [S, B * H]), sb("a1_rinv", [S, H])
        on = sb("a1_on", [S, D])
        oth, otl = sb("a1_oth", [128, KD, S], F16), sb("a1_otl", [128, KD, S], F16)
        ps_s = ps("a1_ps_s", [128, 2, 512])
        ps_t = ps("a1_ps_t", [128, 2, 1024], F16)
        ps_o = ps("a1_ps_o", [128, 512])
        ps_w = ps("a1_ps_w", [128, 512])
        ps_j = ps("a1_ps_j", [128, 2, 512])

        names = ("small_in", "mask_in", "ctx_in", "pt_zeroed", "own_made", "ctx_hi", "ctx_lo", "scored", "masked",
                 "max_ready", "exp_done", "ph_done", "pl_done", "p_transposed", "pt0_ready", "pt1_ready", "pv_done",
                 "job_done", "job_hi", "job_lo", "qm_ready", "o_ready", "wo_done", "x_done", "chain", "bias_ready")
        (small_in, mask_in, ctx_in, pt_zeroed, own_made, ctx_hi, ctx_lo, scored, masked, max_ready, exp_done,
         ph_done, pl_done, p_transposed, pt0_ready, pt1_ready, pv_done, job_done, job_hi, job_lo, qm_ready,
         o_ready, wo_done, x_done, chain, bias_ready) = (sem(f"a1_{n}") for n in names)

        def steps(engine, first, last):
            out = []
            for p in range(NP):
                lag2 = [("T", p - 2) if p >= 2 else ("T'", NP + p - 2)] if p >= 2 or not first else []
                lag3 = [("P", p - 3) if p >= 3 else ("P'", NP + p - 3)] if p >= 3 or not first else []
                if engine == "act":
                    out += lag2
                out.append(("S", p))
                if engine == "pe":
                    out += lag2
                if p == 3 and not first:
                    out.append(("J", "OT"))
                if p == 4 and not last:
                    out += [("J", "K0"), ("J", "Q0")]
                out += lag3
                if p == 2:
                    if not first:
                        out.append(("O'", None))
                    out += [("J", "V0"), ("J", "V1"), ("J", "V2")]
                    if not last:
                        out.append(("C", None))
                if p == 3 and not first:
                    out.append(("W'", None))
                if p == 7 and not last:
                    out += [("J", "K1"), ("J", "Q1")]
                if engine == "act":
                    out.append(("H", p))
                if engine == "dve":
                    out[out.index(("S", p))] = ("S", p, lag2)
            return out

        TAIL = [("P'", 5), ("T'", 6), ("P'", 6), ("T'", 7), ("P'", 7), ("O'", None), ("J", "OT"), ("W'", None)]
        FIRST = ["K0", "Q0", "K1", "Q1"]
        jobs = [a for w, a in steps("pe", False, False) if w == "J"]
        NJ = len(jobs)
        jobs0 = [a for w, a in steps("pe", True, False) if w == "J"]
        N0 = len(FIRST) + len(jobs0)
        jobs_last = [a for w, a in steps("pe", False, True) if w == "J"]

        def job_number(b, kind, name):
            if kind == "first":
                return len(FIRST) + jobs0.index(name)
            if kind == "tail":
                return N0 + (B - 2) * NJ + len(jobs_last)
            return b * NJ + (N0 - NJ + (jobs_last if kind == "last" else jobs).index(name))

        def bank_of(kind, name):
            return job_number(0 if kind == "mid" else B - 1, kind, name) % 2

        def walk(eng, engine, body):
            body(0, "first", steps(engine, True, False))
            with eng.Fori(1, B - 1) as b:
                body(b, "mid", steps(engine, False, False))
            body(B - 1, "last", steps(engine, False, True))
            body(B, "tail", TAIL)

        def copy_probabilities(copy, h, i):
            return copy(pt[:, h % 4, :, :, 0:S].rearrange("p a t s -> p (a t) s"),
                        ps_t[0:KV, i, 0:2 * NKV * S].rearrange("p (a s) -> p a s", a=2 * NKV))

        block = ctx.enter_context(nc.Block())

        @block.sync
        def _(sp):
            sp.dma_start(ctx32[:], A["ctxT"][:, :, 0:NC].rearrange("k p n -> p k n")).then_inc(ctx_in, 16)
            sp.dma_start(bias_in[:], A["L1_qkv_bT"]).then_inc(small_in, 16)
            sp.dma_start(bo[:], A["L1_xattn_wo_b"].partition_broadcast(S)).then_inc(small_in, 16)
            sp.dma_start(maskt[:], A["mask"].rearrange("b s n -> s b n")).then_inc(mask_in, 16)
            with sp.Fori(1, B) as b:
                sp.wait_ge(ctx_lo, b)
                sp.dma_start(ctx32[:], A["ctxT"][:, :, bass.ds(b * NC, NC)].rearrange("k p n -> p k n")
                             ).then_inc(ctx_in, 16)

        @block.tensor
        def _(pe):
            def project(name, bank, b_next):
                i = int(name[1]) if name != "OT" else 0
                if name[0] == "V":
                    last = products(nc, ps_j[0:KV, bank, 0:D], [
                        (ch[:, k, i * KV:(i + 1) * KV], cl[:, k, i * KV:(i + 1) * KV], wv[:, 0, k, :], wv[:, 1, k, :])
                        for k in range(KD)])
                elif name[0] == "K":
                    last = products(nc, ps_j[:, bank, 0:NC], [
                        (wk[:, 0, k, i * 128:(i + 1) * 128], wk[:, 1, k, i * 128:(i + 1) * 128],
                         ch[:, k, :], cl[:, k, :]) for k in range(KD)])
                elif name[0] == "Q":
                    last = products(nc, ps_j[:, bank, 0:S], [
                        (wq[:, 0, k, i * 128:(i + 1) * 128], wq[:, 1, k, i * 128:(i + 1) * 128],
                         xh[:, k, bass.ds(b_next * S, S)], xl[:, k, bass.ds(b_next * S, S)]) for k in range(KD)])
                else:
                    for k in range(KD):
                        last = nc.tensor.transpose(ps_j[:, bank, k * S:(k + 1) * S], on[:, k * 128:(k + 1) * 128],
                                                   ident32[0:S, 0:S])
                last.then_inc(job_done, 1)

            wait(pe, ctx_lo, 1)
            for n, name in enumerate(FIRST):
                if n >= 2:
                    wait(pe, job_lo, n - 1)
                project(name, n % 2, 0)

            def body(b, kind, order):
                for what, arg in order:
                    bb = b - 1 if "'" in what else b
                    if what == "S":
                        if arg % 4 == 0:
                            wait(pe, qm_ready, b * 2 + (1 + arg // 4))
                            if kind == "first":
                                wait(pe, job_lo, 1 + 2 * (arg // 4))
                            elif arg == 0:
                                wait(pe, job_lo, b * NJ + (N0 - NJ))
                        for i in range(2):
                            h = 2 * arg + i
                            wait(pe, masked, b * NP + arg)
                            for n, (part, keys) in enumerate(((0, kh), (0, kl), (1, kh))):
                                last = nc.tensor.matmul(ps_s[0:S, i, 0:NC], qm[:, h, part, :], keys[:, h // HG, :],
                                                        start=(n == 0), stop=(n == 2))
                            last.then_inc(scored, 1)
                    elif what[0] == "T":
                        wait(pe, pl_done, bb * NP + (arg + 1))
                        for i in range(2):
                            wait(pe, (pt0_ready, pt1_ready)[i], bb * NP + arg)
                            for part, src in enumerate((ph, pl)):
                                for t in range(NKV):
                                    c = (part * NKV + t) * S
                                    mm = nc.tensor.transpose(ps_t[0:KV, i, c:c + S],
                                                             src[:, arg % 4, i, t * KV:(t + 1) * KV],
                                                             ident16[0:S, 0:S])
                            mm.then_inc(p_transposed, 1)
                    elif what[0] == "P":
                        if arg == 0:
                            wait(pe, job_lo, job_number(b, kind, "V2") + 1)
                            if kind != "first":
                                wait(pe, o_ready, b)
                        for i in range(2):
                            h = 2 * arg + i
                            wait(pe, (pt0_ready, pt1_ready)[i], bb * NP + (arg + 1))
                            hc = slice(h * DH1, (h + 1) * DH1)
                            mm = products(nc, ps_o[:, hc], [
                                (pt[:, h % 4, 0, t, :], pt[:, h % 4, 1, t, :], vh[:, t, hc], vl[:, t, hc])
                                for t in range(NKV)])
                            mm.then_inc(pv_done, 1)
                    elif what == "J":
                        n = job_number(b, kind, arg)
                        wait(pe, job_lo, n - 1)
                        if arg == "K0":
                            wait(pe, ctx_lo, b + 2)
                        if arg == "OT":
                            wait(pe, o_ready, b)
                        project(arg, bank_of(kind, arg), b + 1)
                    elif what[0] == "W":
                        wait(pe, job_lo, job_number(b, kind, "OT") + 1)
                        if kind != "first":
                            wait(pe, x_done, b - 1)
                        mm = products(nc, ps_w[0:S, 0:D], [
                            (oth[:, k, :], otl[:, k, :], wo[:, 0, k, :], wo[:, 1, k, :]) for k in range(KD)])
                        mm.then_inc(wo_done, 1)

            walk(pe, "pe", body)

        @block.scalar
        def _(act):
            wait(act, small_in, 32)
            nc.scalar.mul(bias[:], bias_in[:], WS).then_inc(bias_ready, 1)
            wait(act, bias_ready, 1)

            def split_context(b):
                wait(act, ctx_in, 16 * b + 16)
                nc.scalar.activation(ch[:], ctx32[:], ACT.Copy).then_inc(ctx_hi, 1)

            def evacuate(name, bank, number, copies=None):
                wait(act, job_done, number + 1)
                i = int(name[1]) if name != "OT" else 0
                if name[0] == "V":
                    nc.scalar.activation(vh[:, i, :], ps_j[0:KV, bank, 0:D], ACT.Copy).then_inc(job_hi, 1)
                elif name[0] == "K":
                    nc.scalar.activation(kh[:, i, :], ps_j[:, bank, 0:NC], ACT.Identity, bias=bias[:, 1, i:i + 1]
                                         ).then_inc(job_hi, 1)
                elif name[0] == "Q":
                    if copies is not None:
                        wait(act, qm_ready, copies)
                    nc.scalar.activation(q2[:, i, 0, :], ps_j[:, bank, 0:S], ACT.Identity, bias=bias[:, 0, i:i + 1]
                                         ).then_inc(job_hi, 1)
                else:
                    for k in range(KD):
                        last = nc.scalar.activation(oth[:, k, :], ps_j[:, bank, k * S:(k + 1) * S], ACT.Identity,
                                                    bias=bias[:, 2, k:k + 1])
                    last.then_inc(job_hi, 1)

            split_context(0)
            for n, name in enumerate(FIRST):
                evacuate(name, n % 2, n)

            def body(b, kind, order):
                for what, arg in order:
                    bb = b - 1 if "'" in what else b
                    if what == "S":
                        wait(act, max_ready, b * NP + (arg + 1))
                        if not (kind == "first" and arg < 2):
                            wait(act, pl_done, b * NP + (arg - 1))
                        for i in range(2):
                            h = 2 * arg + i
                            nc.scalar.activation(p32[:, arg % 2, i, :], s2[:, arg % 2, i, :], ACT.Exp,
                                                 bias=nb[:, arg % 2, i:i + 1], scale=SC,
                                                 accum_out=rsum[:, bass.ds(b * H + h, 1)]).then_inc(exp_done, 1)
                    elif what == "H":
                        wait(act, exp_done, b * H + (2 * arg + 2))
                        if not (kind == "first" and arg < 4):
                            wait(act, p_transposed, b * H + 2 * (arg - 3))
                        nc.scalar.activation(ph[:, arg % 4, :, :], p32[:, arg % 2, :, :], ACT.Copy
                                             ).then_inc(ph_done, 1)
                    elif what[0] == "T":
                        h = 2 * arg + 1
                        wait(act, p_transposed, bb * H + (h + 1))
                        if not (kind == "first" and h < 4):
                            wait(act, pv_done, bb * H + (h - 3))
                        copy_probabilities(nc.scalar.copy, h, 1).then_inc(pt1_ready, 1)
                    elif what == "C":
                        wait(act, job_done, job_number(b, kind, "V2") + 1)
                        split_context(b + 1)
                    elif what == "J":
                        evacuate(arg, bank_of(kind, arg), job_number(b, kind, arg),
                                 b * 2 + (1 + (arg == "Q1")) if arg[0] == "Q" else None)

            walk(act, "act", body)

        @block.gpsimd
        def _(pool):
            nc.gpsimd.memset(pt[:], 0.0).then_inc(pt_zeroed, 1)
            nc.gpsimd.memset(own[:], 1.0).then_inc(own_made, 1)
            wait(pool, own_made, 1)
            nc.gpsimd.affine_select(out=own[:], in_=own[:], compare_op=ALU.is_ge, fill=0.0, base=0,
                                    pattern=[[-DH1, HG]], channel_multiplier=1).then_inc(own_made, 1)
            wait(pool, own_made, 2)
            nc.gpsimd.affine_select(out=own[:], in_=own[:], compare_op=ALU.is_ge, fill=0.0, base=DH1 - 1,
                                    pattern=[[DH1, HG]], channel_multiplier=-1).then_inc(own_made, 1)
            wait(pool, own_made, 3)

            def own_rows(g, number):
                wait(pool, job_lo, number + 1)
                nc.gpsimd.tensor_tensor(
                    qm[:, g * HG:(g + 1) * HG, :, :].rearrange("p h a s -> p h (a s)"),
                    q2[:, g, :, :].rearrange("p a s -> p (a s)").unsqueeze(1).to_broadcast([128, HG, 2 * S]),
                    own[:].unsqueeze(2).to_broadcast([128, HG, 2 * S]), ALU.mult).then_inc(qm_ready, 1)

            own_rows(0, 1)
            own_rows(1, 3)

            def body(b, kind, order):
                for what, arg in order:
                    if what == "S":
                        wait(pool, ph_done, b * NP + (arg + 1))
                        if not (kind == "first" and arg < 4):
                            wait(pool, p_transposed, b * H + 2 * (arg - 3))
                        nc.gpsimd.tensor_tensor(pl[:, arg % 4, :, :], p32[:, arg % 2, :, :], ph[:, arg % 4, :, :],
                                                ALU.subtract).then_inc(pl_done, 1)
                    elif arg in ("Q0", "Q1"):
                        g = int(arg[1])
                        wait(pool, scored, b * H + HG * (g + 1))
                        own_rows(g, job_number(b, kind, arg))

            walk(pool, "pool", body)

        @block.vector
        def _(dve):
            link = Chain(dve, chain)
            wait(dve, bias_ready, 1)
            nc.vector.tensor_scalar(bo_g[:], bo[:], tanh_g[0:S, 1:2], None, ALU.mult)
            link(nc.vector.tensor_scalar(gate[:], tanh_g[0:S, 1:2], 1.0 / (WS * WS), None, ALU.mult))

            def split_context(b):
                wait(dve, ctx_hi, b + 1)
                nc.vector.tensor_tensor(cl[:], ctx32[:], ch[:], ALU.subtract).then_inc(ctx_lo, 1)

            def low(out, src, b, hi):
                return nc.vector.scalar_tensor_tensor(out=out, in0=src, scalar=b, in1=hi, op0=ALU.add,
                                                      op1=ALU.subtract)

            def evacuate(name, bank, number):
                wait(dve, job_hi, number + 1)
                i = int(name[1]) if name != "OT" else 0
                if name[0] == "V":
                    last = nc.vector.tensor_tensor(vl[:, i, :], ps_j[0:KV, bank, 0:D], vh[:, i, :], ALU.subtract)
                elif name[0] == "K":
                    last = low(kl[:, i, :], ps_j[:, bank, 0:NC], bias[:, 1, i:i + 1], kh[:, i, :])
                elif name[0] == "Q":
                    last = low(q2[:, i, 1, :], ps_j[:, bank, 0:S], bias[:, 0, i:i + 1], q2[:, i, 0, :])
                else:
                    for k in range(KD):
                        last = low(otl[:, k, :], ps_j[:, bank, k * S:(k + 1) * S], bias[:, 2, k:k + 1], oth[:, k, :])
                last.then_inc(job_lo, 1)

            split_context(0)
            for n, name in enumerate(FIRST):
                evacuate(name, n % 2, n)
            wait(dve, pt_zeroed, 1)
            wait(dve, mask_in, 16)
            n0 = link.n

            def count(order):
                return sum({"S": 2, "O'": 1, "W'": 1}.get(step[0], 0) for step in order)

            per = count(steps("dve", False, False))
            c_first = count(steps("dve", True, False))

            def body(b, kind, order):
                c = 0

                def chained(instruction):
                    nonlocal c
                    c += 1
                    instruction.then_inc(chain, 1)
                    if kind == "first":
                        wait(dve, chain, n0 + c)
                    elif kind == "tail":
                        wait(dve, chain, n0 + c_first + (B - 2) * per + per + c)
                    else:
                        wait(dve, chain, b * per + (n0 + c_first - per + c))

                def first_probabilities(what, arg):
                    bb = b - 1 if "'" in what else b
                    h = 2 * arg
                    wait(dve, p_transposed, bb * H + (h + 1))
                    if not (kind == "first" and h < 4):
                        wait(dve, pv_done, bb * H + (h - 3))
                    copy_probabilities(nc.vector.tensor_copy, h, 0).then_inc(pt0_ready, 1)

                for what, arg, *between in order:
                    if what == "S":
                        wait(dve, scored, b * H + (2 * arg + 2))
                        mb = maskt[:, bass.ds(b, 1), :].to_broadcast([S, 2, NC])
                        ins = nc.vector.tensor_tensor(s1[:], ps_s[0:S, :, 0:NC], mb, ALU.mult)
                        ins.then_inc(masked, 1)
                        wait(dve, masked, b * NP + (arg + 1))
                        chained(nc.vector.tensor_scalar(fill[:], s1[:], 0.0, FILL, ALU.is_equal, ALU.mult))
                        if not (kind == "first" and arg < 2):
                            wait(dve, exp_done, b * H + 2 * (arg - 1))
                        for step in between[0]:
                            first_probabilities(*step)
                        for i in range(2):
                            ins = nc.vector.tensor_tensor_reduce(
                                out=s2[:, arg % 2, i, :], in0=s1[:, i, :], in1=fill[:, i, :], scale=1.0,
                                scalar=-3.0e38, op0=ALU.add, op1=ALU.max, accum_out=mx[:, arg % 2, i:i + 1])
                        chained(ins)
                        nc.vector.tensor_scalar(nb[:, arg % 2, :], mx[:, arg % 2, :], -SC, None, ALU.mult
                                                ).then_inc(max_ready, 1)
                    elif what[0] == "T":
                        first_probabilities(what, arg)
                    elif what == "C":
                        split_context(b + 1)
                    elif what == "O'":
                        wait(dve, exp_done, b * H)
                        chained(nc.vector.reciprocal(rinv[:], rsum[:, bass.ds((b - 1) * H, H)]))
                        wait(dve, pv_done, b * H)
                        nc.vector.tensor_tensor(
                            on[:].rearrange("p (h d) -> p h d", h=H),
                            ps_o[0:S, 0:D].rearrange("p (h d) -> p h d", h=H),
                            rinv[:].unsqueeze(2).to_broadcast([S, H, DH1]), ALU.mult).then_inc(o_ready, 1)
                    elif what == "J":
                        evacuate(arg, bank_of(kind, arg), job_number(b, kind, arg))
                    elif what == "W'":
                        xb = x_res[:, bass.ds(b - 1, 1), :].rearrange("p a d -> p (a d)")
                        chained(nc.vector.tensor_tensor(xb, xb, bo_g[:], ALU.add))
                        wait(dve, wo_done, b)
                        nc.vector.scalar_tensor_tensor(out=xb, in0=ps_w[0:S, 0:D], scalar=gate[:], in1=xb,
                                                       op0=ALU.mult, op1=ALU.add).then_inc(x_done, 1)

            walk(dve, "dve", body)


def router_phase(nc, A, norm, xh, xl, comb, macc, ident32):
    with ExitStack() as ctx:
        sb, ps, sem = make_allocators(nc, ctx)
        rw = sb("r_w", [128, 2, KD, E], F16)
        split_phase(nc, "rw", [(A["router_wT"], flat(rw[:, 0]), flat(rw[:, 1]))], KD * E)
        b2 = sb("r_b2", [E + 1, D])
        ex, prob = sb("r_ex", [S, B, E]), sb("r_prob", [S, B, E])
        top = sb("r_top", [S, B, 8])
        idx = sb("r_idx", [S, B, 8], U32)
        idxf = sb("r_idxf", [S, B, 2])
        num = sb("r_num", [S, E])
        den, rden = sb("r_den", [S, B]), sb("r_rden", [S, B])
        pick = sb("r_pick", [S, 2, B, E])
        wts = sb("r_wts", [S, B, E])
        wT = sb("r_wT", [E + 1, B, S])
        pr = ps("r_pr", [128, 512])
        pT = ps("r_pT", [128, 4, 512])
        pb = ps("r_pb", [128, 2, 512])
        names = ("b2_in", "logits", "exp_done", "chain", "num_made", "wts_ready", "ones_set", "transposed", "wT_ready",
                 "bias_done", "macc_ready")
        (b2_in, logits, exp_done, chain, num_made, wts_ready, ones_set, transposed, wT_ready, bias_done,
         macc_ready) = (sem(f"r_{n}") for n in names)
        block = ctx.enter_context(nc.Block())

        @block.sync
        def _(sp):
            sp.dma_start(b2[:], A["b2"]).then_inc(b2_in, 16)

        @block.gpsimd
        def _(pool):
            nc.gpsimd.iota(num[:], pattern=[[1, E]], base=0, channel_multiplier=0,
                           allow_small_or_imprecise_dtypes=True).then_inc(num_made, 1)
            nc.gpsimd.memset(wT[:], 1.0).then_inc(ones_set, 1)

        @block.tensor
        def _(pe):
            for t in range(B):
                tt = slice(t * S, (t + 1) * S)
                mm = products(nc, pr[0:S, t * E:(t + 1) * E], [
                    (xh[:, k, tt], xl[:, k, tt], rw[:, 0, k, :], rw[:, 1, k, :]) for k in range(KD)])
            mm.then_inc(logits, 1)
            pe.wait_ge(wts_ready, 1)
            for t in range(B):
                mm = nc.tensor.transpose(pT[0:E, t // 4, (t % 4) * S:(t % 4 + 1) * S], wts[:, t, :],
                                         ident32[0:S, 0:S])
                if t % 4 == 3:
                    mm.then_inc(transposed, 1)
            pe.wait_ge(b2_in, 16)
            pe.wait_ge(wT_ready, 1)
            for t in range(B):
                if t >= 2:
                    pe.wait_ge(macc_ready, t - 1)
                nc.tensor.matmul(pb[0:S, t % 2, 0:D], wT[:, t, :], b2[:], start=True, stop=True).then_inc(bias_done, 1)

        @block.scalar
        def _(act):
            act.wait_ge(logits, 1)
            nc.scalar.activation(ex[:], pr[0:S, 0:B * E].rearrange("p (t e) -> p t e", t=B), ACT.Exp,
                                 scale=-1.0 / WS).then_inc(exp_done, 1)
            act.wait_ge(ones_set, 1)
            act.wait_ge(transposed, 4)
            nc.scalar.activation(wT[0:E, :, :].rearrange("p (g t) s -> p g (t s)", g=4), pT[0:E, :, 0:4 * S],
                                 ACT.Copy).then_inc(wT_ready, 1)

        @block.vector
        def _(dve):
            link = Chain(dve, chain)
            dve.wait_ge(exp_done, 1)
            link(nc.vector.tensor_scalar(ex[:], ex[:], 1.0, None, ALU.add))
            link(nc.vector.reciprocal(prob[:], ex[:]))
            for t in range(B):
                last = nc.vector.max(top[:, t, :], prob[:, t, :])
            link(last)
            for t in range(B):
                last = nc.vector.max_index(idx[:, t, :], top[:, t, :], prob[:, t, :])
            link(last)
            link(nc.vector.tensor_copy(idxf[:], idx[:, :, 0:2]))
            link(nc.vector.tensor_tensor(den[:], top[:, :, 0], top[:, :, 1], ALU.add))
            link(nc.vector.tensor_scalar(den[:], den[:], 1e-6, None, ALU.add))
            link(nc.vector.reciprocal(rden[:], den[:]))
            dve.wait_ge(num_made, 1)
            for i in range(2):
                link(nc.vector.tensor_tensor(pick[:, i], num[:].unsqueeze(1).to_broadcast([S, B, E]),
                                             idxf[:, :, i:i + 1].to_broadcast([S, B, E]), ALU.is_equal))
                link(nc.vector.tensor_tensor(pick[:, i], pick[:, i], top[:, :, i:i + 1].to_broadcast([S, B, E]),
                                             ALU.mult))
            link(nc.vector.tensor_tensor(wts[:], pick[:, 0], pick[:, 1], ALU.add))
            nc.vector.tensor_tensor(wts[:], wts[:], rden[:].unsqueeze(2).to_broadcast([S, B, E]), ALU.mult
                                    ).then_inc(wts_ready, 1)
            dve.wait_ge(wts_ready, 1)
            nc.vector.memset(comb[:, E, :], 1.0 / WS)
            link(nc.vector.tensor_scalar(comb[:, 0:E, :].rearrange("p e t -> p t e"), wts[:], 1.0 / WS, None,
                                         ALU.mult))
            for t in range(B):
                dve.wait_ge(bias_done, t + 1)
                nc.vector.tensor_copy(macc[:, t, :], pb[0:S, t % 2, 0:D]).then_inc(macc_ready, 1)


def experts_phase(nc, A, x_res, xh, xl, comb, macc, tanh_g):
    W1N, W2N = KD * FF1, HC1 * D
    with ExitStack() as ctx:
        sb, ps, sem = make_allocators(nc, ctx)
        b1 = sb("m_b1", [128, E + 1, HC1])
        stage = sb("m_stage", [128, W1N + W2N])
        wh, wl = sb("m_wh", [128, 2, W1N + W2N], F16), sb("m_wl", [128, 2, W1N + W2N], F16)
        h32 = sb("m_h32", [128, 2, GW])
        hh, hl = sb("m_hh", [128, HC1, GW], F16), sb("m_hl", [128, HC1, GW], F16)
        p1 = ps("m_p1", [128, 4, 512])
        p2 = ps("m_p2", [128, 2, 2, 512])
        names = ("b1_in", "w_in", "w_hi", "w_lo", "up_done", "relu_done", "h_hi", "h_lo", "down_done", "added",
                 "x_done")
        (b1_in, w_in, w_hi, w_lo, up_done, relu_done, h_hi, h_lo, down_done, added, x_done) = (
            sem(f"m_{n}") for n in names)
        block = ctx.enter_context(nc.Block())

        def experts(eng, body):
            with eng.Fori(0, E // 2) as i:
                for par in range(2):
                    body(i * 2 + par, par, False)
            body(E, 0, True)

        @block.sync
        def _(sp):
            sp.dma_start(b1[:], A["b1T"]).then_inc(b1_in, 16)

            def load(e):
                sp.dma_start(stage[:, 0:W1N].rearrange("p (k n) -> p k n", k=KD),
                             A["w1"][bass.ds(e, 1)].rearrange("e (k p) n -> p (e k) n", p=128)).then_inc(w_in, 16)
                sp.dma_start(stage[:, W1N:].rearrange("p (k n) -> p k n", k=HC1),
                             A["w2"][bass.ds(e, 1)].rearrange("e (k p) n -> p (e k) n", p=128)).then_inc(w_in, 16)

            load(0)
            with sp.Fori(1, E + 1) as e:
                sp.wait_ge(w_lo, e)
                load(e)


        @block.scalar
        def _(act):
            act.sem_inc(relu_done, 1)

            def split(e, par):
                act.wait_ge(w_in, e * 32 + 32)
                nc.scalar.activation(wh[:, par, :], stage[:], ACT.Copy, scale=WS).then_inc(w_hi, 1)

            split(0, 0)
            act.wait_ge(b1_in, 16)

            def body(e, par, last):
                if not last:
                    act.wait_ge(down_done, e * B + 1)
                    split(e + 1, 1 - par)
                with act.Fori(0, NG) as g:
                    n = (e * NG + g) * HC1
                    for j in range(HC1):
                        act.wait_ge(up_done, n + (j + 1))
                        act.wait_ge(h_lo, n + (j - 1) + 1) if j else act.wait_ge(h_lo, n + 1)
                        nc.scalar.activation(h32[:, j % 2, :], p1[:, j % 4, 0:GW], ACT.Relu,
                                             bias=b1[:, bass.ds(e, 1), j:j + 1].rearrange("p a b -> p (a b)"),
                                             scale=1.0 / WS).then_inc(relu_done, 1)
                        act.wait_ge(relu_done, n + (j + 2))
                        nc.scalar.activation(hh[:, j, :], h32[:, j % 2, :], ACT.Copy).then_inc(h_hi, 1)

            body_ = body
            experts(act, body_)

        @block.vector
        def _(dve):
            dve.sem_inc(h_lo, 1)
            dve.sem_inc(added, 1)

            def split(e, par):
                dve.wait_ge(w_hi, e + 1)
                nc.vector.scalar_tensor_tensor(out=wl[:, par, :], in0=stage[:], scalar=WS, in1=wh[:, par, :],
                                               op0=ALU.mult, op1=ALU.subtract).then_inc(w_lo, 1)

            split(0, 0)

            def body(e, par, last):
                if not last:
                    split(e + 1, 1 - par)
                with dve.Fori(0, NG) as g:
                    n = (e * NG + g) * HC1
                    for j in range(HC1):
                        dve.wait_ge(h_hi, n + (j + 1))
                        nc.vector.tensor_tensor(hl[:, j, :], h32[:, j % 2, :], hh[:, j, :], ALU.subtract
                                                ).then_inc(h_lo, 1)
                    for i in range(TG):
                        dve.wait_ge(down_done, (e * NG + g) * TG + (i + 2))
                        mt = macc[:, bass.ds(g * TG + i, 1), :].rearrange("p a d -> p (a d)")
                        nc.vector.scalar_tensor_tensor(
                            out=mt, in0=p2[0:S, i // 2, i % 2, 0:D],
                            scalar=comb[:].rearrange("p e t -> p (e t)")[:, bass.ds(e * B + g * TG + i, 1)],
                            in1=mt, op0=ALU.mult, op1=ALU.add).then_inc(added, 1)

            experts(dve, body)
            for t in range(B):
                dve.wait_ge(added, (E + 1) * B + 1)
                nc.vector.scalar_tensor_tensor(out=x_res[:, t, :], in0=macc[:, t, :], scalar=tanh_g[0:S, 3:4],
                                               in1=x_res[:, t, :], op0=ALU.mult, op1=ALU.add).then_inc(x_done, 1)

        @block.tensor
        def _(pe):
            pe.sem_inc(down_done, 1)

            def body(e, par, last):
                w1h, w1l = (w[:, par, 0:W1N].rearrange("p (k n) -> p k n", k=KD) for w in (wh, wl))
                w2h, w2l = (w[:, par, W1N:].rearrange("p (k n) -> p k n", k=HC1) for w in (wh, wl))
                with pe.Fori(0, NG) as g:
                    n = (e * NG + g) * HC1
                    pe.wait_ge(w_lo, e + 1)
                    for j in range(HC1):
                        pe.wait_ge(relu_done, n + max(j - 3, 0) + 1)
                        jj = slice(j * 128, (j + 1) * 128)
                        products(nc, p1[:, j % 4, 0:GW], [
                            (w1h[:, k, jj], w1l[:, k, jj], xh[:, k, bass.ds(g * GW, GW)], xl[:, k, bass.ds(g * GW, GW)])
                            for k in range(KD)]).then_inc(up_done, 1)
                    pe.wait_ge(added, (e * NG + g) * TG + 1)
                    for i in range(TG):
                        if i == 0:
                            pe.wait_ge(h_lo, n + (HC1 + 1))
                        ii = slice(i * S, (i + 1) * S)
                        products(nc, p2[0:S, i // 2, i % 2, 0:D], [
                            (hh[:, j, ii], hl[:, j, ii], w2h[:, j, :], w2l[:, j, :]) for j in range(HC1)
                        ]).then_inc(down_done, 1)

            experts(pe, body)


def moe_phase(nc, A, x_res, xh, xl, ident32, tanh_g):
    with ExitStack() as ctx:
        sb, ps, sem = make_allocators(nc, ctx)
        macc = sb("macc", [S, B, D])
        comb = sb("comb", [S, E + 1, B])
        with ExitStack() as c2:
            rms_w = c2.enter_context(nc.sbuf_tensor("rms_w", [S, D], F32))
            norm = c2.enter_context(nc.sbuf_tensor("norm", [S, B, D], F32))
            w_in = c2.enter_context(nc.semaphore("rms_in"))
            with nc.Block() as block:
                @block.sync
                def _(sp):
                    sp.dma_start(rms_w[:], A["L1_ffn_norm_weight"].partition_broadcast(S)).then_inc(w_in, 16)
                    sp.wait_ge(w_in, 16)
            norm_phase(nc, "n3", x_res, ident32, xh, xl, n_out=norm, rms_w=rms_w)
            router_phase(nc, A, norm, xh, xl, comb, macc, ident32)
        experts_phase(nc, A, x_res, xh, xl, comb, macc, tanh_g)


def program(nc, A, out, phases="0ABCD"):
    with ExitStack() as ctx:
        sb, ps, sem = make_allocators(nc, ctx)
        x_res = sb("x_res", [S, B, D])
        ident32, ident16 = sb("ident32", [128, 128]), sb("ident16", [128, 128], F16)
        gates, tanh_g = sb("gates", [128, 4]), sb("tanh_g", [128, 4])
        xh, xl = sb("xh", [128, KD, T], F16), sb("xl", [128, KD, T], F16)
        sx, sx_inv = sb("sx", [128, 1]), sb("sx_inv", [128, 1])
        setup_phase(nc, A, x_res, ident32, ident16, gates, tanh_g)
        if "A" in phases:
            norm_phase(nc, "n0", x_res, ident32, xh, xl)
            attention0_phase(nc, A, x_res, xh, xl, ident32, ident16, tanh_g)
        if "B" in phases:
            norm_phase(nc, "n1", x_res, ident32, xh, xl, quant=(sx, sx_inv))
            feed_forward0_phase(nc, A, x_res, xh, xl, sx, ident32, tanh_g)
        if "C" in phases:
            norm_phase(nc, "n2", x_res, ident32, xh, xl)
            attention1_phase(nc, A, x_res, xh, xl, ident32, ident16, tanh_g)
        if "D" in phases:
            moe_phase(nc, A, x_res, xh, xl, ident32, tanh_g)
        with ExitStack() as c2:
            stored = c2.enter_context(nc.semaphore("stored"))
            block = c2.enter_context(nc.Block())

            @block.sync
            def _(sp):
                sp.dma_start(out.rearrange("t s d -> s t d"), x_res[:]).then_inc(stored, 16)
                sp.wait_ge(stored, 16)


def lay_out(inputs, np):
    g = {k: np.ascontiguousarray(v) for k, v in inputs.items()}
    a = {
        "x": g["x"].reshape(T, D),
        "ctxT": g["ctx_1024"].reshape(B * NC, D).T.reshape(KD, 128, B * NC),
        "g_xattn": g["g_xattn"],
        "g_ffn": g["g_ffn"],
    }
    a["mask"] = g["mask_Bx1xSxS2_ff1"].reshape(B, S, NC)
    a["L1_qkv_bT"] = np.stack([g[f"L1_xattn_{n}_b"] for n in ("wq", "wk", "wv")]).reshape(3, KD, 128).transpose(2, 0, 1)
    a["w1"] = np.concatenate([g["L1_ffn_ew1"], g["L1_ffn_sw1"][None]])
    a["w2"] = np.concatenate([g["L1_ffn_ew2"], g["L1_ffn_sw2"][None]])
    a["b1T"] = np.concatenate([g["L1_ffn_eb1"], g["L1_ffn_sb1"][None]]).reshape(E + 1, HC1, 128).transpose(2, 0, 1)
    a["b2"] = np.concatenate([g["L1_ffn_eb2"], g["L1_ffn_sb2"][None]])
    a["router_wT"] = g["L1_ffn_router_w"].T.reshape(KD, 128, E).transpose(1, 0, 2)
    for n in ("L0_xattn_Wq", "L0_xattn_Wk", "L0_xattn_Wv", "L0_xattn_Wo", "L0_xattn_bo", "L0_ffn_w_gate",
              "L0_ffn_w_up", "L0_ffn_w_down", "L1_xattn_wq_w", "L1_xattn_wk_w", "L1_xattn_wv_w", "L1_xattn_wo_w",
              "L1_xattn_wo_b", "L1_ffn_norm_weight"):
        a[n] = g[n]
    return {k: np.ascontiguousarray(v) for k, v in a.items()}


def kernel(**inputs):
    import numpy as _np
    import concourse.bacc as _bacc
    from concourse import mybir as _mybir
    from concourse.bass_utils import run_bass_kernel_spmd as _run

    nc = _bacc.Bacc("TRN2", target_bir_lowering=False, num_devices=1)
    laid = lay_out(inputs, _np)
    arrays = {f"in_{n}": a for n, a in laid.items()}
    args = {n: nc.dram_tensor(f"in_{n}", a.shape, _mybir.dt.from_np(a.dtype), kind="ExternalInput").ap()
            for n, a in laid.items()}
    out = nc.dram_tensor("out_x", (B, S, D), F32, kind="ExternalOutput").ap()
    program(nc, args, out)
    r = _run(nc, [arrays], core_ids=[0])
    return r.results[0]["out_x"]
```

```python
import concourse.bass as bass
from concourse import mybir
from contextlib import ExitStack

F32 = mybir.dt.float32
F16 = mybir.dt.float16
U32 = mybir.dt.uint32
I32 = mybir.dt.int32
ALU = mybir.AluOpType
ACT = mybir.ActivationFunctionType
AX = mybir.AxisListType

B, S, D, NC = 16, 112, 256, 375
T = B * S
KD = D // 128
NKV, KV = 3, 125
H = 16
DH0, DH1 = 64, 16
IN0 = H * DH0
CK0 = IN0 // 128
FF0 = 768
OC0 = FF0 // 128
FF1 = 1024
HC1 = FF1 // 128
E = 8
MAXT = (2 * T + E * 127) // 128
W1N, W2N = KD * FF1, HC1 * D
WN = W1N + W2N
QBLK = 32
TG = 4
NG = B // TG
GW = TG * S
NP = H // 2

WS = 32.0
MAGIC = 12582912.0
QMAX = 32767.0
UQ = 65536.0


def wait(eng, sem, n):
    if not (isinstance(n, int) and n <= 0):
        eng.wait_ge(sem, n)


class Chain:

    def __init__(self, eng, sem):
        self.eng, self.sem, self.n = eng, sem, 0

    def __call__(self, instruction):
        self.n += 1
        instruction.then_inc(self.sem, 1)
        self.eng.wait_ge(self.sem, self.n)


def make_allocators(nc, ctx):
    def sb(name, shape, dt=F32):
        return ctx.enter_context(nc.sbuf_tensor(name, shape, dt))

    def ps(name, shape, dt=F32):
        return ctx.enter_context(nc.psum_tensor(name, shape, dt))

    def sem(name):
        return ctx.enter_context(nc.semaphore(name))

    return sb, ps, sem


def clear_semaphores(nc):
    used = sorted(nc.released_uncleared_semaphores)
    with nc.Block() as block:
        @block.gpsimd
        def _(pool):
            nc.gpsimd.sem_clear(range(used[0], used[-1] + 1))


def setup_phase(nc, A, x_res, ident32, ident16, gates, tanh_g):
    with ExitStack() as ctx:
        sb, ps, sem = make_allocators(nc, ctx)
        x_in, g_in, zeroed, made = sem("x_in"), sem("g_in"), sem("id_zeroed"), sem("id_made")
        tanh_done = sem("tanh_done")
        block = ctx.enter_context(nc.Block())

        @block.sync
        def _(sp):
            sp.dma_start(x_res[:], A["x"].rearrange("(t p) d -> p t d", p=S)).then_inc(x_in, 16)
            for i, name in enumerate(("g_xattn", "g_ffn")):
                sp.dma_start(gates[:, 2 * i:2 * i + 2], A[name].partition_broadcast(128)).then_inc(g_in, 16)
            sp.wait_ge(x_in, 16)

        @block.gpsimd
        def _(pool):
            for m in (ident32, ident16):
                nc.gpsimd.memset(m[:], 0.0).then_inc(zeroed, 1)
            pool.wait_ge(zeroed, 2)
            for m in (ident32, ident16):
                nc.gpsimd.affine_select(out=m[:], in_=m[:], compare_op=ALU.not_equal, fill=1.0, base=0,
                                        pattern=[[-1, 128]], channel_multiplier=1).then_inc(made, 1)

        @block.scalar
        def _(act):
            act.wait_ge(g_in, 32)
            nc.scalar.activation(tanh_g[:], gates[:], ACT.Tanh).then_inc(tanh_done, 1)


def norm_phase(nc, tag, x_res, ident32, xh, xl, n_out=None, rms_w=None, quant=None):
    with ExitStack() as ctx:
        sb, ps, sem = make_allocators(nc, ctx)
        stats = sb(f"{tag}_stats", [S, B, 6])
        mv = sb(f"{tag}_mv", [S, B, 2])
        eps = sb(f"{tag}_eps", [S, 1])
        var = sb(f"{tag}_var", [S, B])
        std = sb(f"{tag}_std", [S, B])
        rstd = sb(f"{tag}_rstd", [S, B])
        tmp = sb(f"{tag}_tmp", [S, B])
        xn = n_out if n_out is not None else sb(f"{tag}_xn", [S, B, D])
        amax = sb(f"{tag}_amax", [128, 2])
        tp = ps(f"{tag}_tp", [128, 4, 512])
        chain, var_ready, std_ready = sem(f"{tag}_chain"), sem(f"{tag}_var_ready"), sem(f"{tag}_std_ready")
        xn_ready, transposed, hi_done, lo_done = (sem(f"{tag}_{n}") for n in
                                                  ("xn_ready", "transposed", "hi_done", "lo_done"))
        amax_part, amax_all = sem(f"{tag}_amax_part"), sem(f"{tag}_amax_all")
        norms = 1 if rms_w is None else 2
        block = ctx.enter_context(nc.Block())

        @block.vector
        def _(dve):
            link = Chain(dve, chain)

            def statistics(src, epsilon, ms):
                for t in range(B):
                    last = nc.vector.bn_stats(stats[:, t, :], src[:, t, :])
                link(last)
                for t in range(B):
                    last = nc.vector.bn_aggr(mv[:, t, :], stats[:, t, :])
                link(last)
                if ms:
                    link(nc.vector.tensor_tensor(tmp[:], mv[:, :, 0], mv[:, :, 0], ALU.mult))
                    link(nc.vector.tensor_tensor(tmp[:], tmp[:], mv[:, :, 1], ALU.add))
                    link(nc.vector.tensor_scalar(var[:], tmp[:], epsilon, None, ALU.add))
                else:
                    link(nc.vector.tensor_scalar(var[:], mv[:, :, 1], epsilon, None, ALU.add))
                nc.vector.tensor_copy(tmp[:], var[:]).then_inc(var_ready, 1)
                dve.wait_ge(std_ready, 2 if ms else 1)
                link(nc.vector.reciprocal(rstd[:], std[:]))
                link(nc.vector.tensor_tensor(tmp[:], rstd[:], rstd[:], ALU.mult))
                link(nc.vector.tensor_tensor(tmp[:], tmp[:], var[:], ALU.mult))
                link(nc.vector.tensor_scalar(tmp[:], tmp[:], -0.5, 1.5, ALU.mult, ALU.add))
                link(nc.vector.tensor_tensor(rstd[:], rstd[:], tmp[:], ALU.mult))

            nc.vector.memset(amax[:], 0.0)
            statistics(x_res, 1e-5, False)
            for t in range(B):
                last = nc.vector.tensor_scalar(xn[:, t, :], x_res[:, t, :], mv[:, t, 0:1], rstd[:, t:t + 1],
                                               ALU.subtract, ALU.mult)
                if norms == 1 and quant is None:
                    last.then_inc(xn_ready, 1)
            if norms == 2:
                link(last)
                statistics(xn, 1e-8, True)
                for t in range(B):
                    nc.vector.scalar_tensor_tensor(out=xn[:, t, :], in0=xn[:, t, :], scalar=rstd[:, t:t + 1],
                                                   in1=rms_w[:], op0=ALU.mult, op1=ALU.mult).then_inc(xn_ready, 1)
            if quant is not None:
                scale, inv = quant
                link(last)
                nc.vector.tensor_reduce(amax[0:S, 0:1], xn[:], AX.XY, ALU.max,
                                        apply_absolute_value=True).then_inc(amax_part, 1)
                dve.wait_ge(amax_all, 1)
                link(nc.vector.tensor_scalar(scale[:], amax[:, 1:2], 1.0 / QMAX, 1e-12, ALU.mult, ALU.max))
                link(nc.vector.reciprocal(inv[:], scale[:]))
                link(nc.vector.tensor_scalar(xn[:], xn[:], inv[0:S, :], MAGIC, ALU.mult, ALU.add))
                nc.vector.tensor_scalar(xn[:], xn[:], -MAGIC, None, ALU.add).then_inc(xn_ready, B)
            for j in range(NG * KD):
                g, k = j // KD, j % KD
                dve.wait_ge(hi_done, j + 1)
                nc.vector.tensor_tensor(xl[:, k, g * GW:(g + 1) * GW], tp[:, j % 4, 0:GW],
                                        xh[:, k, g * GW:(g + 1) * GW], ALU.subtract).then_inc(lo_done, 1)

        @block.gpsimd
        def _(pool):
            if quant is not None:
                pool.wait_ge(amax_part, 1)
                nc.gpsimd.partition_all_reduce(amax[:, 1:2], amax[:, 0:1], 128,
                                               bass.bass_isa.ReduceOp.max).then_inc(amax_all, 1)

        @block.scalar
        def _(act):
            for n in range(norms):
                act.wait_ge(var_ready, n + 1)
                nc.scalar.activation(std[:], var[:], ACT.Sqrt).then_inc(std_ready, 1)
            for j in range(NG * KD):
                g, k = j // KD, j % KD
                act.wait_ge(transposed, j + 1)
                nc.scalar.activation(xh[:, k, g * GW:(g + 1) * GW], tp[:, j % 4, 0:GW],
                                     ACT.Copy).then_inc(hi_done, 1)

        @block.tensor
        def _(pe):
            for j in range(NG * KD):
                g, k = j // KD, j % KD
                pe.wait_ge(xn_ready, TG * (g + 1))
                if j >= 4:
                    pe.wait_ge(lo_done, j - 3)
                for i in range(TG):
                    last = nc.tensor.transpose(tp[:, j % 4, i * S:(i + 1) * S],
                                               xn[:, g * TG + i, k * 128:(k + 1) * 128], ident32[0:S, 0:S])
                last.then_inc(transposed, 1)


def split_phase(nc, tag, loads, stage_cols):
    with ExitStack() as ctx:
        sb, ps, sem = make_allocators(nc, ctx)
        stage = sb(f"{tag}_stage", [128, 2, stage_cols])
        arrived = [sem(f"{tag}_arrived{i}") for i in range(2)]
        hi_done, lo_done = sem(f"{tag}_hi_done"), sem(f"{tag}_lo_done")
        block = ctx.enter_context(nc.Block())

        @block.sync
        def _(sp):
            for i, (src, hi, lo) in enumerate(loads):
                if i >= 2:
                    sp.wait_ge(lo_done, i - 1)
                sp.dma_start(stage[:, i % 2, 0:hi.free_size()].rearrange("p (a b) -> p a b", a=src.shape[1]),
                             src).then_inc(arrived[i % 2], 16)

        @block.scalar
        def _(act):
            for i, (src, hi, lo) in enumerate(loads):
                act.wait_ge(arrived[i % 2], 16 * (i // 2 + 1))
                nc.scalar.activation(hi, stage[:, i % 2, 0:hi.free_size()], ACT.Copy, scale=WS).then_inc(hi_done, 1)

        @block.vector
        def _(dve):
            for i, (src, hi, lo) in enumerate(loads):
                dve.wait_ge(hi_done, i + 1)
                nc.vector.scalar_tensor_tensor(out=lo, in0=stage[:, i % 2, 0:hi.free_size()], scalar=WS, in1=hi,
                                               op0=ALU.mult, op1=ALU.subtract).then_inc(lo_done, 1)


def flat(ap):
    return ap.rearrange("p a b -> p (a b)")


def products(nc, out, pairs):
    n = len(pairs)
    for i, (wh, wl, mh, ml) in enumerate(pairs):
        nc.tensor.matmul(out, wh, mh, start=(i == 0), stop=False)
        nc.tensor.matmul(out, wh, ml, start=False, stop=False)
        last = nc.tensor.matmul(out, wl, mh, start=False, stop=(i == n - 1))
    return last


def attention0_phase(nc, A, x_res, xh, xl, ident32, ident16, tanh_g):
    SC = float(DH0) ** -0.5 / (WS * WS)
    with ExitStack() as ctx:
        sb, ps, sem = make_allocators(nc, ctx)
        wq, wk, wv = (sb(f"a0_{n}", [128, 2, KD, IN0], F16) for n in ("wq", "wk", "wv"))
        wo = sb("a0_wo", [128, 2, CK0, D], F16)
        split_phase(nc, "a0w", [
            (A[n][k * 128:(k + 1) * 128, :].rearrange("p (a b) -> p a b", a=1), w[:, 0, k, :], w[:, 1, k, :])
            for n, w in (("L0_xattn_Wk", wk), ("L0_xattn_Wq", wq), ("L0_xattn_Wv", wv)) for k in range(KD)
        ] + [
            (A["L0_xattn_Wo"].rearrange("(k p) n -> p k n", p=128)[:, 4 * k:4 * k + 4, :],
             flat(wo[:, 0, 4 * k:4 * k + 4, :]), flat(wo[:, 1, 4 * k:4 * k + 4, :])) for k in range(CK0 // 4)
        ], IN0)

        bo = sb("a0_bo", [S, D])
        bo_g = sb("a0_bo_g", [S, D])
        gate = sb("a0_gate", [S, 1])
        ctx32 = sb("a0_ctx32", [128, KD, NC])
        ch, cl = sb("a0_ch", [128, KD, NC], F16), sb("a0_cl", [128, KD, NC], F16)
        ks = sb("a0_ks", [128, H, NC], F16)
        qs = sb("a0_qs", [128, H, 2, S], F16)
        vh, vl = sb("a0_vh", [KV, NKV, IN0], F16), sb("a0_vl", [KV, NKV, IN0], F16)
        p32 = sb("a0_p32", [S, 2, 2, NC])
        ph, pl = sb("a0_ph", [S, 4, 2, NC], F16), sb("a0_pl", [S, 4, 2, NC], F16)
        pt = sb("a0_pt", [KV, 4, 2, NKV, 128], F16)
        mx, nb = sb("a0_mx", [S, 2, 2]), sb("a0_nb", [S, 2, 2])
        rsum, rinv = sb("a0_rsum", [S, H]), sb("a0_rinv", [S, H])
        on = sb("a0_on", [S, IN0])
        oth, otl = sb("a0_oth", [128, CK0, S], F16), sb("a0_otl", [128, CK0, S], F16)
        ps_s = ps("a0_ps_s", [128, 2, 512])
        ps_t = ps("a0_ps_t", [128, 2, 1024], F16)
        ps_o = ps("a0_ps_o", [128, 2, 512])
        ps_j = ps("a0_ps_j", [128, 2, 512])

        names = ("ctx_in", "bo_in", "pt_zeroed", "ctx_hi", "ctx_lo", "scored", "max_ready", "exp_done", "ph_done",
                 "pl_done", "p_transposed", "pt_ready", "pv_done", "job_done", "job_hi", "job_lo", "o_ready",
                 "wo_done", "x_done", "chain", "p_chain", "bo_scaled", "bo_added")
        (ctx_in, bo_in, pt_zeroed, ctx_hi, ctx_lo, scored, max_ready, exp_done, ph_done, pl_done, p_transposed,
         pt_ready, pv_done, job_done, job_hi, job_lo, o_ready, wo_done, x_done, chain, p_chain, bo_scaled,
         bo_added) = (
            sem(f"a0_{n}") for n in names)

        FIRST = ["K0", "Q0", "K1", "K2", "K3", "K4", "K5"]
        JOBS = [["K6", "V00"], ["K7", "V01"], ["V02", "Q1"], ["V10", "V11", "OT0"], ["V12", "OT1"], ["K0", "Q0"],
                ["K1", "K2"], ["K3", "K4", "K5"]]
        BODY = [n for js in JOBS for n in js]
        NEXT = BODY.index("K0")
        NEXTS, LASTS = BODY[NEXT:], ("OT0", "OT1")
        block = ctx.enter_context(nc.Block())

        def order(engine, b):
            first, last, drain = b == 0, b == B - 1, b == B
            out, late = [], []
            for p in range(NP):
                js = [("J", n, 0) for n in JOBS[p]
                      if not (first and n in LASTS) and not (last and n in NEXTS) and (not drain or n in LASTS)]
                now = [("S", p, 0)] if not drain else []
                if engine == "dve":
                    if p == 0 and not first:
                        late = [("J", n, -1) for n in JOBS[-1][-1:]] if not drain else []
                    now += [("O", 1, -1)] * (p == 3 and not first) + [("O", 0, 0)] * (p == 7 and not drain)
                    now += late + [("W", None, -1)] * (p == 6 and not first)
                if engine in ("pe", "act") and len(js) > 1:
                    now.append(js.pop(0))
                if p < 3 and not first and engine == "pe":
                    now.append(("P", p + NP - 3, -1))
                elif p >= 3 and not drain and engine == "pe":
                    now.append(("P", p - 3, 0))
                if engine in ("pe", "dve"):
                    if p < 2 and not first:
                        now.append(("T", p + NP - 2, -1))
                    elif p >= 2 and not drain:
                        now.append(("T", p - 2, 0))
                if engine == "pe" and p == 4 and not first:
                    now.append(("W", 0, -1))
                if engine == "act" and not drain:
                    now.append(("H", p, 0))
                if engine == "dve":
                    now, late = now + js[:-1], js[-1:]
                else:
                    now += js
                if engine == "pe" and p == 5 and not first:
                    now.append(("W", 1, -1))
                if p == 4 and not last and not drain and engine != "pe":
                    now.append(("C", None, 0))
                out += now
            return out

        def batches(eng, engine, body):
            body(0, order(engine, 0))
            with eng.Fori(1, B - 1) as b:
                body(b, order(engine, 1))
            body(B - 1, order(engine, B - 1))
            body(B, order(engine, B))

        def number(b, name):
            if isinstance(b, int) and b < 1:
                if name in NEXTS:
                    return (FIRST.index(name) if b < 0 else
                            len(FIRST) - len(LASTS) + BODY.index(name))
                return len(FIRST) + [n for n in BODY if n not in LASTS].index(name)
            if isinstance(b, int) and b == B:
                return B * len(BODY) + (len(FIRST) - len(LASTS) - (len(BODY) - NEXT)) + LASTS.index(name)
            return b * len(BODY) + (len(FIRST) - len(LASTS) + BODY.index(name))

        def bank_of(b, name):
            if isinstance(b, int):
                return number(b, name) % 2
            return (len(FIRST) - len(LASTS) + BODY.index(name)) % 2

        @block.sync
        def _(sp):
            sp.dma_start(bo[:], A["L0_xattn_bo"].partition_broadcast(S)).then_inc(bo_in, 16)
            sp.dma_start(ctx32[:], A["ctxT"][:, :, 0:NC].rearrange("k p n -> p k n")).then_inc(ctx_in, 16)
            with sp.Fori(1, B) as b:
                sp.wait_ge(ctx_lo, b)
                sp.dma_start(ctx32[:], A["ctxT"][:, :, bass.ds(b * NC, NC)].rearrange("k p n -> p k n")
                             ).then_inc(ctx_in, 16)

        @block.tensor
        def _(pe):
            def project(name, bank, b_q):
                if name[0] == "V":
                    c, t = int(name[1]), int(name[2])
                    last = products(nc, ps_j[0:KV, bank, :], [
                        (ch[:, k, t * KV:(t + 1) * KV], cl[:, k, t * KV:(t + 1) * KV],
                         wv[:, 0, k, c * 512:(c + 1) * 512], wv[:, 1, k, c * 512:(c + 1) * 512])
                        for k in range(KD)])
                elif name[0] == "K":
                    p = int(name[1])
                    last = products(nc, ps_j[:, bank, 0:NC], [
                        (wk[:, 0, k, p * 128:(p + 1) * 128], wk[:, 1, k, p * 128:(p + 1) * 128],
                         ch[:, k, :], cl[:, k, :]) for k in range(KD)])
                elif name[0] == "Q":
                    for i in range(4):
                        p = 4 * int(name[1]) + i
                        last = products(nc, ps_j[:, bank, i * S:(i + 1) * S], [
                            (wq[:, 0, k, p * 128:(p + 1) * 128], wq[:, 1, k, p * 128:(p + 1) * 128],
                             xh[:, k, bass.ds(b_q * S, S)], xl[:, k, bass.ds(b_q * S, S)]) for k in range(KD)])
                else:
                    for i in range(4):
                        k = 4 * int(name[2]) + i
                        last = nc.tensor.transpose(ps_j[:, bank, i * S:(i + 1) * S], on[:, k * 128:(k + 1) * 128],
                                                   ident32[0:S, 0:S])
                last.then_inc(job_done, 1)

            pe.wait_ge(ctx_lo, 1)
            for n, name in enumerate(FIRST):
                wait(pe, job_lo, n - 1)
                project(name, n % 2, 0)

            def body(b, steps):
                for what, arg, off in steps:
                    bb = b + off
                    if what == "S":
                        if arg in (0, 1, 2, 3, 5):
                            pe.wait_ge(job_lo, number(b - 1, "Q0" if arg == 0 else f"K{arg}") + 1)
                        if arg in (4, 6, 7):
                            pe.wait_ge(job_lo, number(b, "Q1" if arg == 4 else f"K{arg}") + 1)
                        for i in range(2):
                            h = 2 * arg + i
                            wait(pe, exp_done, b * H + (h - 1))
                            for part in range(2):
                                mm = nc.tensor.matmul(ps_s[0:S, i, 0:NC], qs[:, h, part, :], ks[:, h, :],
                                                      start=(part == 0), stop=(part == 1))
                            mm.then_inc(scored, 1)
                    elif what == "T":
                        pe.wait_ge(pl_done, bb * NP + (arg + 1))
                        for i in range(2):
                            h = 2 * arg + i
                            wait(pe, pt_ready, bb * H + (h - 1))
                            for part, src in enumerate((ph, pl)):
                                for t in range(NKV):
                                    c = (part * NKV + t) * S
                                    mm = nc.tensor.transpose(ps_t[0:KV, i, c:c + S],
                                                             src[:, arg % 4, i, t * KV:(t + 1) * KV],
                                                             ident16[0:S, 0:S])
                            mm.then_inc(p_transposed, 1)
                    elif what == "P":
                        for i in range(2):
                            h = 2 * arg + i
                            pe.wait_ge(pt_ready, bb * H + (h + 1))
                            if h == 0:
                                pe.wait_ge(job_lo, number(b, "V02") + 1)
                                wait(pe, o_ready, b * 2 - 1)
                            if h == 8:
                                pe.wait_ge(job_lo, number(b, "V12") + 1)
                                wait(pe, x_done, b)
                            c = (h % 8) * DH0
                            hc = slice(h * DH0, (h + 1) * DH0)
                            mm = products(nc, ps_o[:, h // 8, c:c + DH0], [
                                (pt[:, h % 4, 0, t, :], pt[:, h % 4, 1, t, :], vh[:, t, hc], vl[:, t, hc])
                                for t in range(NKV)])
                            mm.then_inc(pv_done, 1)
                    elif what == "J":
                        wait(pe, job_lo, number(b, arg) - 1)
                        if arg == "K0":
                            pe.wait_ge(ctx_lo, b + 2)
                        if arg in LASTS:
                            pe.wait_ge(o_ready, b * 2 - (1 if arg == "OT0" else 0))
                        project(arg, bank_of(b, arg), b + (1 if arg == "Q0" else 0))
                    elif what == "W":
                        pe.wait_ge(job_lo, number(b, f"OT{arg}") + 1)
                        for k in range(4 * arg, 4 * arg + 4):
                            for part, (a, w) in enumerate(((oth, 0), (oth, 1), (otl, 0))):
                                mm = nc.tensor.matmul(ps_o[0:S, 1, 0:D], a[:, k, :], wo[:, w, k, :],
                                                      start=(k == 0 and part == 0),
                                                      stop=(k == CK0 - 1 and part == 2))
                        if arg == 1:
                            mm.then_inc(wo_done, 1)

            batches(pe, "pe", body)

        @block.scalar
        def _(act):
            def split_context(b):
                wait(act, ctx_in, 16 * b + 16)
                nc.scalar.activation(ch[:], ctx32[:], ACT.Copy).then_inc(ctx_hi, 1)

            def evacuate(name, bank, number):
                wait(act, job_done, number + 1)
                if name[0] == "V":
                    c, t = int(name[1]), int(name[2])
                    last = nc.scalar.activation(vh[:, t, c * 512:(c + 1) * 512], ps_j[0:KV, bank, :], ACT.Copy)
                elif name[0] == "K":
                    p = int(name[1])
                    for i in range(2):
                        r = slice(64 * i, 64 * i + 64)
                        last = nc.scalar.activation(ks[r, 2 * p + i, :], ps_j[r, bank, 0:NC], ACT.Copy)
                elif name[0] == "Q":
                    p = int(name[1])
                    for i in range(2):
                        r = slice(64 * i, 64 * i + 64)
                        last = nc.scalar.activation(
                            qs[r, 8 * p + i:8 * p + 8:2, 0, :],
                            ps_j[r, bank, 0:4 * S].rearrange("p (h s) -> p h s", h=4), ACT.Copy)
                else:
                    k = 4 * int(name[2])
                    last = nc.scalar.activation(flat(oth[:, k:k + 4, :]), ps_j[:, bank, 0:4 * S], ACT.Copy)
                last.then_inc(job_hi, 1)

            split_context(0)
            for n, name in enumerate(FIRST):
                evacuate(name, n % 2, n)

            def body(b, steps):
                for what, arg, off in steps:
                    if what == "S":
                        act.wait_ge(max_ready, b * NP + (arg + 1))
                        wait(act, pl_done, b * NP + (arg - 1))
                        for i in range(2):
                            h = 2 * arg + i
                            nc.scalar.activation(p32[:, arg % 2, i, :], ps_s[0:S, i, 0:NC], ACT.Exp,
                                                 bias=nb[:, arg % 2, i:i + 1], scale=SC,
                                                 accum_out=rsum[:, h:h + 1]).then_inc(exp_done, 1)
                    elif what == "H":
                        act.wait_ge(exp_done, b * H + (2 * arg + 2))
                        wait(act, p_transposed, b * H + 2 * (arg - 3))
                        nc.scalar.activation(ph[:, arg % 4, :, :], p32[:, arg % 2, :, :], ACT.Copy
                                             ).then_inc(ph_done, 1)
                    elif what == "C":
                        act.wait_ge(job_done, number(b, "V12") + 1)
                        split_context(b + 1)
                    elif what == "J":
                        evacuate(arg, bank_of(b, arg), number(b, arg))

            batches(act, "act", body)

        @block.gpsimd
        def _(pool):
            def low(b, p):
                pool.wait_ge(ph_done, b * NP + (p + 1))
                nc.gpsimd.tensor_tensor(pl[:, p % 4, :, :], p32[:, p % 2, :, :], ph[:, p % 4, :, :],
                                        ALU.subtract).then_inc(pl_done, 1)

            nc.gpsimd.memset(pt[:], 0.0).then_inc(pt_zeroed, 1)
            pool.wait_ge(bo_scaled, 1)
            with pool.Fori(0, B) as b:
                xb = x_res[:, bass.ds(b, 1), :].rearrange("p a d -> p (a d)")
                nc.gpsimd.tensor_tensor(xb, xb, bo_g[:], ALU.add).then_inc(bo_added, 1)
            with pool.Fori(0, B) as b:
                for p in range(NP):
                    low(b, p)

        @block.vector
        def _(dve):
            link = Chain(dve, chain)
            wait(dve, bo_in, 16)
            nc.vector.tensor_scalar(bo_g[:], bo[:], tanh_g[0:S, 0:1], None, ALU.mult).then_inc(bo_scaled, 1)
            link(nc.vector.tensor_scalar(gate[:], tanh_g[0:S, 0:1], 1.0 / (WS * WS), None, ALU.mult))

            def split_context(b):
                wait(dve, ctx_hi, b + 1)
                nc.vector.tensor_tensor(cl[:], ctx32[:], ch[:], ALU.subtract).then_inc(ctx_lo, 1)

            def evacuate(name, bank, number, dup_wait):
                wait(dve, job_hi, number + 1)
                if name[0] == "V":
                    c, t = int(name[1]), int(name[2])
                    cc = slice(c * 512, (c + 1) * 512)
                    last = nc.vector.tensor_tensor(vl[:, t, cc], ps_j[0:KV, bank, :], vh[:, t, cc], ALU.subtract)
                elif name[0] == "K":
                    p = int(name[1])
                    for i in range(2):
                        r, o = slice(64 * i, 64 * i + 64), slice(64 - 64 * i, 128 - 64 * i)
                        last = nc.vector.tensor_tensor(ks[o, 2 * p + i, :], ps_j[r, bank, 0:NC],
                                                       ks[r, 2 * p + i, :], ALU.subtract)
                elif name[0] == "Q":
                    p = int(name[1])
                    for i in range(2):
                        r = slice(64 * i, 64 * i + 64)
                        hh = slice(8 * p + i, 8 * p + 8, 2)
                        last = nc.vector.tensor_tensor(
                            qs[r, hh, 1, :], ps_j[r, bank, 0:4 * S].rearrange("p (h s) -> p h s", h=4),
                            qs[r, hh, 0, :], ALU.subtract)
                    last.then_inc(p_chain, 1)
                    wait(dve, p_chain, dup_wait)
                    for i in range(2):
                        r, o = slice(64 * i, 64 * i + 64), slice(64 - 64 * i, 128 - 64 * i)
                        hh = slice(8 * p + i, 8 * p + 8, 2)
                        last = nc.vector.tensor_copy(qs[o, hh, :, :], qs[r, hh, :, :])
                else:
                    k = 4 * int(name[2])
                    last = nc.vector.tensor_tensor(flat(otl[:, k:k + 4, :]), ps_j[:, bank, 0:4 * S],
                                                   flat(oth[:, k:k + 4, :]), ALU.subtract)
                last.then_inc(job_lo, 1)

            split_context(0)
            for n, name in enumerate(FIRST):
                evacuate(name, n % 2, n, 1)
            wait(dve, pt_zeroed, 1)
            wait(dve, bo_added, B)
            n0 = link.n

            def body(b, steps):
                c = 0

                def chained(instruction):
                    nonlocal c
                    c += 1
                    instruction.then_inc(chain, 1)
                    dve.wait_ge(chain, b * (NP + 2) + (n0 + c - (0 if isinstance(b, int) and b == 0 else 1)))

                for what, arg, off in steps:
                    bb = b + off
                    if what == "S":
                        for i in range(2):
                            h = 2 * arg + i
                            dve.wait_ge(scored, b * H + (h + 1))
                            ins = nc.vector.reduce_max(mx[:, arg % 2, i:i + 1], ps_s[0:S, i, 0:NC], AX.X)
                        chained(ins)
                        nc.vector.tensor_scalar(nb[:, arg % 2, :], mx[:, arg % 2, :], -SC, None, ALU.mult
                                                ).then_inc(max_ready, 1)
                    elif what == "T":
                        for i in range(2):
                            h = 2 * arg + i
                            dve.wait_ge(p_transposed, bb * H + (h + 1))
                            wait(dve, pv_done, bb * H + (h - 3))
                            nc.vector.tensor_copy(
                                pt[:, h % 4, :, :, 0:S].rearrange("p a t s -> p (a t) s"),
                                ps_t[0:KV, i, 0:2 * NKV * S].rearrange("p (a s) -> p a s", a=2 * NKV)
                            ).then_inc(pt_ready, 1)
                    elif what == "C":
                        split_context(b + 1)
                    elif what == "O":
                        hh = slice(8 * arg, 8 * arg + 8)
                        dve.wait_ge(exp_done, bb * H + (8 * arg + 8))
                        chained(nc.vector.reciprocal(rinv[:, hh], rsum[:, hh]))
                        dve.wait_ge(pv_done, bb * H + (8 * arg + 8))
                        nc.vector.tensor_tensor(
                            on[:, 512 * arg:512 * arg + 512].rearrange("p (h d) -> p h d", h=8),
                            ps_o[0:S, arg, :].rearrange("p (h d) -> p h d", h=8),
                            rinv[:, hh].unsqueeze(2).to_broadcast([S, 8, DH0]), ALU.mult).then_inc(o_ready, 1)
                    elif what == "J":
                        evacuate(arg, bank_of(bb, arg), number(bb, arg), b * 2 + (2 + (arg == "Q0")))
                    elif what == "W":
                        xb = x_res[:, bass.ds(bb, 1), :].rearrange("p a d -> p (a d)")
                        dve.wait_ge(wo_done, b)
                        nc.vector.scalar_tensor_tensor(out=xb, in0=ps_o[0:S, 1, 0:D], scalar=gate[:],
                                                       in1=xb, op0=ALU.mult, op1=ALU.add).then_inc(x_done, 1)

            batches(dve, "dve", body)


def feed_forward0_phase(nc, A, x_res, xh, xl, sx, ident32, tanh_g):
    with ExitStack() as ctx:
        sb, ps, sem = make_allocators(nc, ctx)
        wup, wgt = (sb(f"f0_{n}", [128, 2, KD, FF0], F16) for n in ("wup", "wgt"))
        wdn = sb("f0_wdn", [128, 2, OC0, D], F16)
        quantise_weights(nc, A, wup, wgt, wdn, ident32)

        U, G = sb("f0_U", [128, OC0, T]), sb("f0_G", [128, OC0, T])
        sg_t = sb("f0_sig", [128, 2, T])
        m_c = sb("f0_mc", [128, 1])
        mx = sb("f0_mx", [128, 8])
        am = sb("f0_am", [128, 8])
        sc = sb("f0_sc", [128, 16])
        oh, ol = sb("f0_oh", [128, 2, OC0, GW], F16), sb("f0_ol", [128, 2, OC0, GW], F16)
        pj = ps("f0_pj", [128, 6, 512])
        po = ps("f0_po", [128, 2, 512])
        names = ("job_done", "copied", "reduced", "mx_part", "mx_all", "chain", "scal", "g_rounded", "g_int", "sig_done",
                 "u_rounded", "t_done", "g2_rounded", "w_done", "o_rounded", "o_split", "down_done", "x_done")
        (job_done, copied, reduced, mx_part, mx_all, chain, scal, g_rounded, g_int, sig_done, u_rounded, t_done,
         g2_rounded, w_done, o_rounded, o_split, down_done, x_done) = (sem(f"f0_{n}") for n in names)
        NJ = 2 * OC0
        KU = 1.0 / WS
        block = ctx.enter_context(nc.Block())

        @block.tensor
        def _(pe):
            def group(g):
                for j in range(NJ):
                    w, o = (wup, wgt)[j // OC0], j % OC0
                    wait(pe, copied, g * NJ + (j - 5))
                    mm = products(nc, pj[:, j % 6, 0:GW], [
                        (w[:, 0, k, o * 128:(o + 1) * 128], w[:, 1, k, o * 128:(o + 1) * 128],
                         xh[:, k, bass.ds(g * GW, GW)], xl[:, k, bass.ds(g * GW, GW)]) for k in range(KD)])
                    mm.then_inc(job_done, 1)

            group(0)
            with pe.Fori(1, NG) as g:
                group(g)
            for t in range(B):
                g = t // TG
                pe.wait_ge(o_split, g + 1)
                if t >= 2:
                    pe.wait_ge(x_done, t - 1)
                i = t % TG
                mm = products(nc, po[0:S, t % 2, 0:D], [
                    (oh[:, g % 2, o, i * S:(i + 1) * S], ol[:, g % 2, o, i * S:(i + 1) * S],
                     wdn[:, 0, o, :], wdn[:, 1, o, :]) for o in range(OC0)])
                mm.then_inc(down_done, 1)

        def gate_sigmoid(act, o):
            act.wait_ge(g_int, o + 1)
            if o >= 2:
                act.wait_ge(t_done, o - 1)
            nc.scalar.activation(sg_t[:, o % 2, :], G[:, o, :], ACT.Sigmoid, scale=sc[:, 3:4]).then_inc(sig_done, 1)

        @block.scalar
        def _(act):
            with act.Fori(0, NG) as g:
                for j in range(NJ):
                    dst, o = (U, G)[j // OC0], j % OC0
                    act.wait_ge(job_done, g * NJ + (j + 1))
                    nc.scalar.activation(dst[:, o, bass.ds(g * GW, GW)], pj[:, j % 6, 0:GW], ACT.Copy
                                         ).then_inc(copied, 1)
            act.wait_ge(scal, 1)
            for o in range(OC0):
                nc.scalar.activation(G[:, o, :], G[:, o, :], ACT.Identity, bias=m_c[:], scale=sc[:, 2:3]
                                     ).then_inc(g_rounded, 1)
                if o >= 1:
                    gate_sigmoid(act, o - 1)
                nc.scalar.activation(U[:, o, :], U[:, o, :], ACT.Identity, bias=m_c[:], scale=sc[:, 1:2]
                                     ).then_inc(u_rounded, 1)
            gate_sigmoid(act, OC0 - 1)
            act.wait_ge(scal, 2)
            for o in range(OC0):
                nc.scalar.activation(G[:, o, :], G[:, o, :], ACT.Identity, bias=m_c[:], scale=sc[:, 5:6]
                                     ).then_inc(g2_rounded, 1)
            act.wait_ge(scal, 3)
            for g in range(NG):
                cc = slice(g * GW, (g + 1) * GW)
                nc.scalar.activation(G[:, :, cc], G[:, :, cc], ACT.Identity, bias=m_c[:], scale=sc[:, 7:8]
                                     ).then_inc(o_rounded, 1)

        @block.gpsimd
        def _(pool):
            for n in range(3):
                k = 2 if n == 0 else 1
                pool.wait_ge(mx_part, n + 1)
                c = (0, 2, 3)[n]
                nc.gpsimd.partition_all_reduce(am[:, c:c + k], mx[:, c:c + k], 128, bass.bass_isa.ReduceOp.max
                                               ).then_inc(mx_all, 1)

        def gated(dve, link, o, omx):
            dve.wait_ge(sig_done, o + 1)
            st = sg_t[:, o % 2, :]
            link(nc.vector.tensor_scalar(st, st, UQ, MAGIC, ALU.mult, ALU.add))
            link(nc.vector.tensor_scalar(st, st, -MAGIC, UQ - 1.0, ALU.add, ALU.min))
            nc.vector.tensor_tensor(G[:, o, :], st, G[:, o, :], ALU.mult).then_inc(t_done, 1)
            dve.wait_ge(t_done, o + 1)
            link(nc.vector.tensor_reduce(omx[:, 0, o:o + 1], G[:, o, :], AX.X, ALU.max, apply_absolute_value=True))

        def add_down(dve, g, gate):
            for t in range(g * TG, (g + 1) * TG):
                dve.wait_ge(down_done, t + 1)
                nc.vector.scalar_tensor_tensor(out=x_res[:, t, :], in0=po[0:S, t % 2, 0:D], scalar=gate[:],
                                               in1=x_res[:, t, :], op0=ALU.mult, op1=ALU.add).then_inc(x_done, 1)

        @block.vector
        def _(dve):
            link = Chain(dve, chain)
            gmx = sb("f0_gmx", [128, NG, 2])
            omx = sb("f0_omx", [128, 2, OC0])
            gate = sb("f0_gate", [S, 1])
            nc.vector.memset(m_c[:], MAGIC)
            with dve.Fori(0, NG) as g:
                for i, src in enumerate((U, G)):
                    dve.wait_ge(copied, g * NJ + (i + 1) * OC0)
                    nc.vector.tensor_reduce(gmx[:, bass.ds(g, 1), i:i + 1].rearrange("p a b -> p (a b)"),
                                            src[:, :, bass.ds(g * GW, GW)], AX.XY, ALU.max,
                                            apply_absolute_value=True).then_inc(reduced, 1)
            dve.wait_ge(reduced, 2 * NG)
            nc.vector.tensor_reduce(mx[:, 0:2], gmx[:].rearrange("p g i -> p i g"), AX.X, ALU.max
                                    ).then_inc(mx_part, 1)
            dve.wait_ge(mx_all, 1)

            def scale_of(raw_max, unit, scale, inv):
                link(nc.vector.tensor_tensor(sc[:, 15:16], raw_max, unit, ALU.mult))
                link(nc.vector.tensor_scalar(scale, sc[:, 15:16], 1.0 / QMAX, 1e-12, ALU.mult, ALU.max))
                link(nc.vector.reciprocal(sc[:, 14:15], scale))
                link(nc.vector.tensor_tensor(inv, sc[:, 14:15], unit, ALU.mult))

            link(nc.vector.tensor_scalar(sc[:, 0:1], sx[:], KU, None, ALU.mult))
            scale_of(am[:, 0:1], sc[:, 0:1], sc[:, 4:5], sc[:, 1:2])
            scale_of(am[:, 1:2], sc[:, 0:1], sc[:, 3:4], sc[:, 2:3])
            nc.vector.tensor_scalar(sc[:, 9:10], sc[:, 3:4], 1.0 / UQ, None, ALU.mult).then_inc(scal, 1)
            for o in range(OC0):
                dve.wait_ge(g_rounded, o + 1)
                nc.vector.tensor_scalar(G[:, o, :], G[:, o, :], -MAGIC, None, ALU.add).then_inc(g_int, 1)
                if o >= 1:
                    gated(dve, link, o - 1, omx)
            gated(dve, link, OC0 - 1, omx)
            nc.vector.tensor_reduce(mx[:, 2:3], omx[:, 0, :], AX.X, ALU.max).then_inc(mx_part, 1)
            dve.wait_ge(mx_all, 2)
            scale_of(am[:, 2:3], sc[:, 9:10], sc[:, 6:7], sc[:, 5:6])
            nc.vector.tensor_tensor(sc[:, 10:11], sc[:, 6:7], sc[:, 4:5], ALU.mult).then_inc(scal, 1)
            for o in range(OC0):
                dve.wait_ge(g2_rounded, o + 1)
                link(nc.vector.tensor_scalar(G[:, o, :], G[:, o, :], -MAGIC, None, ALU.add))
                dve.wait_ge(u_rounded, o + 1)
                nc.vector.scalar_tensor_tensor(out=G[:, o, :], in0=U[:, o, :], scalar=-MAGIC, in1=G[:, o, :],
                                               op0=ALU.add, op1=ALU.mult).then_inc(w_done, 1)
                dve.wait_ge(w_done, o + 1)
                last = nc.vector.tensor_reduce(omx[:, 1, o:o + 1], G[:, o, :], AX.X, ALU.max,
                                               apply_absolute_value=True)
            link(last)
            nc.vector.tensor_reduce(mx[:, 3:4], omx[:, 1, :], AX.X, ALU.max).then_inc(mx_part, 1)
            dve.wait_ge(mx_all, 3)
            scale_of(am[:, 3:4], sc[:, 10:11], sc[:, 8:9], sc[:, 7:8])
            link(nc.vector.tensor_scalar(gate[:], sc[0:S, 8:9], tanh_g[0:S, 2:3], KU, ALU.mult, ALU.mult))
            nc.vector.tensor_copy(sc[:, 11:12], sc[:, 10:11]).then_inc(scal, 1)
            for g in range(NG):
                cc = slice(g * GW, (g + 1) * GW)
                dve.wait_ge(o_rounded, g + 1)
                if g >= 2:
                    dve.wait_ge(down_done, TG * (g - 1))
                link(nc.vector.tensor_scalar(oh[:, g % 2, :, :], G[:, :, cc], -MAGIC, None, ALU.add))
                nc.vector.scalar_tensor_tensor(out=ol[:, g % 2, :, :], in0=G[:, :, cc], scalar=-MAGIC,
                                               in1=oh[:, g % 2, :, :], op0=ALU.add, op1=ALU.subtract
                                               ).then_inc(o_split, 1)
                if g >= 1:
                    add_down(dve, g - 1, gate)
            add_down(dve, NG - 1, gate)


def quantise_weights(nc, A, wup, wgt, wdn, ident32):
    NU, ND = OC0 * D, KD * FF0
    NW = 2 * NU + ND
    with ExitStack() as ctx:
        sb, ps, sem = make_allocators(nc, ctx)
        w = sb("qw_w", [128, NW])
        q = sb("qw_q", [128, NW])
        bmax, bscale, binv = (sb(f"qw_{n}", [128, NW // QBLK]) for n in ("bmax", "bscale", "binv"))
        tp = ps("qw_tp", [128, 4, 512])
        w_in, chain, ready, transposed, hi_done, lo_done = (sem(f"qw_{n}") for n in (
            "w_in", "chain", "ready", "transposed", "hi_done", "lo_done"))
        groups = []
        for m, dst in enumerate((wup, wgt)):
            for k in range(KD):
                for o0 in range(0, OC0, 3):
                    groups.append((dst, k, o0 * 128, [m * NU + o * D + k * 128 for o in range(o0, o0 + 3)]))
        for k in range(OC0):
            groups.append((wdn, k, 0, [2 * NU + o * FF0 + k * 128 for o in range(KD)]))
        block = ctx.enter_context(nc.Block())

        @block.sync
        def _(sp):
            sp.dma_start(w[:, 0:NU].rearrange("p (o d) -> p o d", o=OC0),
                         A["L0_ffn_w_up"].rearrange("(o p) d -> p o d", p=128)).then_inc(w_in, 16)
            sp.dma_start(w[:, NU:2 * NU].rearrange("p (o d) -> p o d", o=OC0),
                         A["L0_ffn_w_gate"].rearrange("(o p) d -> p o d", p=128)).then_inc(w_in, 16)
            sp.dma_start(w[:, 2 * NU:NW].rearrange("p (o d) -> p o d", o=KD),
                         A["L0_ffn_w_down"].rearrange("(o p) d -> p o d", p=128)).then_inc(w_in, 16)

        @block.vector
        def _(dve):
            link = Chain(dve, chain)
            blocks = lambda a: a[:].rearrange("p (n b) -> p n b", b=QBLK)
            spread = lambda a: a[:].unsqueeze(2).to_broadcast([128, NW // QBLK, QBLK])
            dve.wait_ge(w_in, 48)
            link(nc.vector.tensor_reduce(bmax[:], blocks(w), AX.X, ALU.max, apply_absolute_value=True))
            link(nc.vector.tensor_scalar(bscale[:], bmax[:], 1.0 / 7.0, 1e-12, ALU.mult, ALU.max))
            link(nc.vector.reciprocal(binv[:], bscale[:]))
            link(nc.vector.tensor_tensor(blocks(q), blocks(w), spread(binv), ALU.mult))
            link(nc.vector.tensor_scalar(q[:], q[:], MAGIC, None, ALU.add))
            link(nc.vector.tensor_scalar(q[:], q[:], -MAGIC, 7.0, ALU.add, ALU.min))
            nc.vector.tensor_tensor(blocks(q), blocks(q), spread(bscale), ALU.mult).then_inc(ready, 1)
            for n, (dst, k, c0, srcs) in enumerate(groups):
                dve.wait_ge(hi_done, n + 1)
                cc = slice(c0, c0 + 128 * len(srcs))
                nc.vector.scalar_tensor_tensor(out=dst[:, 1, k, cc], in0=tp[:, n % 4, 0:128 * len(srcs)], scalar=WS,
                                               in1=dst[:, 0, k, cc], op0=ALU.mult, op1=ALU.subtract
                                               ).then_inc(lo_done, 1)

        @block.tensor
        def _(pe):
            pe.wait_ge(ready, 1)
            for n, (dst, k, c0, srcs) in enumerate(groups):
                if n >= 4:
                    pe.wait_ge(lo_done, n - 3)
                for i, s in enumerate(srcs):
                    mm = nc.tensor.transpose(tp[:, n % 4, i * 128:(i + 1) * 128], q[:, s:s + 128], ident32[:])
                mm.then_inc(transposed, 1)

        @block.scalar
        def _(act):
            for n, (dst, k, c0, srcs) in enumerate(groups):
                act.wait_ge(transposed, n + 1)
                nc.scalar.activation(dst[:, 0, k, c0:c0 + 128 * len(srcs)], tp[:, n % 4, 0:128 * len(srcs)],
                                     ACT.Copy, scale=WS).then_inc(hi_done, 1)


def attention1_phase(nc, A, x_res, xh, xl, ident32, ident16, tanh_g):
    SC = float(DH1) ** -0.5 / (WS * WS)
    FILL = -1.0e9 / SC
    HG = 8
    HD = HG * DH1
    with ExitStack() as ctx:
        sb, ps, sem = make_allocators(nc, ctx)
        wq, wk, wv, wo = (sb(f"a1_{n}", [128, 2, KD, D], F16) for n in ("wq", "wk", "wv", "wo"))
        split_phase(nc, "a1w", [
            (A[f"L1_xattn_{n}_w"].rearrange("(k p) n -> p k n", p=128), flat(w[:, 0]), flat(w[:, 1]))
            for n, w in (("wk", wk), ("wq", wq), ("wv", wv), ("wo", wo))], KD * D)

        maskt = sb("a1_mask", [S, B, NC])
        bias_in = sb("a1_bias_in", [128, 3, KD])
        bias = sb("a1_bias", [128, 3, KD])
        bo, bo_g = sb("a1_bo", [S, D]), sb("a1_bo_g", [S, D])
        gate = sb("a1_gate", [S, 1])
        own = sb("a1_own", [128, HG], F16)
        ctx32 = sb("a1_ctx32", [128, KD, NC])
        ch, cl = sb("a1_ch", [128, KD, NC], F16), sb("a1_cl", [128, KD, NC], F16)
        kh, kl = sb("a1_kh", [128, KD, NC], F16), sb("a1_kl", [128, KD, NC], F16)
        q2 = sb("a1_q2", [128, KD, 2, S], F16)
        qm = sb("a1_qm", [128, H, 2, S], F16)
        vh, vl = sb("a1_vh", [KV, NKV, D], F16), sb("a1_vl", [KV, NKV, D], F16)
        s1, fill = sb("a1_s1", [S, 2, NC]), sb("a1_fill", [S, 2, NC])
        s2 = sb("a1_s2", [S, 2, 2, NC])
        p32 = sb("a1_p32", [S, 2, 2, NC])
        ph, pl = sb("a1_ph", [S, 4, 2, NC], F16), sb("a1_pl", [S, 4, 2, NC], F16)
        pt = sb("a1_pt", [KV, 4, 2, NKV, 128], F16)
        mx, nb = sb("a1_mx", [S, 2, 2]), sb("a1_nb", [S, 2, 2])
        rsum, rinv = sb("a1_rsum", [S, B * H]), sb("a1_rinv", [S, H])
        on = sb("a1_on", [S, D])
        oth, otl = sb("a1_oth", [128, KD, S], F16), sb("a1_otl", [128, KD, S], F16)
        ps_s = ps("a1_ps_s", [128, 2, 512])
        ps_t = ps("a1_ps_t", [128, 2, 1024], F16)
        ps_o = ps("a1_ps_o", [128, 512])
        ps_w = ps("a1_ps_w", [128, 512])
        ps_j = ps("a1_ps_j", [128, 2, 512])

        names = ("small_in", "mask_in", "ctx_in", "pt_zeroed", "own_made", "ctx_hi", "ctx_lo", "scored", "masked",
                 "max_ready", "exp_done", "ph_done", "pl_done", "p_transposed", "pt0_ready", "pt1_ready", "pv_done",
                 "job_done", "job_hi", "job_lo", "qm_ready", "o_ready", "wo_done", "x_done", "chain", "bias_ready", "bo_scaled", "bo_added")
        (small_in, mask_in, ctx_in, pt_zeroed, own_made, ctx_hi, ctx_lo, scored, masked, max_ready, exp_done,
         ph_done, pl_done, p_transposed, pt0_ready, pt1_ready, pv_done, job_done, job_hi, job_lo, qm_ready,
         o_ready, wo_done, x_done, chain, bias_ready, bo_scaled, bo_added) = (sem(f"a1_{n}") for n in names)

        FIRST = ["K0", "Q0"]
        JOBS = [["K1"], ["Q1"], ["V0"], ["V1"], ["Q0"], ["OT"], ["K0"], []]
        BODY = [n for js in JOBS for n in js]

        def order(engine, b):
            first, last, drain = b == 0, b == B - 1, b == B
            out = []
            for p in range(NP):
                j = [("J", n, 0) for n in JOBS[p]
                     if not (first and n == "OT") and not (last and n in FIRST) and (not drain or n == "OT")]
                lag2 = ([("T", p - 2, 0)] if p >= 2 and not drain else [("T", NP + p - 2, -1)] if p < 2 and not first
                        else [])
                lag3 = ([("P", p - 3, 0)] if p >= 3 and not drain else [("P", NP + p - 3, -1)] if p < 3 and not first
                        else [])
                scores = [] if drain else [("S", p, 0)]
                context = [("C", None, 0)] if not last and not drain else []
                if engine == "pe":
                    out += scores + lag2 + j + lag3 + ([("W", None, -1)] if p == 6 and not first else [])
                elif engine == "act":
                    out += lag2 + j + scores + [("H", p, 0)] * len(scores) + (context if p == 3 else [])
                elif engine == "pool":
                    out += scores + j
                else:
                    out += [("O", 1, -1)] * (p == 3 and not first) + [("O", 0, 0)] * (p == 7 and not drain)
                    out += [("W", None, -1)] * (p == 7 and not first)
                    out += [("S", p, 0, lag2)] if scores else lag2
                    out += j + (context if p == 4 else [])
            return out

        def number(b, name):
            if isinstance(b, int) and b < 0:
                return FIRST.index(name)
            if isinstance(b, int) and b == 0:
                return len(FIRST) + [n for n in BODY if n != "OT"].index(name)
            if isinstance(b, int) and b == B:
                return B * len(BODY) - 1
            if isinstance(b, int) and name == "OT":
                return b * len(BODY) + (len(FIRST) - 2 + BODY.index(name))
            return b * len(BODY) + (len(FIRST) - 1 + BODY.index(name))

        def bank_of(name):
            return BODY.index(name) % 2

        def walk(eng, engine, body):
            body(0, order(engine, 0))
            with eng.Fori(1, B - 1) as b:
                body(b, order(engine, 1))
            body(B - 1, order(engine, B - 1))
            body(B, order(engine, B))

        def copy_probabilities(copy, h, i):
            return copy(pt[:, h % 4, :, :, 0:S].rearrange("p a t s -> p (a t) s"),
                        ps_t[0:KV, i, 0:2 * NKV * S].rearrange("p (a s) -> p a s", a=2 * NKV))

        block = ctx.enter_context(nc.Block())

        @block.sync
        def _(sp):
            sp.dma_start(ctx32[:], A["ctxT"][:, :, 0:NC].rearrange("k p n -> p k n")).then_inc(ctx_in, 16)
            sp.dma_start(bias_in[:], A["L1_qkv_bT"]).then_inc(small_in, 16)
            sp.dma_start(bo[:], A["L1_xattn_wo_b"].partition_broadcast(S)).then_inc(small_in, 16)
            sp.dma_start(maskt[:], A["mask"].rearrange("b s n -> s b n")).then_inc(mask_in, 16)
            with sp.Fori(1, B) as b:
                sp.wait_ge(ctx_lo, b)
                sp.dma_start(ctx32[:], A["ctxT"][:, :, bass.ds(b * NC, NC)].rearrange("k p n -> p k n")
                             ).then_inc(ctx_in, 16)

        @block.tensor
        def _(pe):
            def project(name, bank, b_next):
                i = int(name[1]) if name != "OT" else 0
                if name[0] == "V":
                    hc = slice(i * HD, (i + 1) * HD)
                    for t in range(NKV):
                        kt = slice(t * KV, (t + 1) * KV)
                        last = products(nc, ps_j[0:KV, bank, t * HD:(t + 1) * HD], [
                            (ch[:, k, kt], cl[:, k, kt], wv[:, 0, k, hc], wv[:, 1, k, hc]) for k in range(KD)])
                elif name[0] == "K":
                    last = products(nc, ps_j[:, bank, 0:NC], [
                        (wk[:, 0, k, i * 128:(i + 1) * 128], wk[:, 1, k, i * 128:(i + 1) * 128],
                         ch[:, k, :], cl[:, k, :]) for k in range(KD)])
                elif name[0] == "Q":
                    last = products(nc, ps_j[:, bank, 0:S], [
                        (wq[:, 0, k, i * 128:(i + 1) * 128], wq[:, 1, k, i * 128:(i + 1) * 128],
                         xh[:, k, bass.ds(b_next * S, S)], xl[:, k, bass.ds(b_next * S, S)]) for k in range(KD)])
                else:
                    for k in range(KD):
                        last = nc.tensor.transpose(ps_j[:, bank, k * S:(k + 1) * S], on[:, k * 128:(k + 1) * 128],
                                                   ident32[0:S, 0:S])
                last.then_inc(job_done, 1)

            pe.wait_ge(ctx_lo, 1)
            for n, name in enumerate(FIRST):
                wait(pe, job_lo, n)
                project(name, bank_of(name), 0)

            def body(b, steps):
                for what, arg, off in steps:
                    bb = b + off
                    if what == "S":
                        if arg % 4 == 0:
                            pe.wait_ge(qm_ready, b * 2 + (1 + arg // 4))
                            pe.wait_ge(job_lo, (number(b - 1, "K0") if arg == 0 else number(b, "K1")) + 1)
                        for i in range(2):
                            h = 2 * arg + i
                            wait(pe, masked, b * NP + arg)
                            for n, (part, keys) in enumerate(((0, kh), (0, kl), (1, kh))):
                                last = nc.tensor.matmul(ps_s[0:S, i, 0:NC], qm[:, h, part, :], keys[:, h // HG, :],
                                                        start=(n == 0), stop=(n == 2))
                            last.then_inc(scored, 1)
                    elif what == "T":
                        pe.wait_ge(pl_done, bb * NP + (arg + 1))
                        for i in range(2):
                            wait(pe, (pt0_ready, pt1_ready)[i], bb * NP + arg)
                            for part, src in enumerate((ph, pl)):
                                for t in range(NKV):
                                    c = (part * NKV + t) * S
                                    mm = nc.tensor.transpose(ps_t[0:KV, i, c:c + S],
                                                             src[:, arg % 4, i, t * KV:(t + 1) * KV],
                                                             ident16[0:S, 0:S])
                            mm.then_inc(p_transposed, 1)
                    elif what == "P":
                        if arg == 0:
                            pe.wait_ge(job_lo, number(b, "V0") + 1)
                            wait(pe, o_ready, b * 2 - 1)
                        if arg == 4:
                            pe.wait_ge(job_lo, number(b, "V1") + 1)
                            wait(pe, x_done, b)
                        for i in range(2):
                            h = 2 * arg + i
                            pe.wait_ge((pt0_ready, pt1_ready)[i], bb * NP + (arg + 1))
                            hc = slice(h * DH1, (h + 1) * DH1)
                            c = h % HG * DH1
                            mm = products(nc, (ps_o, ps_w)[h // HG][:, c:c + DH1], [
                                (pt[:, h % 4, 0, t, :], pt[:, h % 4, 1, t, :], vh[:, t, hc], vl[:, t, hc])
                                for t in range(NKV)])
                            mm.then_inc(pv_done, 1)
                    elif what == "J":
                        wait(pe, job_lo, number(b, arg) - (0 if isinstance(b, int) or arg == BODY[0] else 1))
                        if arg == "K0":
                            pe.wait_ge(ctx_lo, b + 2)
                        if arg == "OT":
                            pe.wait_ge(o_ready, b * 2)
                        project(arg, bank_of(arg), b + (1 if arg == "Q0" else 0))
                    elif what == "W":
                        pe.wait_ge(job_lo, number(b, "OT") + 1)
                        mm = products(nc, ps_w[0:S, 0:D], [
                            (oth[:, k, :], otl[:, k, :], wo[:, 0, k, :], wo[:, 1, k, :]) for k in range(KD)])
                        mm.then_inc(wo_done, 1)

            walk(pe, "pe", body)

        @block.scalar
        def _(act):
            wait(act, small_in, 32)
            nc.scalar.mul(bias[:], bias_in[:], WS).then_inc(bias_ready, 1)
            wait(act, bias_ready, 1)

            def split_context(b):
                wait(act, ctx_in, 16 * b + 16)
                nc.scalar.activation(ch[:], ctx32[:], ACT.Copy).then_inc(ctx_hi, 1)

            def evacuate(name, bank, number, copies=None):
                wait(act, job_done, number + 1)
                i = int(name[1]) if name != "OT" else 0
                if name[0] == "V":
                    nc.scalar.activation(vh[:, :, i * HD:(i + 1) * HD],
                                         ps_j[0:KV, bank, 0:NKV * HD].rearrange("p (t n) -> p t n", t=NKV), ACT.Copy
                                         ).then_inc(job_hi, 1)
                elif name[0] == "K":
                    nc.scalar.activation(kh[:, i, :], ps_j[:, bank, 0:NC], ACT.Identity, bias=bias[:, 1, i:i + 1]
                                         ).then_inc(job_hi, 1)
                elif name[0] == "Q":
                    if copies is not None:
                        wait(act, qm_ready, copies)
                    nc.scalar.activation(q2[:, i, 0, :], ps_j[:, bank, 0:S], ACT.Identity, bias=bias[:, 0, i:i + 1]
                                         ).then_inc(job_hi, 1)
                else:
                    for k in range(KD):
                        last = nc.scalar.activation(oth[:, k, :], ps_j[:, bank, k * S:(k + 1) * S], ACT.Identity,
                                                    bias=bias[:, 2, k:k + 1])
                    last.then_inc(job_hi, 1)

            split_context(0)
            for n, name in enumerate(FIRST):
                evacuate(name, bank_of(name), n)

            def body(b, steps):
                for what, arg, off in steps:
                    bb = b + off
                    if what == "S":
                        act.wait_ge(max_ready, b * NP + (arg + 1))
                        wait(act, pl_done, b * NP + (arg - 1))
                        for i in range(2):
                            h = 2 * arg + i
                            nc.scalar.activation(p32[:, arg % 2, i, :], s2[:, arg % 2, i, :], ACT.Exp,
                                                 bias=nb[:, arg % 2, i:i + 1], scale=SC,
                                                 accum_out=rsum[:, bass.ds(b * H + h, 1)]).then_inc(exp_done, 1)
                    elif what == "H":
                        act.wait_ge(exp_done, b * H + (2 * arg + 2))
                        wait(act, p_transposed, b * H + 2 * (arg - 3))
                        nc.scalar.activation(ph[:, arg % 4, :, :], p32[:, arg % 2, :, :], ACT.Copy
                                             ).then_inc(ph_done, 1)
                    elif what == "T":
                        h = 2 * arg + 1
                        act.wait_ge(p_transposed, bb * H + (h + 1))
                        wait(act, pv_done, bb * H + (h - 3))
                        copy_probabilities(nc.scalar.copy, h, 1).then_inc(pt1_ready, 1)
                    elif what == "C":
                        act.wait_ge(job_done, number(b, "V1") + 1)
                        split_context(b + 1)
                    elif what == "J":
                        evacuate(arg, bank_of(arg), number(b, arg),
                                 b * 2 + (1 if arg == "Q0" else 0) if arg[0] == "Q" else None)

            walk(act, "act", body)

        @block.gpsimd
        def _(pool):
            nc.gpsimd.memset(pt[:], 0.0).then_inc(pt_zeroed, 1)
            nc.gpsimd.memset(own[:], 1.0).then_inc(own_made, 1)
            wait(pool, own_made, 1)
            nc.gpsimd.affine_select(out=own[:], in_=own[:], compare_op=ALU.is_ge, fill=0.0, base=0,
                                    pattern=[[-DH1, HG]], channel_multiplier=1).then_inc(own_made, 1)
            wait(pool, own_made, 2)
            nc.gpsimd.affine_select(out=own[:], in_=own[:], compare_op=ALU.is_ge, fill=0.0, base=DH1 - 1,
                                    pattern=[[DH1, HG]], channel_multiplier=-1).then_inc(own_made, 1)
            wait(pool, own_made, 3)

            def own_rows(g, number):
                wait(pool, job_lo, number + 1)
                nc.gpsimd.tensor_tensor(
                    qm[:, g * HG:(g + 1) * HG, :, :].rearrange("p h a s -> p h (a s)"),
                    q2[:, g, :, :].rearrange("p a s -> p (a s)").unsqueeze(1).to_broadcast([128, HG, 2 * S]),
                    own[:].unsqueeze(2).to_broadcast([128, HG, 2 * S]), ALU.mult).then_inc(qm_ready, 1)

            own_rows(0, FIRST.index("Q0"))
            pool.wait_ge(bo_scaled, 1)
            with pool.Fori(0, B) as b:
                xb = x_res[:, bass.ds(b, 1), :].rearrange("p a d -> p (a d)")
                nc.gpsimd.tensor_tensor(xb, xb, bo_g[:], ALU.add).then_inc(bo_added, 1)

            def body(b, steps):
                for what, arg, off in steps:
                    if what == "S":
                        pool.wait_ge(ph_done, b * NP + (arg + 1))
                        wait(pool, p_transposed, b * H + 2 * (arg - 3))
                        nc.gpsimd.tensor_tensor(pl[:, arg % 4, :, :], p32[:, arg % 2, :, :], ph[:, arg % 4, :, :],
                                                ALU.subtract).then_inc(pl_done, 1)
                    elif arg in ("Q0", "Q1"):
                        wait(pool, scored, b * H + (HG if arg == "Q0" else 0))
                        own_rows(int(arg[1]), number(b, arg))

            walk(pool, "pool", body)

        @block.vector
        def _(dve):
            link = Chain(dve, chain)
            wait(dve, bias_ready, 1)
            nc.vector.tensor_scalar(bo_g[:], bo[:], tanh_g[0:S, 1:2], None, ALU.mult).then_inc(bo_scaled, 1)
            link(nc.vector.tensor_scalar(gate[:], tanh_g[0:S, 1:2], 1.0 / (WS * WS), None, ALU.mult))

            def split_context(b):
                wait(dve, ctx_hi, b + 1)
                nc.vector.tensor_tensor(cl[:], ctx32[:], ch[:], ALU.subtract).then_inc(ctx_lo, 1)

            def low(out, src, b, hi):
                return nc.vector.scalar_tensor_tensor(out=out, in0=src, scalar=b, in1=hi, op0=ALU.add,
                                                      op1=ALU.subtract)

            def evacuate(name, bank, number):
                wait(dve, job_hi, number + 1)
                i = int(name[1]) if name != "OT" else 0
                if name[0] == "V":
                    hc = slice(i * HD, (i + 1) * HD)
                    last = nc.vector.tensor_tensor(
                        vl[:, :, hc], ps_j[0:KV, bank, 0:NKV * HD].rearrange("p (t n) -> p t n", t=NKV),
                        vh[:, :, hc], ALU.subtract)
                elif name[0] == "K":
                    last = low(kl[:, i, :], ps_j[:, bank, 0:NC], bias[:, 1, i:i + 1], kh[:, i, :])
                elif name[0] == "Q":
                    last = low(q2[:, i, 1, :], ps_j[:, bank, 0:S], bias[:, 0, i:i + 1], q2[:, i, 0, :])
                else:
                    for k in range(KD):
                        last = low(otl[:, k, :], ps_j[:, bank, k * S:(k + 1) * S], bias[:, 2, k:k + 1], oth[:, k, :])
                last.then_inc(job_lo, 1)

            split_context(0)
            for n, name in enumerate(FIRST):
                evacuate(name, bank_of(name), n)
            wait(dve, pt_zeroed, 1)
            dve.wait_ge(bo_added, B)
            wait(dve, mask_in, 16)
            n0 = link.n

            per = 2 * NP + 2

            def body(b, steps):
                c = 0

                def chained(instruction):
                    nonlocal c
                    c += 1
                    instruction.then_inc(chain, 1)
                    dve.wait_ge(chain, b * per + (n0 + c - (0 if isinstance(b, int) and b == 0 else 1)))

                def first_probabilities(arg, off):
                    h = 2 * arg
                    dve.wait_ge(p_transposed, (b + off) * H + (h + 1))
                    wait(dve, pv_done, (b + off) * H + (h - 3))
                    copy_probabilities(nc.vector.tensor_copy, h, 0).then_inc(pt0_ready, 1)

                for what, arg, off, *between in steps:
                    bb = b + off
                    if what == "S":
                        dve.wait_ge(scored, b * H + (2 * arg + 2))
                        mb = maskt[:, bass.ds(b, 1), :].to_broadcast([S, 2, NC])
                        ins = nc.vector.tensor_tensor(s1[:], ps_s[0:S, :, 0:NC], mb, ALU.mult)
                        ins.then_inc(masked, 1)
                        dve.wait_ge(masked, b * NP + (arg + 1))
                        chained(nc.vector.tensor_scalar(fill[:], s1[:], 0.0, FILL, ALU.is_equal, ALU.mult))
                        wait(dve, exp_done, b * H + 2 * (arg - 1))
                        for _, pair, distance in between[0]:
                            first_probabilities(pair, distance)
                        for i in range(2):
                            ins = nc.vector.tensor_tensor_reduce(
                                out=s2[:, arg % 2, i, :], in0=s1[:, i, :], in1=fill[:, i, :], scale=1.0,
                                scalar=-3.0e38, op0=ALU.add, op1=ALU.max, accum_out=mx[:, arg % 2, i:i + 1])
                        chained(ins)
                        nc.vector.tensor_scalar(nb[:, arg % 2, :], mx[:, arg % 2, :], -SC, None, ALU.mult
                                                ).then_inc(max_ready, 1)
                    elif what == "T":
                        first_probabilities(arg, off)
                    elif what == "C":
                        split_context(b + 1)
                    elif what == "O":
                        hh = slice(arg * HG, (arg + 1) * HG)
                        dve.wait_ge(exp_done, bb * H + HG * (arg + 1))
                        chained(nc.vector.reciprocal(rinv[:, hh], rsum[:, bass.ds(bb * H + arg * HG, HG)]))
                        dve.wait_ge(pv_done, bb * H + HG * (arg + 1))
                        nc.vector.tensor_tensor(
                            on[:, arg * HD:(arg + 1) * HD].rearrange("p (h d) -> p h d", h=HG),
                            (ps_o, ps_w)[arg][0:S, 0:HD].rearrange("p (h d) -> p h d", h=HG),
                            rinv[:, hh].unsqueeze(2).to_broadcast([S, HG, DH1]), ALU.mult).then_inc(o_ready, 1)
                    elif what == "J":
                        evacuate(arg, bank_of(arg), number(b, arg))
                    elif what == "W":
                        xb = x_res[:, bass.ds(bb, 1), :].rearrange("p a d -> p (a d)")
                        dve.wait_ge(wo_done, b)
                        nc.vector.scalar_tensor_tensor(out=xb, in0=ps_w[0:S, 0:D], scalar=gate[:], in1=xb,
                                                       op0=ALU.mult, op1=ALU.add).then_inc(x_done, 1)

            walk(dve, "dve", body)


def router_phase(nc, A, xh, xl, own_gate, slot_idx, tile_expert, tile_b1, wT, b2, xg, ident32, tanh_g):
    with ExitStack() as ctx:
        sb, ps, sem = make_allocators(nc, ctx)
        rw = sb("r_w", [128, 2, KD, E], F16)
        split_phase(nc, "rw", [(A["router_wT"], flat(rw[:, 0]), flat(rw[:, 1]))], KD * E)
        b1, b2_32 = sb("r_b1", [128, E, HC1]), sb("r_b2", [E + 1, D])
        zeros = sb("r_zeros", [128, D])
        ex, prob = sb("r_ex", [S, B, E]), sb("r_prob", [S, B, E])
        top = sb("r_top", [S, B, 8])
        idx = sb("r_idx", [S, B, 8], U32)
        idxf = sb("r_idxf", [S, B, 2])
        num_e, num_t = sb("r_num_e", [128, E]), sb("r_num_t", [128, MAXT])
        den, rden = sb("r_den", [S, B]), sb("r_rden", [S, B])
        hot = sb("r_hot", [S, 2, B, E])
        both = sb("r_both", [S, B, E], F16)
        share = sb("r_share", [S, 2, B])
        wts, tmp = sb("r_wts", [S, B, E]), sb("r_tmp", [S, B, E])
        before = sb("r_before", [S, 128], F16)
        ones = sb("r_ones", [S, 128], F16)
        sums = sb("r_sums", [128, 2, B, E])
        count = sb("r_count", [128, B, E])
        tiles = sb("r_tiles", [128, E])
        ends = sb("r_ends", [128, 2, E])
        base = sb("r_base", [128, E])
        slot = sb("r_slot", [S, B, E])
        pos = sb("r_pos", [S, 2, B])
        reach = sb("r_reach", [128, MAXT, E])
        tile_ex = sb("r_tile_ex", [128, MAXT])
        bsel = sb("r_bsel", [128, MAXT, HC1, E])
        pr = ps("r_pr", [128, 512])
        pc = ps("r_pc", [128, 2, 512])
        pT = ps("r_pT", [128, 4, 512])
        names = ("b1_in", "b2_in", "logits", "exp_done", "chain", "consts", "both_ready", "ranked", "wts_ready",
                 "ones_set", "transposed", "wT_hi", "b2_hi", "split_done", "z_set", "cleared")
        (b1_in, b2_in, logits, exp_done, chain, consts, both_ready, ranked, wts_ready, ones_set, transposed,
         wT_hi, b2_hi, split_done, z_set, cleared) = (sem(f"r_{n}") for n in names)
        block = ctx.enter_context(nc.Block())

        @block.sync
        def _(sp):
            sp.dma_start(b2_32[:], A["b2"]).then_inc(b2_in, 16)
            sp.dma_start(b1[:], A["b1T"][:, 0:E, :]).then_inc(b1_in, 16)
            sp.wait_ge(z_set, 1)
            sp.dma_start(xg.rearrange("(p r) d -> p r d", p=128),
                         zeros[:].unsqueeze(1).to_broadcast([128, MAXT, D])).then_inc(cleared, 16)
            sp.wait_ge(cleared, 16)

        @block.gpsimd
        def _(pool):
            nc.gpsimd.memset(before[:], 1.0).then_inc(ones_set, 1)
            nc.gpsimd.memset(ones[:], 1.0)
            pool.wait_ge(ones_set, 1)
            nc.gpsimd.affine_select(out=before[:], in_=before[:], compare_op=ALU.is_gt, fill=0.0, base=0,
                                    pattern=[[1, 128]], channel_multiplier=-1)
            nc.gpsimd.iota(num_e[:], pattern=[[1, E]], base=0, channel_multiplier=0,
                           allow_small_or_imprecise_dtypes=True)
            nc.gpsimd.iota(num_t[:], pattern=[[1, MAXT]], base=0, channel_multiplier=0,
                           allow_small_or_imprecise_dtypes=True)
            nc.gpsimd.memset(wT[:, 1], 0.0)
            nc.gpsimd.memset(wT[:, 0], 1.0).then_inc(consts, 1)
            nc.gpsimd.memset(zeros[:], 0.0).then_inc(z_set, 1)

        @block.tensor
        def _(pe):
            for t in range(B):
                tt = slice(t * S, (t + 1) * S)
                mm = products(nc, pr[0:S, t * E:(t + 1) * E], [
                    (xh[:, k, tt], xl[:, k, tt], rw[:, 0, k, :], rw[:, 1, k, :]) for k in range(KD)])
            mm.then_inc(logits, 1)
            pe.wait_ge(consts, 1)
            pe.wait_ge(both_ready, 1)
            for i, m in enumerate((before, ones)):
                mm = nc.tensor.matmul(pc[:, i, 0:B * E], m[:], both[:].rearrange("p t e -> p (t e)"),
                                      start=True, stop=True)
            mm.then_inc(ranked, 1)
            pe.wait_ge(wts_ready, 1)
            for t in range(B):
                mm = nc.tensor.transpose(pT[0:E, t // 4, (t % 4) * S:(t % 4 + 1) * S], wts[:, t, :],
                                         ident32[0:S, 0:S])
            mm.then_inc(transposed, 1)

        @block.scalar
        def _(act):
            act.wait_ge(logits, 1)
            nc.scalar.activation(ex[:], pr[0:S, 0:B * E].rearrange("p (t e) -> p t e", t=B), ACT.Exp,
                                 scale=-1.0 / WS).then_inc(exp_done, 1)
            act.wait_ge(b2_in, 16)
            nc.scalar.activation(b2[:, 0], b2_32[:], ACT.Copy, scale=WS).then_inc(b2_hi, 1)
            act.wait_ge(consts, 1)
            act.wait_ge(transposed, 1)
            nc.scalar.activation(wT[0:E, 0].rearrange("p (g t) s -> p g (t s)", g=4), pT[0:E, :, 0:4 * S],
                                 ACT.Copy).then_inc(wT_hi, 1)

        @block.vector
        def _(dve):
            link = Chain(dve, chain)
            dve.wait_ge(exp_done, 1)
            link(nc.vector.tensor_scalar(ex[:], ex[:], 1.0, None, ALU.add))
            link(nc.vector.reciprocal(prob[:], ex[:]))
            for t in range(B):
                last = nc.vector.max(top[:, t, :], prob[:, t, :])
            link(last)
            for t in range(B):
                last = nc.vector.max_index(idx[:, t, :], top[:, t, :], prob[:, t, :])
            link(last)
            link(nc.vector.tensor_copy(idxf[:], idx[:, :, 0:2]))
            dve.wait_ge(consts, 1)
            for i in range(2):
                link(nc.vector.tensor_tensor(hot[:, i], num_e[0:S].unsqueeze(1).to_broadcast([S, B, E]),
                                             idxf[:, :, i:i + 1].to_broadcast([S, B, E]), ALU.is_equal))
            nc.vector.tensor_tensor(both[:], hot[:, 0], hot[:, 1], ALU.add).then_inc(both_ready, 1)
            link(nc.vector.tensor_tensor(den[:], top[:, :, 0], top[:, :, 1], ALU.add))
            link(nc.vector.tensor_scalar(den[:], den[:], 1e-6, None, ALU.add))
            link(nc.vector.reciprocal(rden[:], den[:]))
            for i in range(2):
                link(nc.vector.tensor_tensor(share[:, i], top[:, :, i], rden[:], ALU.mult))
                link(nc.vector.tensor_scalar(own_gate[:, i], share[:, i], tanh_g[0:S, 3:4], 1.0 / WS, ALU.mult,
                                             ALU.mult))
                link(nc.vector.tensor_tensor((wts, tmp)[i][:], hot[:, i],
                                             share[:, i].unsqueeze(2).to_broadcast([S, B, E]), ALU.mult))
            nc.vector.tensor_tensor(wts[:], wts[:], tmp[:], ALU.add).then_inc(wts_ready, 1)
            dve.wait_ge(ranked, 1)
            link(nc.vector.tensor_copy(count[:], pc[:, 1, 0:B * E].rearrange("p (t e) -> p t e", t=B)))
            src, turn = count[:], 0
            for step in (1, 2, 4, 8):
                dst = sums[:, turn]
                nc.vector.tensor_copy(dst[:, 0:step], src[:, 0:step])
                link(nc.vector.tensor_tensor(dst[:, step:], src[:, step:], src[:, 0:B - step], ALU.add))
                src, turn = dst, 1 - turn
            link(nc.vector.tensor_scalar(tiles[:], src[:, B - 1], 63.5, 1.0 / 128.0, ALU.add, ALU.mult))
            link(nc.vector.tensor_scalar(tiles[:], tiles[:], MAGIC, None, ALU.add))
            link(nc.vector.tensor_scalar(tiles[:], tiles[:], -MAGIC, None, ALU.add))
            run, turn = tiles[:], 0
            for step in (1, 2, 4):
                dst = ends[:, turn]
                nc.vector.tensor_copy(dst[:, 0:step], run[:, 0:step])
                link(nc.vector.tensor_tensor(dst[:, step:], run[:, step:], run[:, 0:E - step], ALU.add))
                run, turn = dst, 1 - turn
            link(nc.vector.tensor_tensor(base[:], run, tiles[:], ALU.subtract))
            link(nc.vector.tensor_scalar(base[:], base[:], 128.0, None, ALU.mult))
            link(nc.vector.tensor_tensor(slot[:], src[0:S], count[0:S], ALU.subtract))
            link(nc.vector.tensor_tensor(slot[:], pc[0:S, 0, 0:B * E].rearrange("p (t e) -> p t e", t=B), slot[:],
                                         ALU.add))
            link(nc.vector.tensor_tensor(slot[:], slot[:], base[0:S].unsqueeze(1).to_broadcast([S, B, E]), ALU.add))
            for i in range(2):
                link(nc.vector.tensor_tensor(tmp[:], hot[:, i], slot[:], ALU.mult))
                link(nc.vector.tensor_reduce(pos[:, i], tmp[:], AX.X, ALU.add))
            nc.vector.tensor_copy(slot_idx[:], pos[:])
            link(nc.vector.tensor_tensor(reach[:, :, 0:E - 1], num_t[:].unsqueeze(2).to_broadcast([128, MAXT, E - 1]),
                                         run[:, 0:E - 1].unsqueeze(1).to_broadcast([128, MAXT, E - 1]), ALU.is_ge))
            link(nc.vector.tensor_reduce(tile_ex[:], reach[:, :, 0:E - 1], AX.X, ALU.add))
            nc.vector.tensor_copy(tile_expert[:], tile_ex[0:1, :])
            link(nc.vector.tensor_tensor(reach[:], num_e[:].unsqueeze(1).to_broadcast([128, MAXT, E]),
                                         tile_ex[:].unsqueeze(2).to_broadcast([128, MAXT, E]), ALU.is_equal))
            dve.wait_ge(b1_in, 16)
            for j in range(HC1):
                last = nc.vector.tensor_tensor(bsel[:, :, j, :], reach[:],
                                               b1[:, :, j].unsqueeze(1).to_broadcast([128, MAXT, E]), ALU.mult)
            link(last)
            link(nc.vector.tensor_reduce(tile_b1[:], bsel[:], AX.X, ALU.add))
            nc.vector.tensor_scalar(tile_b1[:], tile_b1[:], WS, None, ALU.mult)
            dve.wait_ge(b2_hi, 1)
            nc.vector.scalar_tensor_tensor(out=b2[:, 1], in0=b2_32[:], scalar=WS, in1=b2[:, 0], op0=ALU.mult,
                                           op1=ALU.subtract)
            dve.wait_ge(wT_hi, 1)
            nc.vector.tensor_tensor(wT[0:E, 1].rearrange("p (g t) s -> p g (t s)", g=4), pT[0:E, :, 0:4 * S],
                                    wT[0:E, 0].rearrange("p (g t) s -> p g (t s)", g=4), ALU.subtract
                                    ).then_inc(split_done, 1)


def shared_expert_phase(nc, A, x_res, xh, xl, norm, wh, wl, wT, b2, slot_idx, xg, tanh_g):
    LAG, RING = 3, 4
    CH, LB = 512, 4
    NCH = WN // CH
    PER = NCH // 4
    with ExitStack() as ctx:
        sb, ps, sem = make_allocators(nc, ctx)
        b1 = sb("s_b1", [128, HC1])
        gate = sb("s_gate", [S, 1])
        stage = sb("s_stage", [128, LB, CH])
        h32 = sb("s_h32", [128, 2, GW])
        hh, hl = sb("s_hh", [128, RING, GW], F16), sb("s_hl", [128, RING, GW], F16)
        p1 = ps("s_p1", [128, 4, 512])
        p2 = ps("s_p2", [128, TG, 512])
        names = ("b1_in", "w_hi", "w_lo", "up_done", "relu_done", "h_hi", "h_lo", "down_done",
                 "added", "gate_made", "scattered")
        (b1_in, w_hi, w_lo, up_done, relu_done, h_hi, h_lo, down_done, added, gate_made,
         scattered) = (sem(f"s_{n}") for n in names)
        arrived = [sem(f"s_w_in{i}") for i in range(LB)]
        block = ctx.enter_context(nc.Block())

        def source(e, q):
            c = q * CH
            if c < W1N:
                k, c = c // FF1, c % FF1
                return A["w1"][bass.ds(e, 1), k * 128:(k + 1) * 128, c:c + CH].rearrange("e p n -> p (e n)")
            r = (c - W1N) // D * 128
            return A["w2"][bass.ds(e, 1), r:r + (CH // D) * 128, :].rearrange("e (k p) n -> p (e k) n", p=128)

        def place(w, e, q):
            return w[:].rearrange("p e n -> p (e n)")[:, bass.ds(e * WN + q * CH, CH)]

        @block.sync
        def _(sp):
            def load(e, q):
                dst = stage[:, q % LB, :]
                if q * CH >= W1N:
                    dst = dst.rearrange("p (k n) -> p k n", n=D)
                sp.dma_start(dst, source(e, q)).then_inc(arrived[q % LB], 16)

            sp.dma_start(b1[:], A["b1T"][:, E, :]).then_inc(b1_in, 16)
            for q in range(NCH):
                wait(sp, w_lo, q - (LB - 1))
                load(E, q)
            with sp.Fori(0, E) as e:
                for q in range(NCH):
                    sp.wait_ge(w_lo, e * NCH + (NCH + q - (LB - 1)))
                    load(e, q)

        @block.gpsimd
        def _(pool):
            for t in range(B):
                for i in range(2):
                    nc.gpsimd.indirect_dma_start(xg, bass.IndirectOffsetOnAxis(slot_idx[:, i, t:t + 1], 0),
                                                 norm[:, t, :], None).then_inc(scattered, 16)
            pool.wait_ge(scattered, 2 * B * 16)

        @block.scalar
        def _(act):
            def split(e, slot, q):
                act.wait_ge(arrived[q % LB], (e + 1) * (16 * NCH // LB) + 16 * (q // LB + 1))
                nc.scalar.activation(place(wh, slot, q), stage[:, q % LB, :], ACT.Copy, scale=WS).then_inc(w_hi, 1)

            for q in range(NCH):
                split(-1, E - 1, q)
            act.wait_ge(b1_in, 16)

            def group(g, weights):
                for j in range(HC1):
                    n = g * HC1 + j
                    act.wait_ge(up_done, n + 1)
                    wait(act, h_lo, n - 1)
                    nc.scalar.activation(h32[:, j % 2, :], p1[:, j % 4, 0:GW], ACT.Relu, bias=b1[:, j:j + 1],
                                         scale=1.0 / WS).then_inc(relu_done, 1)
                    act.wait_ge(relu_done, n + 1)
                    wait(act, down_done, n - (RING - 1))
                    nc.scalar.activation(hh[:, j % RING, :], h32[:, j % 2, :], ACT.Copy).then_inc(h_hi, 1)
                    if j // 4 < weights:
                        for q in range(j % 4 * PER, (j % 4 + 1) * PER):
                            split(g * 2 + j // 4, g * 2 + j // 4, q)

            group(0, 2)
            with act.Fori(1, NG - 1) as g:
                group(g, 2)
            group(NG - 1, 1)
            act.wait_ge(down_done, NG * HC1)
            for q in range(NCH):
                split(E - 1, E - 1, q)

        @block.vector
        def _(dve):
            def split(e, slot, q):
                dve.wait_ge(w_hi, e * NCH + (NCH + q + 1))
                nc.vector.scalar_tensor_tensor(out=place(wl, slot, q), in0=stage[:, q % LB, :], scalar=WS,
                                               in1=place(wh, slot, q), op0=ALU.mult, op1=ALU.subtract
                                               ).then_inc(w_lo, 1)

            nc.vector.tensor_scalar(gate[:], tanh_g[0:S, 3:4], 1.0 / WS, None, ALU.mult).then_inc(gate_made, 1)
            for q in range(NCH):
                split(-1, E - 1, q)
            dve.wait_ge(gate_made, 1)

            def add(g):
                dve.wait_ge(down_done, g * HC1 + HC1)
                for i in range(TG):
                    xt = x_res[:, bass.ds(g * TG + i, 1), :].rearrange("p a d -> p (a d)")
                    nc.vector.scalar_tensor_tensor(out=xt, in0=p2[0:S, i, 0:D], scalar=gate[:], in1=xt,
                                                   op0=ALU.mult, op1=ALU.add).then_inc(added, 1)

            def group(g, weights, first=False):
                for j in range(HC1):
                    dve.wait_ge(h_hi, g * HC1 + (j + 1))
                    nc.vector.tensor_tensor(hl[:, j % RING, :], h32[:, j % 2, :], hh[:, j % RING, :], ALU.subtract
                                            ).then_inc(h_lo, 1)
                    if j == LAG - 1 and not first:
                        add(g - 1)
                    if j // 4 < weights:
                        for q in range(j % 4 * PER, (j % 4 + 1) * PER):
                            split(g * 2 + j // 4, g * 2 + j // 4, q)

            group(0, 2, first=True)
            with dve.Fori(1, NG - 1) as g:
                group(g, 2)
            group(NG - 1, 1)
            add(NG - 1)
            for q in range(NCH):
                split(E - 1, E - 1, q)

        @block.tensor
        def _(pe):
            w1h, w1l = (w[:, E - 1, 0:W1N].rearrange("p (k n) -> p k n", k=KD) for w in (wh, wl))
            w2h, w2l = (w[:, E - 1, W1N:].rearrange("p (k n) -> p k n", k=HC1) for w in (wh, wl))
            pe.wait_ge(w_lo, NCH)

            def second(g, j):
                if j == 0:
                    wait(pe, added, g * TG)
                    for i in range(TG):
                        wt = [wT[:, part, bass.ds(g * TG + i, 1), :].rearrange("p a s -> p (a s)") for part in (0, 1)]
                        for part, (a, b) in enumerate(((0, 0), (0, 1), (1, 0))):
                            nc.tensor.matmul(p2[0:S, i, 0:D], wt[a], b2[:, b], start=(part == 0), stop=False)
                pe.wait_ge(h_lo, g * HC1 + (j + 1))
                for i in range(TG):
                    ii, r = slice(i * S, (i + 1) * S), j % RING
                    for part, (a, b) in enumerate(((hh, w2h), (hh, w2l), (hl, w2h))):
                        mm = nc.tensor.matmul(p2[0:S, i, 0:D], a[:, r, ii], b[:, j, :], start=False,
                                              stop=(j == HC1 - 1 and part == 2))
                mm.then_inc(down_done, 1)

            def group(g, first=False):
                for j in range(HC1):
                    wait(pe, relu_done, g * HC1 + (j - 3))
                    jj = slice(j * 128, (j + 1) * 128)
                    products(nc, p1[:, j % 4, 0:GW], [
                        (w1h[:, k, jj], w1l[:, k, jj], xh[:, k, bass.ds(g * GW, GW)], xl[:, k, bass.ds(g * GW, GW)])
                        for k in range(KD)]).then_inc(up_done, 1)
                    if j >= LAG:
                        second(g, j - LAG)
                    elif not first:
                        second(g - 1, j + HC1 - LAG)

            group(0, first=True)
            with pe.Fori(1, NG) as g:
                group(g)
            for j in range(HC1 - LAG, HC1):
                second(NG - 1, j)


def routed_experts_phase(nc, x_res, wh, wl, own_gate, slot_idx, tile_expert, tile_b1, xg, yg, out, ident32):
    RT = 4
    with ExitStack() as ctx:
        sb, ps, sem = make_allocators(nc, ctx)
        xt32 = sb("e_xt32", [128, 2, D])
        xth, xtl = sb("e_xth", [128, 2, D], F16), sb("e_xtl", [128, 2, D], F16)
        hb, h32 = sb("e_hb", [128, 2, 512]), sb("e_h32", [128, 2, 512])
        hh, hl = sb("e_hh", [128, 2, FF1], F16), sb("e_hl", [128, 2, FF1], F16)
        y = sb("e_y", [128, 2, D])
        yt = sb("e_yt", [S, RT, 2, D])
        px = ps("e_px", [128, 512])
        p1 = ps("e_p1", [128, 4, 512])
        p2 = ps("e_p2", [128, 2, 512])
        names = ("xt_in0", "xt_in1", "x_transposed", "x_hi", "x_lo", "up_done", "biased", "relu_done", "h_hi", "h_lo",
                 "down_done", "y_ready", "y_out", "added1", "added", "stored")
        (xt_in0, xt_in1, x_transposed, x_hi, x_lo, up_done, biased, relu_done, h_hi, h_lo, down_done, y_ready,
         y_out, added1, added, stored) = (sem(f"e_{n}") for n in names)
        xt_in = (xt_in0, xt_in1)
        got = [sem(f"e_got{i}") for i in range(RT)]
        y_outs = (y_out, sem("e_y_out1"))
        block = ctx.enter_context(nc.Block())

        def walk(eng, body):
            for i in range(3):
                body(i, i % 2)
            with eng.Fori(0, (MAXT - 5) // 2) as r:
                for par in (1, 0):
                    body(r * 2 + (4 - par), par)
            for i in range(3 + (MAXT - 5) // 2 * 2, MAXT + 1):
                body(i, i % 2)

        def given(i, low, high):
            return not isinstance(i, int) or low <= i <= high

        @block.sync
        def _(sp):
            def load(i, par):
                wait(sp, x_transposed, i - 1)
                sp.dma_start(xt32[:, par, :], xg[bass.ds(i * 128, 128), :]).then_inc(xt_in[par], 16)

            load(0, 0)

            def body(i, par):
                if given(i, 0, MAXT - 2):
                    load(i + 1, 1 - par)

            walk(sp, body)
            for t in range(B):
                sp.wait_ge(added, t + 1)
                sp.dma_start(out[t], x_res[:, t, :]).then_inc(stored, 16)
            sp.wait_ge(stored, B * 16)

        @block.tensor
        def _(pe):
            wfh, wfl = (w[:].rearrange("p e n -> p (e n)") for w in (wh, wl))

            def transpose(i, par):
                pe.wait_ge(xt_in[par], 8 * (i - par) + 16)
                wait(pe, x_lo, i)
                for k in range(KD):
                    mm = nc.tensor.transpose(px[:, k * 128:(k + 1) * 128], xt32[:, par, k * 128:(k + 1) * 128],
                                             ident32[:])
                mm.then_inc(x_transposed, 1)

            transpose(0, 0)

            def body(i, par):
                if given(i, 0, MAXT - 2):
                    transpose(i + 1, 1 - par)
                if given(i, 0, MAXT - 1):
                    e = pe.value_load(tile_expert[0:1, bass.ds(i, 1)], min_val=0, max_val=E - 1)
                    pe.wait_ge(x_lo, i + 1)
                    for j in range(HC1):
                        if j % 4 == 0:
                            wait(pe, biased, 2 * (i - 1) + (j // 4 - 1))
                        at = [e * WN + (k * FF1 + j * 128) for k in range(KD)]
                        mm = products(nc, p1[:, 2 * par + j // 4, (j % 4) * 128:(j % 4 + 1) * 128], [
                            (wfh[:, bass.ds(at[k], 128)], wfl[:, bass.ds(at[k], 128)],
                             xth[:, par, k * 128:(k + 1) * 128], xtl[:, par, k * 128:(k + 1) * 128])
                            for k in range(KD)])
                        if j % 4 == 3:
                            mm.then_inc(up_done, 1)
                if given(i, 1, MAXT):
                    e = pe.value_load(tile_expert[0:1, bass.ds(i - 1, 1)], min_val=0, max_val=E - 1)
                    wait(pe, y_ready, i - 2)
                    pe.wait_ge(h_lo, 2 * i)
                    q = 1 - par
                    products(nc, p2[:, q, 0:D], [
                        (hh[:, q, j * 128:(j + 1) * 128], hl[:, q, j * 128:(j + 1) * 128],
                         wfh[:, bass.ds(e * WN + (W1N + j * D), D)], wfl[:, bass.ds(e * WN + (W1N + j * D), D)])
                        for j in range(HC1)]).then_inc(down_done, 1)

            walk(pe, body)

        @block.scalar
        def _(act):
            def split_x(i, par):
                act.wait_ge(x_transposed, i + 1)
                wait(act, up_done, 2 * (i - 1))
                nc.scalar.activation(xth[:, par, :], px[:, 0:D], ACT.Copy).then_inc(x_hi, 1)

            split_x(0, 0)

            def body(i, par):
                if given(i, 0, MAXT - 2):
                    split_x(i + 1, 1 - par)
                if given(i, 0, MAXT - 1):
                    for c in range(2):
                        n = i * 2 + c
                        act.wait_ge(biased, n + 1)
                        wait(act, h_lo, n - 1)
                        nc.scalar.activation(h32[:, c, :], hb[:, c, :], ACT.Relu, scale=1.0 / WS
                                             ).then_inc(relu_done, 1)
                        act.wait_ge(relu_done, n + 1)
                        wait(act, down_done, i - 1)
                        nc.scalar.activation(hh[:, par, c * 512:(c + 1) * 512], h32[:, c, :], ACT.Copy
                                             ).then_inc(h_hi, 1)

            walk(act, body)

        @block.vector
        def _(dve):
            def split_x(i, par):
                dve.wait_ge(x_hi, i + 1)
                nc.vector.tensor_tensor(xtl[:, par, :], px[:, 0:D], xth[:, par, :], ALU.subtract).then_inc(x_lo, 1)

            split_x(0, 0)

            def body(i, par):
                if given(i, 0, MAXT - 2):
                    split_x(i + 1, 1 - par)
                if given(i, 0, MAXT - 1):
                    for c in range(2):
                        n = i * 2 + c
                        dve.wait_ge(up_done, n + 1)
                        wait(dve, relu_done, n - 1)
                        nc.vector.tensor_tensor(
                            hb[:, c, :].rearrange("p (j s) -> p j s", j=4),
                            p1[:, 2 * par + c, :].rearrange("p (j s) -> p j s", j=4),
                            tile_b1[:, bass.ds(i, 1), 4 * c:4 * c + 4].rearrange("p a j -> p (a j)")
                            .unsqueeze(2).to_broadcast([128, 4, 128]), ALU.add).then_inc(biased, 1)
                if given(i, 1, MAXT):
                    dve.wait_ge(down_done, i)
                    q = 1 - par
                    if given(i, 3, MAXT):
                        dve.wait_ge(y_outs[q], 8 * (i - 1 - q))
                    nc.vector.tensor_copy(y[:, q, :], p2[:, q, 0:D]).then_inc(y_ready, 1)
                if given(i, 0, MAXT - 1):
                    for c in range(2):
                        n = i * 2 + c
                        dve.wait_ge(h_hi, n + 1)
                        nc.vector.tensor_tensor(hl[:, par, c * 512:(c + 1) * 512], h32[:, c, :],
                                                hh[:, par, c * 512:(c + 1) * 512], ALU.subtract).then_inc(h_lo, 1)

            walk(dve, body)
            for t in range(B):
                dve.wait_ge(got[t % RT], 32 * (t // RT + 1))
                for i in range(2):
                    ins = nc.vector.scalar_tensor_tensor(out=x_res[:, t, :], in0=yt[:, t % RT, i, :],
                                                         scalar=own_gate[:, i, t:t + 1], in1=x_res[:, t, :],
                                                         op0=ALU.mult, op1=ALU.add)
                    if i == 0:
                        ins.then_inc(added1, 1)
                        dve.wait_ge(added1, t + 1)
                ins.then_inc(added, 1)

        @block.gpsimd
        def _(pool):
            def body(i, par):
                if given(i, 1, MAXT):
                    pool.wait_ge(y_ready, i)
                    nc.gpsimd.dma_start(yg[bass.ds((i - 1) * 128, 128), :], y[:, 1 - par, :]
                                        ).then_inc(y_outs[1 - par], 16)

            walk(pool, body)
            pool.wait_ge(y_outs[0], 16 * ((MAXT + 1) // 2))
            pool.wait_ge(y_outs[1], 16 * (MAXT // 2))
            for t in range(B):
                wait(pool, added, t - (RT - 1))
                for i in range(2):
                    nc.gpsimd.indirect_dma_start(yt[:, t % RT, i, :], None, yg,
                                                 bass.IndirectOffsetOnAxis(slot_idx[:, i, t:t + 1], 0)
                                                 ).then_inc(got[t % RT], 16)


def moe_phase(nc, A, x_res, xh, xl, ident32, tanh_g, xg, yg, out):
    with ExitStack() as ctx:
        sb, ps, sem = make_allocators(nc, ctx)
        own_gate = sb("own_gate", [S, 2, B])
        slot_idx = sb("slot_idx", [S, 2, B], U32)
        tile_expert = sb("tile_expert", [1, MAXT], I32)
        tile_b1 = sb("tile_b1", [128, MAXT, HC1])
        wT, b2 = sb("wT", [E + 1, 2, B, S], F16), sb("b2", [E + 1, 2, D], F16)
        wh, wl = sb("wh", [128, E, WN], F16), sb("wl", [128, E, WN], F16)
        with ExitStack() as c2:
            norm = c2.enter_context(nc.sbuf_tensor("norm", [S, B, D], F32))
            with ExitStack() as c3:
                rms_w = c3.enter_context(nc.sbuf_tensor("rms_w", [S, D], F32))
                w_in = c3.enter_context(nc.semaphore("rms_in"))
                with nc.Block() as block:
                    @block.sync
                    def _(sp):
                        sp.dma_start(rms_w[:], A["L1_ffn_norm_weight"].partition_broadcast(S)).then_inc(w_in, 16)
                        sp.wait_ge(w_in, 16)
                norm_phase(nc, "n3", x_res, ident32, xh, xl, n_out=norm, rms_w=rms_w)
                router_phase(nc, A, xh, xl, own_gate, slot_idx, tile_expert, tile_b1, wT, b2, xg, ident32, tanh_g)
            shared_expert_phase(nc, A, x_res, xh, xl, norm, wh, wl, wT, b2, slot_idx, xg, tanh_g)
        routed_experts_phase(nc, x_res, wh, wl, own_gate, slot_idx, tile_expert, tile_b1, xg, yg, out, ident32)


def program(nc, A, out, phases="0ABCD"):
    with ExitStack() as ctx:
        sb, ps, sem = make_allocators(nc, ctx)
        x_res = sb("x_res", [S, B, D])
        ident32, ident16 = sb("ident32", [128, 128]), sb("ident16", [128, 128], F16)
        gates, tanh_g = sb("gates", [128, 4]), sb("tanh_g", [128, 4])
        xh, xl = sb("xh", [128, KD, T], F16), sb("xl", [128, KD, T], F16)
        sx, sx_inv = sb("sx", [128, 1]), sb("sx_inv", [128, 1])
        xg = nc.dram_tensor("slots_in", (MAXT * 128, D), F32, kind="Internal").ap()
        yg = nc.dram_tensor("slots_out", (MAXT * 128, D), F32, kind="Internal").ap()
        setup_phase(nc, A, x_res, ident32, ident16, gates, tanh_g)
        if "A" in phases:
            norm_phase(nc, "n0", x_res, ident32, xh, xl)
            attention0_phase(nc, A, x_res, xh, xl, ident32, ident16, tanh_g)
        if "B" in phases:
            norm_phase(nc, "n1", x_res, ident32, xh, xl, quant=(sx, sx_inv))
            feed_forward0_phase(nc, A, x_res, xh, xl, sx, ident32, tanh_g)
        if "C" in phases:
            norm_phase(nc, "n2", x_res, ident32, xh, xl)
            attention1_phase(nc, A, x_res, xh, xl, ident32, ident16, tanh_g)
        clear_semaphores(nc)
        if "D" in phases:
            moe_phase(nc, A, x_res, xh, xl, ident32, tanh_g, xg, yg, out)
            return
        with ExitStack() as c2:
            stored = c2.enter_context(nc.semaphore("stored"))
            block = c2.enter_context(nc.Block())

            @block.sync
            def _(sp):
                sp.dma_start(out.rearrange("t s d -> s t d"), x_res[:]).then_inc(stored, 16)
                sp.wait_ge(stored, 16)


def lay_out(inputs, np):
    g = {k: np.ascontiguousarray(v) for k, v in inputs.items()}
    a = {
        "x": g["x"].reshape(T, D),
        "ctxT": g["ctx_1024"].reshape(B * NC, D).T.reshape(KD, 128, B * NC),
        "g_xattn": g["g_xattn"],
        "g_ffn": g["g_ffn"],
    }
    a["mask"] = g["mask_Bx1xSxS2_ff1"].reshape(B, S, NC)
    a["L1_qkv_bT"] = np.stack([g[f"L1_xattn_{n}_b"] for n in ("wq", "wk", "wv")]).reshape(3, KD, 128).transpose(2, 0, 1)
    a["w1"] = np.concatenate([g["L1_ffn_ew1"], g["L1_ffn_sw1"][None]])
    a["w2"] = np.concatenate([g["L1_ffn_ew2"], g["L1_ffn_sw2"][None]])
    a["b1T"] = np.concatenate([g["L1_ffn_eb1"], g["L1_ffn_sb1"][None]]).reshape(E + 1, HC1, 128).transpose(2, 0, 1)
    a["b2"] = np.concatenate([g["L1_ffn_eb2"], g["L1_ffn_sb2"][None]])
    a["router_wT"] = g["L1_ffn_router_w"].T.reshape(KD, 128, E).transpose(1, 0, 2)
    for n in ("L0_xattn_Wq", "L0_xattn_Wk", "L0_xattn_Wv", "L0_xattn_Wo", "L0_xattn_bo", "L0_ffn_w_gate",
              "L0_ffn_w_up", "L0_ffn_w_down", "L1_xattn_wq_w", "L1_xattn_wk_w", "L1_xattn_wv_w", "L1_xattn_wo_w",
              "L1_xattn_wo_b", "L1_ffn_norm_weight"):
        a[n] = g[n]
    return {k: np.ascontiguousarray(v) for k, v in a.items()}


def kernel(**inputs):
    import numpy as _np
    import concourse.bacc as _bacc
    from concourse import mybir as _mybir
    from concourse.bass_utils import run_bass_kernel_spmd as _run

    nc = _bacc.Bacc("TRN2", target_bir_lowering=False, num_devices=1)
    laid = lay_out(inputs, _np)
    arrays = {f"in_{n}": a for n, a in laid.items()}
    args = {n: nc.dram_tensor(f"in_{n}", a.shape, _mybir.dt.from_np(a.dtype), kind="ExternalInput").ap()
            for n, a in laid.items()}
    out = nc.dram_tensor("out_x", (B, S, D), F32, kind="ExternalOutput").ap()
    program(nc, args, out)
    r = _run(nc, [arrays], core_ids=[0])
    return r.results[0]["out_x"]
```

```python
import concourse.bass as bass
from concourse import mybir
from contextlib import ExitStack

F32 = mybir.dt.float32
F16 = mybir.dt.float16
U32 = mybir.dt.uint32
I32 = mybir.dt.int32
ALU = mybir.AluOpType
ACT = mybir.ActivationFunctionType
AX = mybir.AxisListType

B, S, D, NC = 16, 112, 256, 375
T = B * S
KD = D // 128
NKV, KV = 3, 125
H = 16
DH0, DH1 = 64, 16
IN0 = H * DH0
CK0 = IN0 // 128
FF0 = 768
OC0 = FF0 // 128
FF1 = 1024
HC1 = FF1 // 128
E = 8
MAXT = (2 * T + E * 127) // 128
W1N, W2N = KD * FF1, HC1 * D
WN = W1N + W2N
CH, LB = 512, 4
NCH = WN // CH
QBLK = 32
TG = 4
NG = B // TG
GW = TG * S
NP = H // 2

WS = 32.0
MAGIC = 12582912.0
QMAX = 32767.0
UQ = 65536.0


def wait(eng, sem, n):
    if not (isinstance(n, int) and n <= 0):
        eng.wait_ge(sem, n)


class Chain:

    def __init__(self, eng, sem):
        self.eng, self.sem, self.n = eng, sem, 0

    def __call__(self, instruction):
        self.n += 1
        instruction.then_inc(self.sem, 1)
        self.eng.wait_ge(self.sem, self.n)


def make_allocators(nc, ctx):
    def sb(name, shape, dt=F32):
        return ctx.enter_context(nc.sbuf_tensor(name, shape, dt))

    def ps(name, shape, dt=F32):
        return ctx.enter_context(nc.psum_tensor(name, shape, dt))

    def sem(name):
        return ctx.enter_context(nc.semaphore(name))

    return sb, ps, sem


def clear_semaphores(nc):
    used = sorted(nc.released_uncleared_semaphores)
    with nc.Block() as block:
        @block.gpsimd
        def _(pool):
            nc.gpsimd.sem_clear(range(used[0], used[-1] + 1))


def setup_phase(nc, A, x_res, ident32, ident16, gates, x_in, g_in):
    with ExitStack() as ctx:
        sb, ps, sem = make_allocators(nc, ctx)
        zeroed, made = sem("id_zeroed"), sem("id_made")
        block = ctx.enter_context(nc.Block())

        @block.sync
        def _(sp):
            sp.dma_start(x_res[:], A["x"].rearrange("(t p) d -> p t d", p=S)).then_inc(x_in, 16)
            for i, name in enumerate(("g_xattn", "g_ffn")):
                sp.dma_start(gates[:, 2 * i:2 * i + 2], A[name].partition_broadcast(128)).then_inc(g_in, 16)

        @block.gpsimd
        def _(pool):
            for m in (ident32, ident16):
                nc.gpsimd.memset(m[:], 0.0).then_inc(zeroed, 1)
            pool.wait_ge(zeroed, 2)
            for m in (ident32, ident16):
                nc.gpsimd.affine_select(out=m[:], in_=m[:], compare_op=ALU.not_equal, fill=1.0, base=0,
                                        pattern=[[-1, 128]], channel_multiplier=1).then_inc(made, 1)


def norm_phase(nc, tag, x_res, ident32, xh, xl, n_out=None, rms_w=None, quant=None, weights=((), 0), start=None,
               quantiser=None):
    with ExitStack() as ctx:
        sb, ps, sem = make_allocators(nc, ctx)
        stats = sb(f"{tag}_stats", [S, B, 6])
        mv = sb(f"{tag}_mv", [S, B, 2])
        eps = sb(f"{tag}_eps", [S, 1])
        var = sb(f"{tag}_var", [S, B])
        std = sb(f"{tag}_std", [S, B])
        rstd = sb(f"{tag}_rstd", [S, B])
        tmp = sb(f"{tag}_tmp", [S, B])
        xn = n_out if n_out is not None else sb(f"{tag}_xn", [S, B, D])
        amax, inv = sb(f"{tag}_amax", [128, 2]), sb(f"{tag}_inv", [128, 1])
        tp = ps(f"{tag}_tp", [128, 4, 512])
        loads, stage_cols = weights
        SB = 3
        stage = sb(f"{tag}_stage", [128, SB, stage_cols]) if loads else None
        arrived = [sem(f"{tag}_w_in{i}") for i in range(SB)]
        scaled, w_hi, w_lo, rms_in, tanh_done = (sem(f"{tag}_{n}") for n in (
            "scaled", "w_hi", "w_lo", "rms_in", "tanh_done"))
        chain, var_ready, std_ready = sem(f"{tag}_chain"), sem(f"{tag}_var_ready"), sem(f"{tag}_std_ready")
        xn_ready, transposed, hi_done, lo_done = (sem(f"{tag}_{n}") for n in
                                                  ("xn_ready", "transposed", "hi_done", "lo_done"))
        amax_part, amax_all = sem(f"{tag}_amax_part"), sem(f"{tag}_amax_all")
        norms = 1 if rms_w is None else 2
        if quantiser is not None:
            quantiser.allocate(sb, ps, sem)
        block = ctx.enter_context(nc.Block())

        @block.sync
        def _(sp):
            if rms_w is not None:
                sp.dma_start(rms_w[1][:], rms_w[0].partition_broadcast(S)).then_inc(rms_in, 16)
            if quantiser is not None:
                quantiser.load(sp)
            for i, (src, hi, lo) in enumerate(loads):
                wait(sp, w_lo, i - (SB - 1))
                sp.dma_start(stage[:, i % SB, 0:hi.free_size()].rearrange("p (a b) -> p a b", a=src.shape[1]),
                             src).then_inc(arrived[i % SB], 16)

        @block.vector
        def _(dve):
            link = Chain(dve, chain)

            def statistics(src, epsilon, ms):
                for t in range(B):
                    last = nc.vector.bn_stats(stats[:, t, :], src[:, t, :])
                link(last)
                if quantiser is not None:
                    quantiser.block_scales(dve)
                for t in range(B):
                    last = nc.vector.bn_aggr(mv[:, t, :], stats[:, t, :])
                link(last)
                if ms:
                    link(nc.vector.tensor_tensor(tmp[:], mv[:, :, 0], mv[:, :, 0], ALU.mult))
                    link(nc.vector.tensor_tensor(tmp[:], tmp[:], mv[:, :, 1], ALU.add))
                    link(nc.vector.tensor_scalar(var[:], tmp[:], epsilon, None, ALU.add))
                else:
                    link(nc.vector.tensor_scalar(var[:], mv[:, :, 1], epsilon, None, ALU.add))
                nc.vector.tensor_copy(tmp[:], var[:]).then_inc(var_ready, 1)
                dve.wait_ge(std_ready, 2 if ms else 1)
                link(nc.vector.reciprocal(rstd[:], std[:]))
                link(nc.vector.tensor_tensor(tmp[:], rstd[:], rstd[:], ALU.mult))
                link(nc.vector.tensor_tensor(tmp[:], tmp[:], var[:], ALU.mult))
                link(nc.vector.tensor_scalar(tmp[:], tmp[:], -0.5, 1.5, ALU.mult, ALU.add))
                link(nc.vector.tensor_tensor(rstd[:], rstd[:], tmp[:], ALU.mult))

            nc.vector.memset(amax[:], 0.0)
            if start is not None:
                dve.wait_ge(start[0], 16)
            statistics(x_res, 1e-5, False)
            for t in range(B):
                last = nc.vector.tensor_scalar(xn[:, t, :], x_res[:, t, :], mv[:, t, 0:1], rstd[:, t:t + 1],
                                               ALU.subtract, ALU.mult)
                if norms == 1 and quant is None:
                    last.then_inc(xn_ready, 1)
            if norms == 2:
                link(last)
                statistics(xn, 1e-8, True)
                dve.wait_ge(rms_in, 16)
                for t in range(B):
                    nc.vector.scalar_tensor_tensor(out=xn[:, t, :], in0=xn[:, t, :], scalar=rstd[:, t:t + 1],
                                                   in1=rms_w[1][:], op0=ALU.mult, op1=ALU.mult).then_inc(xn_ready, 1)
            if quant is not None:
                link(last)
                nc.vector.tensor_reduce(amax[0:S, 0:1], xn[:], AX.XY, ALU.max,
                                        apply_absolute_value=True).then_inc(amax_part, 1)
                quantiser.integers(dve)
                dve.wait_ge(amax_all, 1)
                link(nc.vector.tensor_scalar(quant[:], amax[:, 1:2], 1.0 / QMAX, 1e-12, ALU.mult, ALU.max))
                link(nc.vector.reciprocal(inv[:], quant[:]))
                link(nc.vector.tensor_scalar(xn[:], xn[:], inv[0:S, :], MAGIC, ALU.mult, ALU.add))
                nc.vector.tensor_scalar(xn[:], xn[:], -MAGIC, None, ALU.add).then_inc(xn_ready, B)
            for j in range(NG * KD):
                g, k = j // KD, j % KD
                dve.wait_ge(hi_done, j + 1)
                nc.vector.tensor_tensor(xl[:, k, g * GW:(g + 1) * GW], tp[:, j % 4, 0:GW],
                                        xh[:, k, g * GW:(g + 1) * GW], ALU.subtract).then_inc(lo_done, 1)
            if quantiser is not None:
                quantiser.low(dve)

        @block.gpsimd
        def _(pool):
            for i, (src, hi, lo) in enumerate(loads):
                pool.wait_ge(w_hi, i + 1)
                nc.gpsimd.tensor_tensor(lo, stage[:, i % SB, 0:hi.free_size()], hi, ALU.subtract).then_inc(w_lo, 1)
            if quant is not None:
                quantiser.divide(pool)
                pool.wait_ge(amax_part, 1)
                nc.gpsimd.partition_all_reduce(amax[:, 1:2], amax[:, 0:1], 128,
                                               bass.bass_isa.ReduceOp.max).then_inc(amax_all, 1)
                quantiser.multiply(pool)

        @block.scalar
        def _(act):
            def split(i):
                src, hi, lo = loads[i]
                st = stage[:, i % SB, 0:hi.free_size()]
                act.wait_ge(arrived[i % SB], 16 * (i // SB + 1))
                nc.scalar.activation(st, st, ACT.Copy, scale=WS).then_inc(scaled, 1)
                act.wait_ge(scaled, i + 1)
                nc.scalar.activation(hi, st, ACT.Copy).then_inc(w_hi, 1)

            for i in range(min(2, len(loads))):
                split(i)
            for n in range(norms):
                act.wait_ge(var_ready, n + 1)
                nc.scalar.activation(std[:], var[:], ACT.Sqrt).then_inc(std_ready, 1)
            if quantiser is not None:
                for m in range(3):
                    quantiser.add_magic(act, m)
            for i in range(2, len(loads)):
                split(i)
            if start is not None:
                _, g_in, gates, tanh_g = start
                act.wait_ge(g_in, 32)
                nc.scalar.activation(tanh_g[:], gates[:], ACT.Tanh).then_inc(tanh_done, 1)
            for j in range(NG * KD):
                g, k = j // KD, j % KD
                act.wait_ge(transposed, j + 1)
                nc.scalar.activation(xh[:, k, g * GW:(g + 1) * GW], tp[:, j % 4, 0:GW],
                                     ACT.Copy).then_inc(hi_done, 1)
            if quantiser is not None:
                quantiser.high(act)

        @block.tensor
        def _(pe):
            for j in range(NG * KD):
                g, k = j // KD, j % KD
                pe.wait_ge(xn_ready, TG * (g + 1))
                if j >= 4:
                    pe.wait_ge(lo_done, j - 3)
                for i in range(TG):
                    last = nc.tensor.transpose(tp[:, j % 4, i * S:(i + 1) * S],
                                               xn[:, g * TG + i, k * 128:(k + 1) * 128], ident32[0:S, 0:S])
                last.then_inc(transposed, 1)
            if quantiser is not None:
                quantiser.transpose(pe)


def flat(ap):
    return ap.rearrange("p a b -> p (a b)")


def products(nc, out, pairs):
    n = len(pairs)
    for i, (wh, wl, mh, ml) in enumerate(pairs):
        nc.tensor.matmul(out, wh, mh, start=(i == 0), stop=False)
        nc.tensor.matmul(out, wh, ml, start=False, stop=False)
        last = nc.tensor.matmul(out, wl, mh, start=False, stop=(i == n - 1))
    return last


def attention0_phase(nc, A, x_res, xh, xl, ident32, ident16, tanh_g, start):
    SC = float(DH0) ** -0.5 / (WS * WS)
    with ExitStack() as ctx:
        sb, ps, sem = make_allocators(nc, ctx)
        wq, wk, wv = (sb(f"a0_{n}", [128, 2, KD, IN0], F16) for n in ("wq", "wk", "wv"))
        wo = sb("a0_wo", [128, 2, CK0, D], F16)
        norm_phase(nc, "n0", x_res, ident32, xh, xl, start=start, weights=([
            (A[n][k * 128:(k + 1) * 128, :].rearrange("p (a b) -> p a b", a=1), w[:, 0, k, :], w[:, 1, k, :])
            for n, w in (("L0_xattn_Wk", wk), ("L0_xattn_Wq", wq), ("L0_xattn_Wv", wv)) for k in range(KD)
        ] + [
            (A["L0_xattn_Wo"].rearrange("(k p) n -> p k n", p=128)[:, 4 * k:4 * k + 4, :],
             flat(wo[:, 0, 4 * k:4 * k + 4, :]), flat(wo[:, 1, 4 * k:4 * k + 4, :])) for k in range(CK0 // 4)
        ], IN0))

        bo = sb("a0_bo", [S, D])
        bo_g = sb("a0_bo_g", [S, D])
        gate = sb("a0_gate", [S, 1])
        ctx32 = sb("a0_ctx32", [128, KD, NC])
        ch, cl = sb("a0_ch", [128, KD, NC], F16), sb("a0_cl", [128, KD, NC], F16)
        ks = sb("a0_ks", [128, H, NC], F16)
        qs = sb("a0_qs", [128, H, 2, S], F16)
        vh, vl = sb("a0_vh", [KV, NKV, IN0], F16), sb("a0_vl", [KV, NKV, IN0], F16)
        p32 = sb("a0_p32", [S, 2, 2, NC])
        ph, pl = sb("a0_ph", [S, 4, 2, NC], F16), sb("a0_pl", [S, 4, 2, NC], F16)
        pt = sb("a0_pt", [KV, 4, 2, NKV, 128], F16)
        mx, nb = sb("a0_mx", [S, 2, 2]), sb("a0_nb", [S, 2, 2])
        rsum, rinv = sb("a0_rsum", [S, H]), sb("a0_rinv", [S, H])
        on = sb("a0_on", [S, IN0])
        oth, otl = sb("a0_oth", [128, CK0, S], F16), sb("a0_otl", [128, CK0, S], F16)
        ps_s = ps("a0_ps_s", [128, 2, 512])
        ps_t = ps("a0_ps_t", [128, 2, 1024], F16)
        ps_o = ps("a0_ps_o", [128, 2, 512])
        ps_j = ps("a0_ps_j", [128, 2, 512])

        names = ("ctx_in", "bo_in", "pt_zeroed", "ctx_hi", "ctx_lo", "scored", "max_ready", "exp_done", "ph_done",
                 "pl_done", "p_transposed", "pt0_ready", "pt1_ready", "pv_done", "job_done", "job_hi", "job_lo",
                 "o_ready", "wo_done", "x_done", "chain", "p_chain", "bo_scaled", "bo_added")
        (ctx_in, bo_in, pt_zeroed, ctx_hi, ctx_lo, scored, max_ready, exp_done, ph_done, pl_done, p_transposed,
         pt0_ready, pt1_ready, pv_done, job_done, job_hi, job_lo, o_ready, wo_done, x_done, chain, p_chain, bo_scaled,
         bo_added) = (
            sem(f"a0_{n}") for n in names)

        FIRST = ["Q0", "K0", "K1", "K2", "K3", "K4", "K5"]
        JOBS = [["V00", "K6"], ["V01", "Q1"], ["V02", "K7"], ["V10", "OT0"],
                ["V11", "OT1", "V12"], ["Q0", "K0"], ["K1", "K2"], ["K3", "K4", "K5"]]
        BODY = [n for js in JOBS for n in js]
        NEXT = BODY.index("Q0")
        NEXTS, LASTS = BODY[NEXT:], ("OT0", "OT1")
        block = ctx.enter_context(nc.Block())

        def order(engine, b):
            first, last, drain = b == 0, b == B - 1, b == B
            out, late = [], []
            for p in range(NP):
                js = [("J", n, 0) for n in JOBS[p]
                      if not (first and n in LASTS) and not (last and n in NEXTS) and (not drain or n in LASTS)]
                now = [("S", p, 0)] if not drain else []
                if engine == "dve":
                    if p == 0 and not first:
                        late = [("J", n, -1) for n in JOBS[-1][-1:]] if not drain else []
                    now += [("O", 1, -1)] * (p == 3 and not first) + [("O", 0, 0)] * (p == 7 and not drain)
                    now += late + [("W", None, -1)] * (p == 6 and not first)
                    now += [("C", None, 0)] * (p == 5 and not last and not drain)
                if engine in ("pe", "act") and len(js) > 1:
                    now.append(js.pop(0))
                if p < 3 and not first and engine == "pe":
                    now.append(("P", p + NP - 3, -1))
                elif p >= 3 and not drain and engine == "pe":
                    now.append(("P", p - 3, 0))
                if engine in ("pe", "dve", "act"):
                    if p < 2 and not first:
                        now.append(("T", p + NP - 2, -1))
                    elif p >= 2 and not drain:
                        now.append(("T", p - 2, 0))
                if engine == "pe" and p == 4 and not first:
                    now.append(("W", 0, -1))
                if engine == "act" and not drain:
                    now.append(("H", p, 0))
                if engine == "dve":
                    now, late = now + js[:-1], js[-1:]
                else:
                    now += js
                if engine == "pe" and p == 5 and not first:
                    now.append(("W", 1, -1))
                if p == 4 and not last and not drain and engine == "act":
                    now.append(("C", None, 0))
                out += now
            return out

        def batches(eng, engine, body):
            body(0, order(engine, 0))
            with eng.Fori(1, B - 1) as b:
                body(b, order(engine, 1))
            body(B - 1, order(engine, B - 1))
            body(B, order(engine, B))

        def number(b, name):
            if isinstance(b, int) and b < 1:
                if name in NEXTS:
                    return (FIRST.index(name) if b < 0 else
                            len(FIRST) - len(LASTS) + BODY.index(name))
                return len(FIRST) + [n for n in BODY if n not in LASTS].index(name)
            if isinstance(b, int) and b == B:
                return B * len(BODY) + (len(FIRST) - len(LASTS) - (len(BODY) - NEXT)) + LASTS.index(name)
            return b * len(BODY) + (len(FIRST) - len(LASTS) + BODY.index(name))

        def bank_of(b, name):
            if isinstance(b, int):
                return number(b, name) % 2
            return (len(FIRST) - len(LASTS) + BODY.index(name)) % 2

        def copy_probabilities(copy, h, i):
            return copy(pt[:, h % 4, :, :, 0:S].rearrange("p a t s -> p (a t) s"),
                        ps_t[0:KV, i, 0:2 * NKV * S].rearrange("p (a s) -> p a s", a=2 * NKV))

        @block.sync
        def _(sp):
            sp.dma_start(bo[:], A["L0_xattn_bo"].partition_broadcast(S)).then_inc(bo_in, 16)
            sp.dma_start(ctx32[:], A["ctxT"][:, :, 0:NC].rearrange("k p n -> p k n")).then_inc(ctx_in, 16)
            with sp.Fori(1, B) as b:
                sp.wait_ge(ctx_lo, b)
                sp.dma_start(ctx32[:], A["ctxT"][:, :, bass.ds(b * NC, NC)].rearrange("k p n -> p k n")
                             ).then_inc(ctx_in, 16)

        @block.tensor
        def _(pe):
            def project(name, bank, b_q):
                if name[0] == "V":
                    c, t = int(name[1]), int(name[2])
                    last = products(nc, ps_j[0:KV, bank, :], [
                        (ch[:, k, t * KV:(t + 1) * KV], cl[:, k, t * KV:(t + 1) * KV],
                         wv[:, 0, k, c * 512:(c + 1) * 512], wv[:, 1, k, c * 512:(c + 1) * 512])
                        for k in range(KD)])
                elif name[0] == "K":
                    p = int(name[1])
                    last = products(nc, ps_j[:, bank, 0:NC], [
                        (wk[:, 0, k, p * 128:(p + 1) * 128], wk[:, 1, k, p * 128:(p + 1) * 128],
                         ch[:, k, :], cl[:, k, :]) for k in range(KD)])
                elif name[0] == "Q":
                    for i in range(4):
                        p = 4 * int(name[1]) + i
                        last = products(nc, ps_j[:, bank, i * S:(i + 1) * S], [
                            (wq[:, 0, k, p * 128:(p + 1) * 128], wq[:, 1, k, p * 128:(p + 1) * 128],
                             xh[:, k, bass.ds(b_q * S, S)], xl[:, k, bass.ds(b_q * S, S)]) for k in range(KD)])
                else:
                    for i in range(4):
                        k = 4 * int(name[2]) + i
                        last = nc.tensor.transpose(ps_j[:, bank, i * S:(i + 1) * S], on[:, k * 128:(k + 1) * 128],
                                                   ident32[0:S, 0:S])
                last.then_inc(job_done, 1)

            pe.wait_ge(ctx_lo, 1)
            for n, name in enumerate(FIRST):
                wait(pe, job_lo, n - 1)
                project(name, n % 2, 0)

            def body(b, steps):
                for what, arg, off in steps:
                    bb = b + off
                    if what == "S":
                        if arg in (0, 1, 2, 3, 5):
                            pe.wait_ge(job_lo, number(b - 1, f"K{arg}") + 1)
                        if arg in (4, 6, 7):
                            pe.wait_ge(job_lo, number(b, "Q1" if arg == 4 else f"K{arg}") + 1)
                        for i in range(2):
                            h = 2 * arg + i
                            wait(pe, exp_done, b * H + (h - 1))
                            for part in range(2):
                                mm = nc.tensor.matmul(ps_s[0:S, i, 0:NC], qs[:, h, part, :], ks[:, h, :],
                                                      start=(part == 0), stop=(part == 1))
                            mm.then_inc(scored, 1)
                    elif what == "T":
                        pe.wait_ge(pl_done, bb * NP + (arg + 1))
                        for i in range(2):
                            h = 2 * arg + i
                            wait(pe, (pt0_ready, pt1_ready)[i], bb * NP + arg)
                            for part, src in enumerate((ph, pl)):
                                for t in range(NKV):
                                    c = (part * NKV + t) * S
                                    mm = nc.tensor.transpose(ps_t[0:KV, i, c:c + S],
                                                             src[:, arg % 4, i, t * KV:(t + 1) * KV],
                                                             ident16[0:S, 0:S])
                            mm.then_inc(p_transposed, 1)
                    elif what == "P":
                        for i in range(2):
                            h = 2 * arg + i
                            pe.wait_ge((pt0_ready, pt1_ready)[i], bb * NP + (arg + 1))
                            if h == 0:
                                pe.wait_ge(job_lo, number(b, "V02") + 1)
                                wait(pe, o_ready, b * 2 - 1)
                            if h == 8:
                                pe.wait_ge(job_lo, number(b, "V12") + 1)
                                wait(pe, x_done, b)
                            c = (h % 8) * DH0
                            hc = slice(h * DH0, (h + 1) * DH0)
                            mm = products(nc, ps_o[:, h // 8, c:c + DH0], [
                                (pt[:, h % 4, 0, t, :], pt[:, h % 4, 1, t, :], vh[:, t, hc], vl[:, t, hc])
                                for t in range(NKV)])
                            mm.then_inc(pv_done, 1)
                    elif what == "J":
                        wait(pe, job_lo, number(b, arg) - 1)
                        if arg == "K0":
                            pe.wait_ge(ctx_lo, b + 2)
                        if arg in LASTS:
                            pe.wait_ge(o_ready, b * 2 - (1 if arg == "OT0" else 0))
                        project(arg, bank_of(b, arg), b + (1 if arg == "Q0" else 0))
                    elif what == "W":
                        pe.wait_ge(job_lo, number(b, f"OT{arg}") + 1)
                        for k in range(4 * arg, 4 * arg + 4):
                            for part, (a, w) in enumerate(((oth, 0), (oth, 1), (otl, 0))):
                                mm = nc.tensor.matmul(ps_o[0:S, 1, 0:D], a[:, k, :], wo[:, w, k, :],
                                                      start=(k == 0 and part == 0),
                                                      stop=(k == CK0 - 1 and part == 2))
                        if arg == 1:
                            mm.then_inc(wo_done, 1)

            batches(pe, "pe", body)

        @block.scalar
        def _(act):
            def split_context(b):
                wait(act, ctx_in, 16 * b + 16)
                nc.scalar.activation(ch[:], ctx32[:], ACT.Copy).then_inc(ctx_hi, 1)

            def evacuate(name, bank, number):
                wait(act, job_done, number + 1)
                if name[0] == "V":
                    c, t = int(name[1]), int(name[2])
                    last = nc.scalar.activation(vh[:, t, c * 512:(c + 1) * 512], ps_j[0:KV, bank, :], ACT.Copy)
                elif name[0] == "K":
                    p = int(name[1])
                    for i in range(2):
                        r = slice(64 * i, 64 * i + 64)
                        last = nc.scalar.activation(ks[r, 2 * p + i, :], ps_j[r, bank, 0:NC], ACT.Copy)
                elif name[0] == "Q":
                    p = int(name[1])
                    for i in range(2):
                        r = slice(64 * i, 64 * i + 64)
                        last = nc.scalar.activation(
                            qs[r, 8 * p + i:8 * p + 8:2, 0, :],
                            ps_j[r, bank, 0:4 * S].rearrange("p (h s) -> p h s", h=4), ACT.Copy)
                else:
                    k = 4 * int(name[2])
                    last = nc.scalar.activation(flat(oth[:, k:k + 4, :]), ps_j[:, bank, 0:4 * S], ACT.Copy)
                last.then_inc(job_hi, 1)

            split_context(0)
            for n, name in enumerate(FIRST):
                evacuate(name, n % 2, n)
            act.wait_ge(pt_zeroed, 1)

            def body(b, steps):
                for what, arg, off in steps:
                    bb = b + off
                    if what == "S":
                        act.wait_ge(max_ready, b * NP + (arg + 1))
                        wait(act, pl_done, b * NP + (arg - 1))
                        for i in range(2):
                            h = 2 * arg + i
                            nc.scalar.activation(p32[:, arg % 2, i, :], ps_s[0:S, i, 0:NC], ACT.Exp,
                                                 bias=nb[:, arg % 2, i:i + 1], scale=SC,
                                                 accum_out=rsum[:, h:h + 1]).then_inc(exp_done, 1)
                    elif what == "H":
                        act.wait_ge(exp_done, b * H + (2 * arg + 2))
                        wait(act, p_transposed, b * H + 2 * (arg - 3))
                        nc.scalar.activation(ph[:, arg % 4, :, :], p32[:, arg % 2, :, :], ACT.Copy
                                             ).then_inc(ph_done, 1)
                    elif what == "T":
                        h = 2 * arg + 1
                        act.wait_ge(p_transposed, bb * H + (h + 1))
                        wait(act, pv_done, bb * H + (h - 3))
                        copy_probabilities(nc.scalar.copy, h, 1).then_inc(pt1_ready, 1)
                    elif what == "C":
                        act.wait_ge(job_done, number(b, "V12") + 1)
                        split_context(b + 1)
                    elif what == "J":
                        evacuate(arg, bank_of(b, arg), number(b, arg))

            batches(act, "act", body)

        @block.gpsimd
        def _(pool):
            def low(b, p):
                pool.wait_ge(ph_done, b * NP + (p + 1))
                nc.gpsimd.tensor_tensor(pl[:, p % 4, :, :], p32[:, p % 2, :, :], ph[:, p % 4, :, :],
                                        ALU.subtract).then_inc(pl_done, 1)

            nc.gpsimd.memset(pt[:], 0.0).then_inc(pt_zeroed, 1)
            pool.wait_ge(bo_scaled, 1)
            with pool.Fori(0, B) as b:
                xb = x_res[:, bass.ds(b, 1), :].rearrange("p a d -> p (a d)")
                nc.gpsimd.tensor_tensor(xb, xb, bo_g[:], ALU.add).then_inc(bo_added, 1)
            with pool.Fori(0, B) as b:
                for p in range(NP):
                    low(b, p)

        @block.vector
        def _(dve):
            link = Chain(dve, chain)
            wait(dve, bo_in, 16)
            nc.vector.tensor_scalar(bo_g[:], bo[:], tanh_g[0:S, 0:1], None, ALU.mult).then_inc(bo_scaled, 1)
            link(nc.vector.tensor_scalar(gate[:], tanh_g[0:S, 0:1], 1.0 / (WS * WS), None, ALU.mult))

            def split_context(b):
                wait(dve, ctx_hi, b + 1)
                nc.vector.tensor_tensor(cl[:], ctx32[:], ch[:], ALU.subtract).then_inc(ctx_lo, 1)

            def evacuate(name, bank, number, dup_wait):
                wait(dve, job_hi, number + 1)
                if name[0] == "V":
                    c, t = int(name[1]), int(name[2])
                    cc = slice(c * 512, (c + 1) * 512)
                    last = nc.vector.tensor_tensor(vl[:, t, cc], ps_j[0:KV, bank, :], vh[:, t, cc], ALU.subtract)
                elif name[0] == "K":
                    p = int(name[1])
                    for i in range(2):
                        r, o = slice(64 * i, 64 * i + 64), slice(64 - 64 * i, 128 - 64 * i)
                        last = nc.vector.tensor_tensor(ks[o, 2 * p + i, :], ps_j[r, bank, 0:NC],
                                                       ks[r, 2 * p + i, :], ALU.subtract)
                elif name[0] == "Q":
                    p = int(name[1])
                    for i in range(2):
                        r = slice(64 * i, 64 * i + 64)
                        hh = slice(8 * p + i, 8 * p + 8, 2)
                        last = nc.vector.tensor_tensor(
                            qs[r, hh, 1, :], ps_j[r, bank, 0:4 * S].rearrange("p (h s) -> p h s", h=4),
                            qs[r, hh, 0, :], ALU.subtract)
                    last.then_inc(p_chain, 1)
                    wait(dve, p_chain, dup_wait)
                    for i in range(2):
                        r, o = slice(64 * i, 64 * i + 64), slice(64 - 64 * i, 128 - 64 * i)
                        hh = slice(8 * p + i, 8 * p + 8, 2)
                        last = nc.vector.tensor_copy(qs[o, hh, :, :], qs[r, hh, :, :])
                else:
                    k = 4 * int(name[2])
                    last = nc.vector.tensor_tensor(flat(otl[:, k:k + 4, :]), ps_j[:, bank, 0:4 * S],
                                                   flat(oth[:, k:k + 4, :]), ALU.subtract)
                last.then_inc(job_lo, 1)

            split_context(0)
            for n, name in enumerate(FIRST):
                evacuate(name, n % 2, n, 1)
            wait(dve, pt_zeroed, 1)
            wait(dve, bo_added, B)
            n0 = link.n

            def body(b, steps):
                c = 0

                def chained(instruction):
                    nonlocal c
                    c += 1
                    instruction.then_inc(chain, 1)
                    dve.wait_ge(chain, b * (NP + 2) + (n0 + c - (0 if isinstance(b, int) and b == 0 else 1)))

                for what, arg, off in steps:
                    bb = b + off
                    if what == "S":
                        for i in range(2):
                            h = 2 * arg + i
                            dve.wait_ge(scored, b * H + (h + 1))
                            ins = nc.vector.reduce_max(mx[:, arg % 2, i:i + 1], ps_s[0:S, i, 0:NC], AX.X)
                        chained(ins)
                        nc.vector.tensor_scalar(nb[:, arg % 2, :], mx[:, arg % 2, :], -SC, None, ALU.mult
                                                ).then_inc(max_ready, 1)
                    elif what == "T":
                        h = 2 * arg
                        dve.wait_ge(p_transposed, bb * H + (h + 1))
                        wait(dve, pv_done, bb * H + (h - 3))
                        copy_probabilities(nc.vector.tensor_copy, h, 0).then_inc(pt0_ready, 1)
                    elif what == "C":
                        split_context(b + 1)
                    elif what == "O":
                        hh = slice(8 * arg, 8 * arg + 8)
                        dve.wait_ge(exp_done, bb * H + (8 * arg + 8))
                        chained(nc.vector.reciprocal(rinv[:, hh], rsum[:, hh]))
                        dve.wait_ge(pv_done, bb * H + (8 * arg + 8))
                        nc.vector.tensor_tensor(
                            on[:, 512 * arg:512 * arg + 512].rearrange("p (h d) -> p h d", h=8),
                            ps_o[0:S, arg, :].rearrange("p (h d) -> p h d", h=8),
                            rinv[:, hh].unsqueeze(2).to_broadcast([S, 8, DH0]), ALU.mult).then_inc(o_ready, 1)
                    elif what == "J":
                        evacuate(arg, bank_of(bb, arg), number(bb, arg), b * 2 + (2 + (arg == "Q0")))
                    elif what == "W":
                        xb = x_res[:, bass.ds(bb, 1), :].rearrange("p a d -> p (a d)")
                        dve.wait_ge(wo_done, b)
                        nc.vector.scalar_tensor_tensor(out=xb, in0=ps_o[0:S, 1, 0:D], scalar=gate[:],
                                                       in1=xb, op0=ALU.mult, op1=ALU.add).then_inc(x_done, 1)

            batches(dve, "dve", body)


def feed_forward0_phase(nc, A, x_res, xh, xl, ident32, tanh_g):
    with ExitStack() as ctx:
        sb, ps, sem = make_allocators(nc, ctx)
        wup, wgt = (sb(f"f0_{n}", [128, 2, KD, FF0], F16) for n in ("wup", "wgt"))
        wdn = sb("f0_wdn", [128, 2, OC0, D], F16)
        sx = sb("f0_sx", [128, 1])
        norm_phase(nc, "n1", x_res, ident32, xh, xl, quant=sx,
                   quantiser=WeightQuantiser(nc, A, wup, wgt, wdn, ident32))

        U, G = sb("f0_U", [128, OC0, T]), sb("f0_G", [128, OC0, T])
        sg_t = sb("f0_sig", [128, 2, T])
        gmx, omx = sb("f0_gmx", [128, NG, 2]), sb("f0_omx", [128, 2, OC0])
        gate = sb("f0_gate", [S, 1])
        m_c, m_neg = sb("f0_mc", [128, 1]), sb("f0_mneg", [128, 1])
        mx = sb("f0_mx", [128, 8])
        am = sb("f0_am", [128, 8])
        sc = sb("f0_sc", [128, 16])
        oh, ol = sb("f0_oh", [128, NG, OC0, GW], F16), sb("f0_ol", [128, NG, OC0, GW], F16)
        pj, po = ps("f0_pj", [128, 6, 512]), ps("f0_po", [128, 2, 512])
        names = ("job_done", "copied", "reduced", "mx_part", "mx_all", "chain", "scal", "g_rounded", "g_int",
                 "sig_done", "u_rounded", "t_done", "g2_rounded", "w_done", "o_rounded", "o_split", "down_done",
                 "x_done", "sig_raw", "g2_int", "o_hi")
        (job_done, copied, reduced, mx_part, mx_all, chain, scal, g_rounded, g_int, sig_done, u_rounded, t_done,
         g2_rounded, w_done, o_rounded, o_split, down_done, x_done,
         sig_raw, g2_int, o_hi) = (sem(f"f0_{n}") for n in names)
        NJ = 2 * OC0
        KU = 1.0 / WS
        block = ctx.enter_context(nc.Block())

        @block.tensor
        def _(pe):
            def group(g):
                for j in range(NJ):
                    w, o = (wup, wgt)[j // OC0], j % OC0
                    wait(pe, copied, g * NJ + (j - 5))
                    mm = products(nc, pj[:, j % 6, 0:GW], [
                        (w[:, 0, k, o * 128:(o + 1) * 128], w[:, 1, k, o * 128:(o + 1) * 128],
                         xh[:, k, bass.ds(g * GW, GW)], xl[:, k, bass.ds(g * GW, GW)]) for k in range(KD)])
                    mm.then_inc(job_done, 1)

            group(0)
            with pe.Fori(1, NG) as g:
                group(g)
            for t in range(B):
                g = t // TG
                pe.wait_ge(o_split, g + 1)
                if t >= 2:
                    pe.wait_ge(x_done, t - 1)
                i = t % TG
                mm = products(nc, po[0:S, t % 2, 0:D], [
                    (oh[:, g, o, i * S:(i + 1) * S], ol[:, g, o, i * S:(i + 1) * S],
                     wdn[:, 0, o, :], wdn[:, 1, o, :]) for o in range(OC0)])
                mm.then_inc(down_done, 1)

        def gate_sigmoid(act, o):
            act.wait_ge(g_int, o + 1)
            if o >= 2:
                act.wait_ge(t_done, o - 1)
            nc.scalar.activation(sg_t[:, o % 2, :], G[:, o, :], ACT.Sigmoid, scale=sc[:, 3:4]).then_inc(sig_raw, 1)
            act.wait_ge(sig_raw, o + 1)
            nc.scalar.activation(sg_t[:, o % 2, :], sg_t[:, o % 2, :], ACT.Identity, bias=m_c[:], scale=UQ
                                 ).then_inc(sig_done, 1)

        @block.scalar
        def _(act):
            with act.Fori(0, NG) as g:
                for j in range(NJ):
                    dst, o = (U, G)[j // OC0], j % OC0
                    act.wait_ge(job_done, g * NJ + (j + 1))
                    nc.scalar.activation(dst[:, o, bass.ds(g * GW, GW)], pj[:, j % 6, 0:GW], ACT.Copy
                                         ).then_inc(copied, 1)
            act.wait_ge(scal, 1)
            for o in range(OC0):
                nc.scalar.activation(G[:, o, :], G[:, o, :], ACT.Identity, bias=m_c[:], scale=sc[:, 2:3]
                                     ).then_inc(g_rounded, 1)
                if o >= 1:
                    gate_sigmoid(act, o - 1)
            gate_sigmoid(act, OC0 - 1)
            act.wait_ge(scal, 2)
            for o in range(OC0 + 1):
                if o < OC0:
                    nc.scalar.activation(G[:, o, :], G[:, o, :], ACT.Identity, bias=m_c[:], scale=sc[:, 5:6]
                                         ).then_inc(g2_rounded, 1)
                if o >= 1:
                    act.wait_ge(g2_rounded, o)
                    nc.scalar.activation(G[:, o - 1, :], G[:, o - 1, :], ACT.Identity, bias=m_neg[:]
                                         ).then_inc(g2_int, 1)
            act.wait_ge(scal, 3)
            for g in range(NG):
                cc = slice(g * GW, (g + 1) * GW)
                nc.scalar.activation(G[:, :, cc], G[:, :, cc], ACT.Identity, bias=m_c[:], scale=sc[:, 7:8]
                                     ).then_inc(o_rounded, 1)
                act.wait_ge(o_rounded, g + 1)
                nc.scalar.activation(oh[:, g, :, :], G[:, :, cc], ACT.Identity, bias=m_neg[:]).then_inc(o_hi, 1)

        @block.gpsimd
        def _(pool):
            for n in range(3):
                k = 2 if n == 0 else 1
                pool.wait_ge(mx_part, n + 1)
                c = (0, 2, 3)[n]
                nc.gpsimd.partition_all_reduce(am[:, c:c + k], mx[:, c:c + k], 128, bass.bass_isa.ReduceOp.max
                                               ).then_inc(mx_all, 1)
                if n == 0:
                    pool.wait_ge(scal, 1)
                    for o in range(OC0):
                        nc.gpsimd.tensor_scalar(U[:, o, :], U[:, o, :], sc[:, 1:2], MAGIC, ALU.mult, ALU.add
                                                ).then_inc(u_rounded, 1)

        def gated(dve, link, o):
            dve.wait_ge(sig_done, o + 1)
            st = sg_t[:, o % 2, :]
            link(nc.vector.tensor_scalar(st, st, -MAGIC, UQ - 1.0, ALU.add, ALU.min))
            nc.vector.tensor_tensor(G[:, o, :], st, G[:, o, :], ALU.mult).then_inc(t_done, 1)
            dve.wait_ge(t_done, o + 1)
            link(nc.vector.tensor_reduce(omx[:, 0, o:o + 1], G[:, o, :], AX.X, ALU.max, apply_absolute_value=True))

        def add_down(dve, g):
            for t in range(g * TG, (g + 1) * TG):
                dve.wait_ge(down_done, t + 1)
                nc.vector.scalar_tensor_tensor(out=x_res[:, t, :], in0=po[0:S, t % 2, 0:D], scalar=gate[:],
                                               in1=x_res[:, t, :], op0=ALU.mult, op1=ALU.add).then_inc(x_done, 1)

        @block.vector
        def _(dve):
            link = Chain(dve, chain)
            nc.vector.memset(m_c[:], MAGIC)
            nc.vector.memset(m_neg[:], -MAGIC)
            with dve.Fori(0, NG) as g:
                for i, src in enumerate((U, G)):
                    dve.wait_ge(copied, g * NJ + (i + 1) * OC0)
                    nc.vector.tensor_reduce(gmx[:, bass.ds(g, 1), i:i + 1].rearrange("p a b -> p (a b)"),
                                            src[:, :, bass.ds(g * GW, GW)], AX.XY, ALU.max,
                                            apply_absolute_value=True).then_inc(reduced, 1)
            dve.wait_ge(reduced, 2 * NG)
            nc.vector.tensor_reduce(mx[:, 0:2], gmx[:].rearrange("p g i -> p i g"), AX.X, ALU.max
                                    ).then_inc(mx_part, 1)
            dve.wait_ge(mx_all, 1)

            def scale_of(raw_max, unit, scale, inv):
                link(nc.vector.tensor_tensor(sc[:, 15:16], raw_max, unit, ALU.mult))
                link(nc.vector.tensor_scalar(scale, sc[:, 15:16], 1.0 / QMAX, 1e-12, ALU.mult, ALU.max))
                link(nc.vector.reciprocal(sc[:, 14:15], scale))
                link(nc.vector.tensor_tensor(inv, sc[:, 14:15], unit, ALU.mult))

            link(nc.vector.tensor_scalar(sc[:, 0:1], sx[:], KU, None, ALU.mult))
            scale_of(am[:, 0:1], sc[:, 0:1], sc[:, 4:5], sc[:, 1:2])
            scale_of(am[:, 1:2], sc[:, 0:1], sc[:, 3:4], sc[:, 2:3])
            nc.vector.tensor_scalar(sc[:, 9:10], sc[:, 3:4], 1.0 / UQ, None, ALU.mult).then_inc(scal, 1)
            for o in range(OC0):
                dve.wait_ge(g_rounded, o + 1)
                nc.vector.tensor_scalar(G[:, o, :], G[:, o, :], -MAGIC, None, ALU.add).then_inc(g_int, 1)
                if o >= 1:
                    gated(dve, link, o - 1)
            gated(dve, link, OC0 - 1)
            nc.vector.tensor_reduce(mx[:, 2:3], omx[:, 0, :], AX.X, ALU.max).then_inc(mx_part, 1)
            dve.wait_ge(mx_all, 2)
            scale_of(am[:, 2:3], sc[:, 9:10], sc[:, 6:7], sc[:, 5:6])
            nc.vector.tensor_tensor(sc[:, 10:11], sc[:, 6:7], sc[:, 4:5], ALU.mult).then_inc(scal, 1)
            for o in range(OC0):
                dve.wait_ge(g2_int, o + 1)
                dve.wait_ge(u_rounded, o + 1)
                nc.vector.scalar_tensor_tensor(out=G[:, o, :], in0=U[:, o, :], scalar=-MAGIC, in1=G[:, o, :],
                                               op0=ALU.add, op1=ALU.mult).then_inc(w_done, 1)
                dve.wait_ge(w_done, o + 1)
                last = nc.vector.tensor_reduce(omx[:, 1, o:o + 1], G[:, o, :], AX.X, ALU.max,
                                               apply_absolute_value=True)
            link(last)
            nc.vector.tensor_reduce(mx[:, 3:4], omx[:, 1, :], AX.X, ALU.max).then_inc(mx_part, 1)
            dve.wait_ge(mx_all, 3)
            scale_of(am[:, 3:4], sc[:, 10:11], sc[:, 8:9], sc[:, 7:8])
            link(nc.vector.tensor_scalar(gate[:], sc[0:S, 8:9], tanh_g[0:S, 2:3], KU, ALU.mult, ALU.mult))
            nc.vector.tensor_copy(sc[:, 11:12], sc[:, 10:11]).then_inc(scal, 1)
            for g in range(NG):
                cc = slice(g * GW, (g + 1) * GW)
                dve.wait_ge(o_hi, g + 1)
                nc.vector.scalar_tensor_tensor(out=ol[:, g, :, :], in0=G[:, :, cc], scalar=-MAGIC,
                                               in1=oh[:, g, :, :], op0=ALU.add, op1=ALU.subtract
                                               ).then_inc(o_split, 1)
                if g >= 1:
                    add_down(dve, g - 1)
            add_down(dve, NG - 1)


class WeightQuantiser:
    NAMES = ("L0_ffn_w_up", "L0_ffn_w_gate", "L0_ffn_w_down")

    def __init__(self, nc, A, wup, wgt, wdn, ident32):
        self.nc, self.A, self.out, self.ident32 = nc, A, (wup, wgt, wdn), ident32

    def allocate(self, sb, ps, sem):
        NU, ND = OC0 * D, KD * FF0
        self.cols = (slice(0, NU), slice(NU, 2 * NU), slice(2 * NU, 2 * NU + ND))
        self.w, self.q = sb("qw_w", [128, 2 * NU + ND]), sb("qw_q", [128, 2 * NU + ND])
        self.bmax, self.bscale, self.binv = (sb(f"qw_{n}", [128, (2 * NU + ND) // QBLK])
                                             for n in ("bmax", "bscale", "binv"))
        self.magic = sb("qw_magic", [128, 1])
        self.tp = ps("qw_tp", [128, 4, 512])
        self.w_in = [sem(f"qw_w_in{m}") for m in range(3)]
        (self.chain, self.scales, self.divided, self.rounded, self.whole, self.ready, self.transposed, self.hi_done,
         self.lo_done) = (sem(f"qw_{n}") for n in ("chain", "scales", "divided", "rounded", "whole", "ready",
                                                   "transposed", "hi_done", "lo_done"))
        self.groups = []
        for m in range(2):
            for k in range(KD):
                for o0 in range(0, OC0, 3):
                    self.groups.append((m, k, o0 * 128, [m * NU + o * D + k * 128 for o in range(o0, o0 + 3)]))
        for k in range(OC0):
            self.groups.append((2, k, 0, [2 * NU + o * FF0 + k * 128 for o in range(KD)]))

    def blocks(self, a, m):
        return a[:, self.cols[m]].rearrange("p (n b) -> p n b", b=QBLK)

    def per_block(self, a, m):
        c = self.cols[m]
        return a[:, c.start // QBLK:c.stop // QBLK]

    def spread(self, a, m):
        one = self.per_block(a, m)
        return one.unsqueeze(2).to_broadcast([128, one.shape[1], QBLK])

    def load(self, sp):
        for m, name in enumerate(self.NAMES):
            c = self.cols[m]
            sp.dma_start(self.w[:, c].rearrange("p (o d) -> p o d", d=self.A[name].shape[1]),
                         self.A[name].rearrange("(o p) d -> p o d", p=128)).then_inc(self.w_in[m], 16)

    def block_scales(self, dve):
        link = Chain(dve, self.chain)
        link(self.nc.vector.memset(self.magic[:], MAGIC))
        for m in range(3):
            dve.wait_ge(self.w_in[m], 16)
            bmax, bscale, binv = (self.per_block(a, m) for a in (self.bmax, self.bscale, self.binv))
            link(self.nc.vector.tensor_reduce(bmax, self.blocks(self.w, m), AX.X, ALU.max,
                                              apply_absolute_value=True))
            link(self.nc.vector.tensor_scalar(bscale, bmax, 1.0 / 7.0, 1e-12, ALU.mult, ALU.max))
            self.nc.vector.reciprocal(binv, bscale).then_inc(self.scales, 1)

    def divide(self, pool):
        for m in range(3):
            pool.wait_ge(self.scales, m + 1)
            self.nc.gpsimd.tensor_tensor(self.blocks(self.q, m), self.blocks(self.w, m), self.spread(self.binv, m),
                                         ALU.mult).then_inc(self.divided, 1)

    def add_magic(self, act, m):
        act.wait_ge(self.divided, m + 1)
        c = self.cols[m]
        self.nc.scalar.activation(self.q[:, c], self.q[:, c], ACT.Identity, bias=self.magic[:]
                                  ).then_inc(self.rounded, 1)

    def integers(self, dve):
        for m in range(3):
            dve.wait_ge(self.rounded, m + 1)
            c = self.cols[m]
            self.nc.vector.tensor_scalar(self.q[:, c], self.q[:, c], -MAGIC, 7.0, ALU.add, ALU.min
                                         ).then_inc(self.whole, 1)

    def multiply(self, pool):
        for m in range(3):
            pool.wait_ge(self.whole, m + 1)
            self.nc.gpsimd.tensor_tensor(self.blocks(self.q, m), self.blocks(self.q, m), self.spread(self.bscale, m),
                                         ALU.mult).then_inc(self.ready, 1)

    def transpose(self, pe):
        for n, (m, k, c0, srcs) in enumerate(self.groups):
            pe.wait_ge(self.ready, m + 1)
            wait(pe, self.lo_done, n - 3)
            for i, s in enumerate(srcs):
                mm = self.nc.tensor.transpose(self.tp[:, n % 4, i * 128:(i + 1) * 128], self.q[:, s:s + 128],
                                              self.ident32[:])
            mm.then_inc(self.transposed, 1)

    def high(self, act):
        for n, (m, k, c0, srcs) in enumerate(self.groups):
            w = 128 * len(srcs)
            act.wait_ge(self.transposed, n + 1)
            self.nc.scalar.activation(self.out[m][:, 0, k, c0:c0 + w], self.tp[:, n % 4, 0:w], ACT.Copy, scale=WS
                                      ).then_inc(self.hi_done, 1)

    def low(self, dve):
        for n, (m, k, c0, srcs) in enumerate(self.groups):
            w = 128 * len(srcs)
            dve.wait_ge(self.hi_done, n + 1)
            self.nc.vector.scalar_tensor_tensor(out=self.out[m][:, 1, k, c0:c0 + w], in0=self.tp[:, n % 4, 0:w],
                                                scalar=WS, in1=self.out[m][:, 0, k, c0:c0 + w], op0=ALU.mult,
                                                op1=ALU.subtract).then_inc(self.lo_done, 1)


def attention1_phase(nc, A, x_res, xh, xl, ident32, ident16, tanh_g):
    SC = float(DH1) ** -0.5 / (WS * WS)
    FILL = -1.0e9 / SC
    HG = 8
    HD = HG * DH1
    with ExitStack() as ctx:
        sb, ps, sem = make_allocators(nc, ctx)
        wq, wk, wv, wo = (sb(f"a1_{n}", [128, 2, KD, D], F16) for n in ("wq", "wk", "wv", "wo"))
        norm_phase(nc, "n2", x_res, ident32, xh, xl, weights=([
            (A[f"L1_xattn_{n}_w"].rearrange("(k p) n -> p k n", p=128), flat(w[:, 0]), flat(w[:, 1]))
            for n, w in (("wk", wk), ("wq", wq), ("wv", wv), ("wo", wo))], KD * D))

        maskt = sb("a1_mask", [S, B, NC])
        bias_in = sb("a1_bias_in", [128, 3, KD])
        bias = sb("a1_bias", [128, 3, KD])
        bo, bo_g = sb("a1_bo", [S, D]), sb("a1_bo_g", [S, D])
        gate = sb("a1_gate", [S, 1])
        own = sb("a1_own", [128, HG], F16)
        ctx32 = sb("a1_ctx32", [128, KD, NC])
        ch, cl = sb("a1_ch", [128, KD, NC], F16), sb("a1_cl", [128, KD, NC], F16)
        kh, kl = sb("a1_kh", [128, KD, NC], F16), sb("a1_kl", [128, KD, NC], F16)
        q2 = sb("a1_q2", [128, KD, 2, S], F16)
        qm = sb("a1_qm", [128, H, 2, S], F16)
        vh, vl = sb("a1_vh", [KV, NKV, D], F16), sb("a1_vl", [KV, NKV, D], F16)
        s1, fill = sb("a1_s1", [S, 2, NC]), sb("a1_fill", [S, 2, NC])
        s2 = sb("a1_s2", [S, 2, 2, NC])
        p32 = sb("a1_p32", [S, 2, 2, NC])
        ph, pl = sb("a1_ph", [S, 4, 2, NC], F16), sb("a1_pl", [S, 4, 2, NC], F16)
        pt = sb("a1_pt", [KV, 4, 2, NKV, 128], F16)
        mx, nb = sb("a1_mx", [S, 2, 2]), sb("a1_nb", [S, 2, 2])
        rsum, rinv = sb("a1_rsum", [S, B * H]), sb("a1_rinv", [S, H])
        on = sb("a1_on", [S, D])
        pad = sb("a1_pad", [S, 1])
        oth, otl = sb("a1_oth", [128, KD, S], F16), sb("a1_otl", [128, KD, S], F16)
        ps_s = ps("a1_ps_s", [128, 2, 512])
        ps_t = ps("a1_ps_t", [128, 2, 1024], F16)
        ps_o = ps("a1_ps_o", [128, 512])
        ps_w = ps("a1_ps_w", [128, 512])
        ps_j = ps("a1_ps_j", [128, 2, 512])

        names = ("small_in", "mask_in", "ctx_in", "pt_zeroed", "own_made", "ctx_hi", "ctx_lo", "scored", "masked",
                 "max_ready", "exp_done", "ph_done", "pl_done", "p_transposed", "pt_ready", "pv_done",
                 "job_done", "job_hi", "job_lo", "qm_ready", "o_ready", "wo_done", "x_done", "chain",
                 "bias_ready", "bo_scaled", "bo_added")
        (small_in, mask_in, ctx_in, pt_zeroed, own_made, ctx_hi, ctx_lo, scored, masked, max_ready, exp_done,
         ph_done, pl_done, p_transposed, pt_ready, pv_done, job_done, job_hi, job_lo, qm_ready,
         o_ready, wo_done, x_done, chain, bias_ready, bo_scaled, bo_added) = (sem(f"a1_{n}") for n in names)

        FIRST = ["K0", "Q0"]
        JOBS = [["Q1"], ["K1"], ["V0"], ["V1"], ["Q0"], ["OT"], ["K0"], []]
        BODY = [n for js in JOBS for n in js]

        def order(engine, b):
            first, last, drain = b == 0, b == B - 1, b == B
            out = []
            for p in range(NP):
                j = [("J", n, 0) for n in JOBS[p]
                     if not (first and n == "OT") and not (last and n in FIRST) and (not drain or n == "OT")]
                lag2 = ([("T", p - 2, 0)] if p >= 2 and not drain else [("T", NP + p - 2, -1)] if p < 2 and not first
                        else [])
                lag3 = ([("P", p - 3, 0)] if p >= 3 and not drain else [("P", NP + p - 3, -1)] if p < 3 and not first
                        else [])
                scores = [] if drain else [("S", p, 0)]
                context = [("C", None, 0)] if not last and not drain else []
                if engine == "pe":
                    out += scores + lag2 + j + lag3 + ([("W", None, -1)] if p == 6 and not first else [])
                elif engine == "act":
                    out += j + lag2 + scores + [("H", p, 0)] * len(scores) + (context if p == 3 else [])
                elif engine == "pool":
                    out += scores + j
                else:
                    out += [("O", 1, -1)] * (p == 3 and not first) + [("O", 0, 0)] * (p == 7 and not drain)
                    out += [("W", None, -1)] * (p == 7 and not first)
                    out += scores + j + (context if p == 4 else [])
            return out

        def number(b, name):
            known = isinstance(b, int)
            if known and b < 0:
                return FIRST.index(name)
            if known and b == 0:
                return len(FIRST) + [n for n in BODY if n != "OT"].index(name)
            start = b * len(BODY) + (len(FIRST) - 1)
            if known and b == B:
                return start - len(FIRST)
            names = [n for n in BODY if n not in FIRST] if known and b == B - 1 else BODY
            return start + names.index(name)

        def bank_of(name):
            return BODY.index(name) % 2

        def walk(eng, engine, body):
            body(0, order(engine, 0))
            with eng.Fori(1, B - 1) as b:
                body(b, order(engine, 1))
            body(B - 1, order(engine, B - 1))
            body(B, order(engine, B))

        block = ctx.enter_context(nc.Block())

        @block.sync
        def _(sp):
            sp.dma_start(ctx32[:], A["ctxT"][:, :, 0:NC].rearrange("k p n -> p k n")).then_inc(ctx_in, 16)
            sp.dma_start(bias_in[:], A["L1_qkv_bT"]).then_inc(small_in, 16)
            sp.dma_start(bo[:], A["L1_xattn_wo_b"].partition_broadcast(S)).then_inc(small_in, 16)
            sp.dma_start(maskt[:], A["mask"].rearrange("b s n -> s b n")).then_inc(mask_in, 16)
            with sp.Fori(1, B) as b:
                sp.wait_ge(ctx_lo, b)
                sp.dma_start(ctx32[:], A["ctxT"][:, :, bass.ds(b * NC, NC)].rearrange("k p n -> p k n")
                             ).then_inc(ctx_in, 16)

        @block.tensor
        def _(pe):
            def project(name, bank, b_next):
                i = int(name[1]) if name != "OT" else 0
                if name[0] == "V":
                    hc = slice(i * HD, (i + 1) * HD)
                    for t in range(NKV):
                        kt = slice(t * KV, (t + 1) * KV)
                        last = products(nc, ps_j[0:KV, bank, t * HD:(t + 1) * HD], [
                            (ch[:, k, kt], cl[:, k, kt], wv[:, 0, k, hc], wv[:, 1, k, hc]) for k in range(KD)])
                elif name[0] == "K":
                    last = products(nc, ps_j[:, bank, 0:NC], [
                        (wk[:, 0, k, i * 128:(i + 1) * 128], wk[:, 1, k, i * 128:(i + 1) * 128],
                         ch[:, k, :], cl[:, k, :]) for k in range(KD)])
                elif name[0] == "Q":
                    last = products(nc, ps_j[:, bank, 0:S], [
                        (wq[:, 0, k, i * 128:(i + 1) * 128], wq[:, 1, k, i * 128:(i + 1) * 128],
                         xh[:, k, bass.ds(b_next * S, S)], xl[:, k, bass.ds(b_next * S, S)]) for k in range(KD)])
                else:
                    for k in range(KD):
                        last = nc.tensor.transpose(ps_j[:, bank, k * S:(k + 1) * S], on[:, k * 128:(k + 1) * 128],
                                                   ident32[0:S, 0:S])
                last.then_inc(job_done, 1)

            pe.wait_ge(ctx_lo, 1)
            for n, name in enumerate(FIRST):
                wait(pe, job_lo, n)
                project(name, bank_of(name), 0)

            def body(b, steps):
                for what, arg, off in steps:
                    bb = b + off
                    if what == "S":
                        if arg % 4 == 0:
                            pe.wait_ge(qm_ready, b * 2 + (1 + arg // 4))
                            pe.wait_ge(job_lo, (number(b - 1, "K0") if arg == 0 else number(b, "K1")) + 1)
                        for i in range(2):
                            h = 2 * arg + i
                            wait(pe, masked, b * NP + arg)
                            for n, (part, keys) in enumerate(((0, kh), (0, kl), (1, kh))):
                                last = nc.tensor.matmul(ps_s[0:S, i, 0:NC], qm[:, h, part, :], keys[:, h // HG, :],
                                                        start=(n == 0), stop=(n == 2))
                            last.then_inc(scored, 1)
                    elif what == "T":
                        pe.wait_ge(pl_done, bb * NP + (arg + 1))
                        for i in range(2):
                            wait(pe, pt_ready, bb * H + (2 * arg + i - 1))
                            for part, src in enumerate((ph, pl)):
                                for t in range(NKV):
                                    c = (part * NKV + t) * S
                                    mm = nc.tensor.transpose(ps_t[0:KV, i, c:c + S],
                                                             src[:, arg % 4, i, t * KV:(t + 1) * KV],
                                                             ident16[0:S, 0:S])
                            mm.then_inc(p_transposed, 1)
                    elif what == "P":
                        if arg == 0:
                            pe.wait_ge(job_lo, number(b, "V0") + 1)
                            wait(pe, o_ready, b * 2 - 1)
                        if arg == 4:
                            pe.wait_ge(job_lo, number(b, "V1") + 1)
                            wait(pe, x_done, b)
                        for i in range(2):
                            h = 2 * arg + i
                            pe.wait_ge(pt_ready, bb * H + (h + 1))
                            hc = slice(h * DH1, (h + 1) * DH1)
                            c = h % HG * DH1
                            mm = products(nc, (ps_o, ps_w)[h // HG][:, c:c + DH1], [
                                (pt[:, h % 4, 0, t, :], pt[:, h % 4, 1, t, :], vh[:, t, hc], vl[:, t, hc])
                                for t in range(NKV)])
                            mm.then_inc(pv_done, 1)
                    elif what == "J":
                        wait(pe, job_lo, number(b, arg) - (0 if isinstance(b, int) or arg == BODY[0] else 1))
                        if arg == "K0":
                            pe.wait_ge(ctx_lo, b + 2)
                        if arg == "OT":
                            pe.wait_ge(o_ready, b * 2)
                        project(arg, bank_of(arg), b + (1 if arg == "Q0" else 0))
                    elif what == "W":
                        pe.wait_ge(job_lo, number(b, "OT") + 1)
                        mm = products(nc, ps_w[0:S, 0:D], [
                            (oth[:, k, :], otl[:, k, :], wo[:, 0, k, :], wo[:, 1, k, :]) for k in range(KD)])
                        mm.then_inc(wo_done, 1)

            walk(pe, "pe", body)

        @block.scalar
        def _(act):
            wait(act, small_in, 32)
            nc.scalar.mul(bias[:], bias_in[:], WS).then_inc(bias_ready, 1)
            wait(act, bias_ready, 1)

            def split_context(b):
                wait(act, ctx_in, 16 * b + 16)
                nc.scalar.activation(ch[:], ctx32[:], ACT.Copy).then_inc(ctx_hi, 1)

            def evacuate(name, bank, number, copies=None):
                wait(act, job_done, number + 1)
                i = int(name[1]) if name != "OT" else 0
                if name[0] == "V":
                    nc.scalar.activation(vh[:, :, i * HD:(i + 1) * HD],
                                         ps_j[0:KV, bank, 0:NKV * HD].rearrange("p (t n) -> p t n", t=NKV), ACT.Copy
                                         ).then_inc(job_hi, 1)
                elif name[0] == "K":
                    nc.scalar.activation(kh[:, i, :], ps_j[:, bank, 0:NC], ACT.Identity, bias=bias[:, 1, i:i + 1]
                                         ).then_inc(job_hi, 1)
                elif name[0] == "Q":
                    if copies is not None:
                        wait(act, qm_ready, copies)
                    nc.scalar.activation(q2[:, i, 0, :], ps_j[:, bank, 0:S], ACT.Identity, bias=bias[:, 0, i:i + 1]
                                         ).then_inc(job_hi, 1)
                else:
                    for k in range(KD):
                        last = nc.scalar.activation(oth[:, k, :], ps_j[:, bank, k * S:(k + 1) * S], ACT.Identity,
                                                    bias=bias[:, 2, k:k + 1])
                    last.then_inc(job_hi, 1)

            split_context(0)
            for n, name in enumerate(FIRST):
                evacuate(name, bank_of(name), n)
            act.wait_ge(pt_zeroed, 1)

            def body(b, steps):
                for what, arg, off in steps:
                    bb = b + off
                    if what == "S":
                        act.wait_ge(max_ready, b * NP + (arg + 1))
                        wait(act, pl_done, b * NP + (arg - 1))
                        for i in range(2):
                            h = 2 * arg + i
                            nc.scalar.activation(p32[:, arg % 2, i, :], s2[:, arg % 2, i, :], ACT.Exp,
                                                 bias=nb[:, arg % 2, i:i + 1], scale=SC,
                                                 accum_out=rsum[:, bass.ds(b * H + h, 1)]).then_inc(exp_done, 1)
                    elif what == "H":
                        act.wait_ge(exp_done, b * H + (2 * arg + 2))
                        wait(act, p_transposed, b * H + 2 * (arg - 3))
                        nc.scalar.activation(ph[:, arg % 4, :, :], p32[:, arg % 2, :, :], ACT.Copy
                                             ).then_inc(ph_done, 1)
                    elif what == "T":
                        for i in range(2):
                            h = 2 * arg + i
                            act.wait_ge(p_transposed, bb * H + (h + 1))
                            wait(act, pv_done, bb * H + (h - 3))
                            nc.scalar.copy(pt[:, h % 4, :, :, 0:S].rearrange("p a t s -> p (a t) s"),
                                           ps_t[0:KV, i, 0:2 * NKV * S].rearrange("p (a s) -> p a s", a=2 * NKV)
                                           ).then_inc(pt_ready, 1)
                    elif what == "C":
                        act.wait_ge(job_done, number(b, "V1") + 1)
                        split_context(b + 1)
                    elif what == "J":
                        evacuate(arg, bank_of(arg), number(b, arg),
                                 b * 2 + (1 if arg == "Q0" else 0) if arg[0] == "Q" else None)

            walk(act, "act", body)

        @block.gpsimd
        def _(pool):
            nc.gpsimd.memset(pt[:], 0.0).then_inc(pt_zeroed, 1)
            nc.gpsimd.memset(own[:], 1.0).then_inc(own_made, 1)
            wait(pool, own_made, 1)
            nc.gpsimd.affine_select(out=own[:], in_=own[:], compare_op=ALU.is_ge, fill=0.0, base=0,
                                    pattern=[[-DH1, HG]], channel_multiplier=1).then_inc(own_made, 1)
            wait(pool, own_made, 2)
            nc.gpsimd.affine_select(out=own[:], in_=own[:], compare_op=ALU.is_ge, fill=0.0, base=DH1 - 1,
                                    pattern=[[DH1, HG]], channel_multiplier=-1).then_inc(own_made, 1)
            wait(pool, own_made, 3)

            def own_rows(g, number):
                wait(pool, job_lo, number + 1)
                nc.gpsimd.tensor_tensor(
                    qm[:, g * HG:(g + 1) * HG, :, :].rearrange("p h a s -> p h (a s)"),
                    q2[:, g, :, :].rearrange("p a s -> p (a s)").unsqueeze(1).to_broadcast([128, HG, 2 * S]),
                    own[:].unsqueeze(2).to_broadcast([128, HG, 2 * S]), ALU.mult).then_inc(qm_ready, 1)

            own_rows(0, FIRST.index("Q0"))
            pool.wait_ge(bo_scaled, 1)
            with pool.Fori(0, B) as b:
                xb = x_res[:, bass.ds(b, 1), :].rearrange("p a d -> p (a d)")
                nc.gpsimd.tensor_tensor(xb, xb, bo_g[:], ALU.add).then_inc(bo_added, 1)

            def body(b, steps):
                for what, arg, off in steps:
                    if what == "S":
                        pool.wait_ge(ph_done, b * NP + (arg + 1))
                        wait(pool, p_transposed, b * H + 2 * (arg - 3))
                        nc.gpsimd.tensor_tensor(pl[:, arg % 4, :, :], p32[:, arg % 2, :, :], ph[:, arg % 4, :, :],
                                                ALU.subtract).then_inc(pl_done, 1)
                    elif arg in ("Q0", "Q1"):
                        wait(pool, scored, b * H + (HG if arg == "Q0" else 0))
                        own_rows(int(arg[1]), number(b, arg))

            walk(pool, "pool", body)

        @block.vector
        def _(dve):
            link = Chain(dve, chain)
            wait(dve, bias_ready, 1)
            nc.vector.tensor_scalar(bo_g[:], bo[:], tanh_g[0:S, 1:2], None, ALU.mult).then_inc(bo_scaled, 1)
            link(nc.vector.tensor_scalar(gate[:], tanh_g[0:S, 1:2], 1.0 / (WS * WS), None, ALU.mult))

            def split_context(b):
                wait(dve, ctx_hi, b + 1)
                nc.vector.tensor_tensor(cl[:], ctx32[:], ch[:], ALU.subtract).then_inc(ctx_lo, 1)

            def low(out, src, b, hi):
                return nc.vector.scalar_tensor_tensor(out=out, in0=src, scalar=b, in1=hi, op0=ALU.add,
                                                      op1=ALU.subtract)

            def evacuate(name, bank, number):
                wait(dve, job_hi, number + 1)
                i = int(name[1]) if name != "OT" else 0
                if name[0] == "V":
                    hc = slice(i * HD, (i + 1) * HD)
                    last = nc.vector.tensor_tensor(
                        vl[:, :, hc], ps_j[0:KV, bank, 0:NKV * HD].rearrange("p (t n) -> p t n", t=NKV),
                        vh[:, :, hc], ALU.subtract)
                elif name[0] == "K":
                    last = low(kl[:, i, :], ps_j[:, bank, 0:NC], bias[:, 1, i:i + 1], kh[:, i, :])
                elif name[0] == "Q":
                    last = low(q2[:, i, 1, :], ps_j[:, bank, 0:S], bias[:, 0, i:i + 1], q2[:, i, 0, :])
                else:
                    for k in range(KD):
                        last = low(otl[:, k, :], ps_j[:, bank, k * S:(k + 1) * S], bias[:, 2, k:k + 1], oth[:, k, :])
                last.then_inc(job_lo, 1)

            split_context(0)
            for n, name in enumerate(FIRST):
                evacuate(name, bank_of(name), n)
            dve.wait_ge(bo_added, B)
            wait(dve, mask_in, 16)
            n0 = link.n

            per = 2 * NP + 2

            def body(b, steps):
                c = 0

                def chained(instruction):
                    nonlocal c
                    c += 1
                    instruction.then_inc(chain, 1)
                    dve.wait_ge(chain, b * per + (n0 + c - (0 if isinstance(b, int) and b == 0 else 1)))

                for what, arg, off in steps:
                    bb = b + off
                    if what == "S":
                        dve.wait_ge(scored, b * H + (2 * arg + 2))
                        mb = maskt[:, bass.ds(b, 1), :].to_broadcast([S, 2, NC])
                        ins = nc.vector.tensor_tensor(s1[:], ps_s[0:S, :, 0:NC], mb, ALU.mult)
                        ins.then_inc(masked, 1)
                        dve.wait_ge(masked, b * NP + (arg + 1))
                        chained(nc.vector.tensor_scalar(fill[:], s1[:], 0.0, FILL, ALU.is_equal, ALU.mult))
                        wait(dve, exp_done, b * H + 2 * (arg - 1))
                        nc.vector.memset(pad[:], 0.0)
                        for i in range(2):
                            ins = nc.vector.tensor_tensor_reduce(
                                out=s2[:, arg % 2, i, :], in0=s1[:, i, :], in1=fill[:, i, :], scale=1.0,
                                scalar=-3.0e38, op0=ALU.add, op1=ALU.max, accum_out=mx[:, arg % 2, i:i + 1])
                        chained(ins)
                        nc.vector.tensor_scalar(nb[:, arg % 2, :], mx[:, arg % 2, :], -SC, None, ALU.mult
                                                ).then_inc(max_ready, 1)
                    elif what == "C":
                        split_context(b + 1)
                    elif what == "O":
                        hh = slice(arg * HG, (arg + 1) * HG)
                        dve.wait_ge(exp_done, bb * H + HG * (arg + 1))
                        chained(nc.vector.reciprocal(rinv[:, hh], rsum[:, bass.ds(bb * H + arg * HG, HG)]))
                        dve.wait_ge(pv_done, bb * H + HG * (arg + 1))
                        nc.vector.tensor_tensor(
                            on[:, arg * HD:(arg + 1) * HD].rearrange("p (h d) -> p h d", h=HG),
                            (ps_o, ps_w)[arg][0:S, 0:HD].rearrange("p (h d) -> p h d", h=HG),
                            rinv[:, hh].unsqueeze(2).to_broadcast([S, HG, DH1]), ALU.mult).then_inc(o_ready, 1)
                    elif what == "J":
                        evacuate(arg, bank_of(arg), number(b, arg))
                    elif what == "W":
                        xb = x_res[:, bass.ds(bb, 1), :].rearrange("p a d -> p (a d)")
                        dve.wait_ge(wo_done, b)
                        nc.vector.scalar_tensor_tensor(out=xb, in0=ps_w[0:S, 0:D], scalar=gate[:], in1=xb,
                                                       op0=ALU.mult, op1=ALU.add).then_inc(x_done, 1)

            walk(dve, "dve", body)


def load_chunk(sp, A, stage, arrived, e, q):
    c, dst = q * CH, stage[:, q % LB, :]
    if c < W1N:
        k, c = c // FF1, c % FF1
        src = A["w1"][bass.ds(e, 1), k * 128:(k + 1) * 128, c:c + CH].rearrange("e p n -> p (e n)")
    else:
        r = (c - W1N) // D * 128
        src = A["w2"][bass.ds(e, 1), r:r + (CH // D) * 128, :].rearrange("e (k p) n -> p (e k) n", p=128)
        dst = dst.rearrange("p (k n) -> p k n", n=D)
    sp.dma_start(dst, src).then_inc(arrived[q % LB], 16)


def router_phase(nc, A, xh, xl, rw, own_gate, slot_idx, tile_expert, tile_hot, wT, b2, xg, stage, arrived, ident32,
                 tanh_g):
    with ExitStack() as ctx:
        sb, ps, sem = make_allocators(nc, ctx)
        b2_32 = sb("r_b2", [E + 1, D])
        zeros = sb("r_zeros", [128, D])
        ex, prob = sb("r_ex", [S, B, E]), sb("r_prob", [S, B, E])
        top = sb("r_top", [S, B, 8])
        idx = sb("r_idx", [S, B, 8], U32)
        idxf = sb("r_idxf", [S, B, 2])
        num_e, num_t = sb("r_num_e", [128, E]), sb("r_num_t", [128, MAXT])
        den, rden = sb("r_den", [S, B]), sb("r_rden", [S, B])
        hot = sb("r_hot", [S, 2, B, E])
        both = sb("r_both", [S, B, E], F16)
        share = sb("r_share", [S, 2, B])
        wts, tmp = sb("r_wts", [S, B, E]), sb("r_tmp", [S, B, E])
        before = sb("r_before", [S, 128], F16)
        ones = sb("r_ones", [S, 128], F16)
        sums = sb("r_sums", [128, 2, B, E])
        count = sb("r_count", [128, B, E])
        tiles = sb("r_tiles", [128, E])
        ends = sb("r_ends", [128, 2, E])
        base = sb("r_base", [128, E])
        slot = sb("r_slot", [S, B, E])
        pos = sb("r_pos", [S, 2, B])
        reach = sb("r_reach", [128, MAXT, E - 1])
        tile_ex = sb("r_tile_ex", [128, MAXT])
        pr = ps("r_pr", [128, 512])
        pc = ps("r_pc", [128, 2, 512])
        pT = ps("r_pT", [128, 4, 512])
        names = ("b2_in", "logits", "exp_done", "chain", "consts", "both_ready", "ranked", "wts_ready",
                 "ones_set", "transposed", "wT_hi", "b2_hi", "z_set", "cleared")
        (b2_in, logits, exp_done, chain, consts, both_ready, ranked, wts_ready, ones_set, transposed,
         wT_hi, b2_hi, z_set, cleared) = (sem(f"r_{n}") for n in names)
        block = ctx.enter_context(nc.Block())

        @block.sync
        def _(sp):
            sp.dma_start(b2_32[:], A["b2"]).then_inc(b2_in, 16)
            for q in range(LB):
                load_chunk(sp, A, stage, arrived, E, q)
            sp.wait_ge(z_set, 1)
            sp.dma_start(xg.rearrange("(p r) d -> p r d", p=128),
                         zeros[:].unsqueeze(1).to_broadcast([128, MAXT, D])).then_inc(cleared, 16)
            sp.wait_ge(cleared, 16)

        @block.gpsimd
        def _(pool):
            nc.gpsimd.memset(before[:], 1.0).then_inc(ones_set, 1)
            nc.gpsimd.memset(ones[:], 1.0)
            pool.wait_ge(ones_set, 1)
            nc.gpsimd.affine_select(out=before[:], in_=before[:], compare_op=ALU.is_gt, fill=0.0, base=0,
                                    pattern=[[1, 128]], channel_multiplier=-1)
            nc.gpsimd.iota(num_e[:], pattern=[[1, E]], base=0, channel_multiplier=0,
                           allow_small_or_imprecise_dtypes=True)
            nc.gpsimd.iota(num_t[:], pattern=[[1, MAXT]], base=0, channel_multiplier=0,
                           allow_small_or_imprecise_dtypes=True)
            nc.gpsimd.memset(wT[:, 1], 0.0)
            nc.gpsimd.memset(wT[:, 0], 1.0).then_inc(consts, 1)
            nc.gpsimd.memset(zeros[:], 0.0).then_inc(z_set, 1)

        @block.tensor
        def _(pe):
            for t in range(B):
                tt = slice(t * S, (t + 1) * S)
                mm = products(nc, pr[0:S, t * E:(t + 1) * E], [
                    (xh[:, k, tt], xl[:, k, tt], rw[:, 0, k, :], rw[:, 1, k, :]) for k in range(KD)])
            mm.then_inc(logits, 1)
            pe.wait_ge(consts, 1)
            pe.wait_ge(both_ready, 1)
            for i, m in enumerate((before, ones)):
                mm = nc.tensor.matmul(pc[:, i, 0:B * E], m[:], both[:].rearrange("p t e -> p (t e)"),
                                      start=True, stop=True)
            mm.then_inc(ranked, 1)
            pe.wait_ge(wts_ready, 1)
            for t in range(B):
                mm = nc.tensor.transpose(pT[0:E, t // 4, (t % 4) * S:(t % 4 + 1) * S], wts[:, t, :],
                                         ident32[0:S, 0:S])
            mm.then_inc(transposed, 1)

        @block.scalar
        def _(act):
            act.wait_ge(logits, 1)
            nc.scalar.activation(ex[:], pr[0:S, 0:B * E].rearrange("p (t e) -> p t e", t=B), ACT.Exp,
                                 scale=-1.0 / WS).then_inc(exp_done, 1)
            act.wait_ge(b2_in, 16)
            nc.scalar.activation(b2[:, 0], b2_32[:], ACT.Copy, scale=WS).then_inc(b2_hi, 1)
            act.wait_ge(consts, 1)
            act.wait_ge(transposed, 1)
            nc.scalar.activation(wT[0:E, 0].rearrange("p (g t) s -> p g (t s)", g=4), pT[0:E, :, 0:4 * S],
                                 ACT.Copy).then_inc(wT_hi, 1)

        @block.vector
        def _(dve):
            link = Chain(dve, chain)
            dve.wait_ge(exp_done, 1)
            link(nc.vector.tensor_scalar(ex[:], ex[:], 1.0, None, ALU.add))
            link(nc.vector.reciprocal(prob[:], ex[:]))
            for t in range(B):
                last = nc.vector.max(top[:, t, :], prob[:, t, :])
            link(last)
            for t in range(B):
                last = nc.vector.max_index(idx[:, t, :], top[:, t, :], prob[:, t, :])
            link(last)
            link(nc.vector.tensor_copy(idxf[:], idx[:, :, 0:2]))
            dve.wait_ge(consts, 1)
            for i in range(2):
                link(nc.vector.tensor_tensor(hot[:, i], num_e[0:S].unsqueeze(1).to_broadcast([S, B, E]),
                                             idxf[:, :, i:i + 1].to_broadcast([S, B, E]), ALU.is_equal))
            nc.vector.tensor_tensor(both[:], hot[:, 0], hot[:, 1], ALU.add).then_inc(both_ready, 1)
            link(nc.vector.tensor_tensor(den[:], top[:, :, 0], top[:, :, 1], ALU.add))
            link(nc.vector.tensor_scalar(den[:], den[:], 1e-6, None, ALU.add))
            link(nc.vector.reciprocal(rden[:], den[:]))
            for i in range(2):
                link(nc.vector.tensor_tensor(share[:, i], top[:, :, i], rden[:], ALU.mult))
                link(nc.vector.tensor_scalar(own_gate[:, i], share[:, i], tanh_g[0:S, 3:4], 1.0 / WS, ALU.mult,
                                             ALU.mult))
                link(nc.vector.tensor_tensor((wts, tmp)[i][:], hot[:, i],
                                             share[:, i].unsqueeze(2).to_broadcast([S, B, E]), ALU.mult))
            nc.vector.tensor_tensor(wts[:], wts[:], tmp[:], ALU.add).then_inc(wts_ready, 1)
            dve.wait_ge(ranked, 1)
            link(nc.vector.tensor_copy(count[:], pc[:, 1, 0:B * E].rearrange("p (t e) -> p t e", t=B)))
            src, turn = count[:], 0
            for step in (1, 2, 4, 8):
                dst = sums[:, turn]
                nc.vector.tensor_copy(dst[:, 0:step], src[:, 0:step])
                link(nc.vector.tensor_tensor(dst[:, step:], src[:, step:], src[:, 0:B - step], ALU.add))
                src, turn = dst, 1 - turn
            link(nc.vector.tensor_scalar(tiles[:], src[:, B - 1], 63.5, 1.0 / 128.0, ALU.add, ALU.mult))
            link(nc.vector.tensor_scalar(tiles[:], tiles[:], MAGIC, None, ALU.add))
            link(nc.vector.tensor_scalar(tiles[:], tiles[:], -MAGIC, None, ALU.add))
            run, turn = tiles[:], 0
            for step in (1, 2, 4):
                dst = ends[:, turn]
                nc.vector.tensor_copy(dst[:, 0:step], run[:, 0:step])
                link(nc.vector.tensor_tensor(dst[:, step:], run[:, step:], run[:, 0:E - step], ALU.add))
                run, turn = dst, 1 - turn
            link(nc.vector.tensor_tensor(base[:], run, tiles[:], ALU.subtract))
            link(nc.vector.tensor_scalar(base[:], base[:], 128.0, None, ALU.mult))
            link(nc.vector.tensor_tensor(slot[:], src[0:S], count[0:S], ALU.subtract))
            link(nc.vector.tensor_tensor(slot[:], pc[0:S, 0, 0:B * E].rearrange("p (t e) -> p t e", t=B), slot[:],
                                         ALU.add))
            link(nc.vector.tensor_tensor(slot[:], slot[:], base[0:S].unsqueeze(1).to_broadcast([S, B, E]), ALU.add))
            for i in range(2):
                link(nc.vector.tensor_tensor(tmp[:], hot[:, i], slot[:], ALU.mult))
                link(nc.vector.tensor_reduce(pos[:, i], tmp[:], AX.X, ALU.add))
            nc.vector.tensor_copy(slot_idx[:], pos[:])
            link(nc.vector.tensor_tensor(reach[:], num_t[:].unsqueeze(2).to_broadcast([128, MAXT, E - 1]),
                                         run[:, 0:E - 1].unsqueeze(1).to_broadcast([128, MAXT, E - 1]), ALU.is_ge))
            link(nc.vector.tensor_reduce(tile_ex[:], reach[:], AX.X, ALU.add))
            nc.vector.tensor_copy(tile_expert[:], tile_ex[0:1, :])
            nc.vector.tensor_tensor(tile_hot[:], num_e[:].unsqueeze(1).to_broadcast([128, MAXT, E]),
                                    tile_ex[:].unsqueeze(2).to_broadcast([128, MAXT, E]), ALU.is_equal)
            dve.wait_ge(b2_hi, 1)
            nc.vector.scalar_tensor_tensor(out=b2[:, 1], in0=b2_32[:], scalar=WS, in1=b2[:, 0], op0=ALU.mult,
                                           op1=ALU.subtract)
            dve.wait_ge(wT_hi, 1)
            nc.vector.tensor_tensor(wT[0:E, 1].rearrange("p (g t) s -> p g (t s)", g=4), pT[0:E, :, 0:4 * S],
                                    wT[0:E, 0].rearrange("p (g t) s -> p g (t s)", g=4), ALU.subtract)


def shared_expert_phase(nc, A, x_res, xh, xl, norm, wh, wl, wT, b2, slot_idx, tile_hot, tile_b1, xg, stage, arrived,
                        tanh_g):
    LAG, RING = 3, 4
    PER = NCH // 4
    with ExitStack() as ctx:
        sb, ps, sem = make_allocators(nc, ctx)
        b1 = sb("s_b1", [128, E + 1, HC1])
        bsel = sb("s_bsel", [128, MAXT, E])
        gate = sb("s_gate", [S, 1])
        h32 = sb("s_h32", [128, 2, GW])
        hh, hl = sb("s_hh", [128, RING, GW], F16), sb("s_hl", [128, RING, GW], F16)
        p1 = ps("s_p1", [128, 4, 512])
        p2 = ps("s_p2", [128, TG, 512])
        names = ("b1_in", "w_hi", "w_lo", "up_done", "relu_done", "h_hi", "h_lo", "down_done", "bias_chain",
                 "added", "gate_made", "scattered")
        (b1_in, w_hi, w_lo, up_done, relu_done, h_hi, h_lo, down_done, bias_chain, added, gate_made,
         scattered) = (sem(f"s_{n}") for n in names)
        block = ctx.enter_context(nc.Block())

        def place(w, e, q):
            return w[:].rearrange("p e n -> p (e n)")[:, bass.ds(e * WN + q * CH, CH)]

        @block.sync
        def _(sp):
            sp.dma_start(b1[:], A["b1T"]).then_inc(b1_in, 16)
            for q in range(LB, NCH):
                wait(sp, w_lo, q - (LB - 1))
                load_chunk(sp, A, stage, arrived, E, q)
            with sp.Fori(0, E) as e:
                for q in range(NCH):
                    sp.wait_ge(w_lo, e * NCH + (NCH + q - (LB - 1)))
                    load_chunk(sp, A, stage, arrived, e, q)

        @block.gpsimd
        def _(pool):
            for t in range(B):
                for i in range(2):
                    nc.gpsimd.indirect_dma_start(xg, bass.IndirectOffsetOnAxis(slot_idx[:, i, t:t + 1], 0),
                                                 norm[:, t, :], None).then_inc(scattered, 16)
            pool.wait_ge(scattered, 2 * B * 16)

        @block.scalar
        def _(act):
            def split(e, slot, q):
                act.wait_ge(arrived[q % LB], (e + 1) * (16 * NCH // LB) + 16 * (q // LB + 1))
                nc.scalar.activation(place(wh, slot, q), stage[:, q % LB, :], ACT.Copy, scale=WS).then_inc(w_hi, 1)

            for q in range(NCH):
                split(-1, E - 1, q)
            act.wait_ge(b1_in, 16)

            def group(g, weights):
                for j in range(HC1):
                    n = g * HC1 + j
                    act.wait_ge(up_done, n + 1)
                    wait(act, h_lo, n - 1)
                    nc.scalar.activation(h32[:, j % 2, :], p1[:, j % 4, 0:GW], ACT.Relu, bias=b1[:, E, j:j + 1],
                                         scale=1.0 / WS).then_inc(relu_done, 1)
                    act.wait_ge(relu_done, n + 1)
                    wait(act, down_done, n - (RING - 1))
                    nc.scalar.activation(hh[:, j % RING, :], h32[:, j % 2, :], ACT.Copy).then_inc(h_hi, 1)
                    if j // 4 < weights:
                        for q in range(j % 4 * PER, (j % 4 + 1) * PER):
                            split(g * 2 + j // 4, g * 2 + j // 4, q)

            group(0, 2)
            with act.Fori(1, NG - 1) as g:
                group(g, 2)
            group(NG - 1, 1)
            act.wait_ge(down_done, NG * HC1)
            for q in range(NCH):
                split(E - 1, E - 1, q)

        @block.vector
        def _(dve):
            def split(e, slot, q):
                dve.wait_ge(w_hi, e * NCH + (NCH + q + 1))
                nc.vector.scalar_tensor_tensor(out=place(wl, slot, q), in0=stage[:, q % LB, :], scalar=WS,
                                               in1=place(wh, slot, q), op0=ALU.mult, op1=ALU.subtract
                                               ).then_inc(w_lo, 1)

            nc.vector.tensor_scalar(gate[:], tanh_g[0:S, 3:4], 1.0 / WS, None, ALU.mult).then_inc(gate_made, 1)
            for q in range(NCH):
                split(-1, E - 1, q)
            dve.wait_ge(gate_made, 1)

            link = Chain(dve, bias_chain)

            def choose_bias(j):
                link(nc.vector.scalar_tensor_tensor(out=bsel[:], in0=tile_hot[:], scalar=WS,
                                                    in1=b1[:, 0:E, j].unsqueeze(1).to_broadcast([128, MAXT, E]),
                                                    op0=ALU.mult, op1=ALU.mult))
                link(nc.vector.tensor_reduce(tile_b1[:, :, j], bsel[:], AX.X, ALU.add))

            def add(g):
                dve.wait_ge(down_done, g * HC1 + HC1)
                for i in range(TG):
                    xt = x_res[:, bass.ds(g * TG + i, 1), :].rearrange("p a d -> p (a d)")
                    nc.vector.scalar_tensor_tensor(out=xt, in0=p2[0:S, i, 0:D], scalar=gate[:], in1=xt,
                                                   op0=ALU.mult, op1=ALU.add).then_inc(added, 1)

            def group(g, weights, first=False):
                for j in range(HC1):
                    dve.wait_ge(h_hi, g * HC1 + (j + 1))
                    nc.vector.tensor_tensor(hl[:, j % RING, :], h32[:, j % 2, :], hh[:, j % RING, :], ALU.subtract
                                            ).then_inc(h_lo, 1)
                    if j == LAG - 1 and not first:
                        add(g - 1)
                    if j // 4 < weights:
                        for q in range(j % 4 * PER, (j % 4 + 1) * PER):
                            split(g * 2 + j // 4, g * 2 + j // 4, q)
                    if first:
                        choose_bias(j)

            dve.wait_ge(b1_in, 16)
            group(0, 2, first=True)
            with dve.Fori(1, NG - 1) as g:
                group(g, 2)
            group(NG - 1, 1)
            add(NG - 1)
            for q in range(NCH):
                split(E - 1, E - 1, q)

        @block.tensor
        def _(pe):
            w1h, w1l = (w[:, E - 1, 0:W1N].rearrange("p (k n) -> p k n", k=KD) for w in (wh, wl))
            w2h, w2l = (w[:, E - 1, W1N:].rearrange("p (k n) -> p k n", k=HC1) for w in (wh, wl))
            pe.wait_ge(w_lo, W1N // CH)

            def second(g, j):
                if j == 0:
                    wait(pe, added, g * TG)
                    for i in range(TG):
                        wt = [wT[:, part, bass.ds(g * TG + i, 1), :].rearrange("p a s -> p (a s)") for part in (0, 1)]
                        for part, (a, b) in enumerate(((0, 0), (0, 1), (1, 0))):
                            nc.tensor.matmul(p2[0:S, i, 0:D], wt[a], b2[:, b], start=(part == 0), stop=False)
                pe.wait_ge(h_lo, g * HC1 + (j + 1))
                for i in range(TG):
                    ii, r = slice(i * S, (i + 1) * S), j % RING
                    for part, (a, b) in enumerate(((hh, w2h), (hh, w2l), (hl, w2h))):
                        mm = nc.tensor.matmul(p2[0:S, i, 0:D], a[:, r, ii], b[:, j, :], start=False,
                                              stop=(j == HC1 - 1 and part == 2))
                mm.then_inc(down_done, 1)

            def group(g, first=False):
                for j in range(HC1):
                    wait(pe, relu_done, g * HC1 + (j - 3))
                    jj = slice(j * 128, (j + 1) * 128)
                    products(nc, p1[:, j % 4, 0:GW], [
                        (w1h[:, k, jj], w1l[:, k, jj], xh[:, k, bass.ds(g * GW, GW)], xl[:, k, bass.ds(g * GW, GW)])
                        for k in range(KD)]).then_inc(up_done, 1)
                    if j == LAG and first:
                        pe.wait_ge(w_lo, NCH)
                    if j >= LAG:
                        second(g, j - LAG)
                    elif not first:
                        second(g - 1, j + HC1 - LAG)

            group(0, first=True)
            with pe.Fori(1, NG) as g:
                group(g)
            for j in range(HC1 - LAG, HC1):
                second(NG - 1, j)


def routed_experts_phase(nc, x_res, wh, wl, own_gate, slot_idx, tile_expert, tile_b1, xg, yg, out, ident32):
    RT = 4
    with ExitStack() as ctx:
        sb, ps, sem = make_allocators(nc, ctx)
        xt32 = sb("e_xt32", [128, 2, D])
        xth, xtl = sb("e_xth", [128, 2, D], F16), sb("e_xtl", [128, 2, D], F16)
        hb, h32 = sb("e_hb", [128, 2, 512]), sb("e_h32", [128, 2, 512])
        hh, hl = sb("e_hh", [128, 2, FF1], F16), sb("e_hl", [128, 2, FF1], F16)
        y = sb("e_y", [128, 2, D])
        yt = sb("e_yt", [S, RT, 2, D])
        px = ps("e_px", [128, 512])
        p1 = ps("e_p1", [128, 4, 512])
        p2 = ps("e_p2", [128, 2, 512])
        names = ("xt_in0", "xt_in1", "x_transposed", "x_hi", "x_lo", "up_done", "biased", "relu_done", "h_hi", "h_lo",
                 "down_done", "y_ready", "y_out0", "y_out1", "added1", "added", "stored")
        (xt_in0, xt_in1, x_transposed, x_hi, x_lo, up_done, biased, relu_done, h_hi, h_lo, down_done, y_ready,
         y_out0, y_out1, added1, added, stored) = (sem(f"e_{n}") for n in names)
        xt_in = (xt_in0, xt_in1)
        got = [sem(f"e_got{i}") for i in range(RT)]
        y_outs = (y_out0, y_out1)
        block = ctx.enter_context(nc.Block())

        def walk(eng, body):
            for i in range(3):
                body(i, i % 2)
            with eng.Fori(0, (MAXT - 5) // 2) as r:
                for par in (1, 0):
                    body(r * 2 + (4 - par), par)
            for i in range(3 + (MAXT - 5) // 2 * 2, MAXT + 1):
                body(i, i % 2)

        def given(i, low, high):
            return not isinstance(i, int) or low <= i <= high

        @block.sync
        def _(sp):
            def load(i, par):
                wait(sp, x_transposed, i - 1)
                sp.dma_start(xt32[:, par, :], xg[bass.ds(i * 128, 128), :]).then_inc(xt_in[par], 16)

            load(0, 0)

            def body(i, par):
                if given(i, 0, MAXT - 2):
                    load(i + 1, 1 - par)

            walk(sp, body)
            for t in range(B):
                sp.wait_ge(added, t + 1)
                sp.dma_start(out[t], x_res[:, t, :]).then_inc(stored, 16)
            sp.wait_ge(stored, B * 16)

        @block.tensor
        def _(pe):
            wfh, wfl = (w[:].rearrange("p e n -> p (e n)") for w in (wh, wl))

            def transpose(i, par):
                pe.wait_ge(xt_in[par], 8 * (i - par) + 16)
                wait(pe, x_lo, i)
                for k in range(KD):
                    mm = nc.tensor.transpose(px[:, k * 128:(k + 1) * 128], xt32[:, par, k * 128:(k + 1) * 128],
                                             ident32[:])
                mm.then_inc(x_transposed, 1)

            transpose(0, 0)

            def body(i, par):
                if given(i, 0, MAXT - 2):
                    transpose(i + 1, 1 - par)
                if given(i, 0, MAXT - 1):
                    first = pe.snap(pe.value_load(tile_expert[0:1, bass.ds(i, 1)], min_val=0, max_val=E - 1) * WN)
                    pe.wait_ge(x_lo, i + 1)
                    for j in range(HC1):
                        if j % 4 == 0:
                            wait(pe, biased, 2 * (i - 1) + (j // 4 - 1))
                        at = [first + (k * FF1 + j * 128) for k in range(KD)]
                        mm = products(nc, p1[:, 2 * par + j // 4, (j % 4) * 128:(j % 4 + 1) * 128], [
                            (wfh[:, bass.ds(at[k], 128)], wfl[:, bass.ds(at[k], 128)],
                             xth[:, par, k * 128:(k + 1) * 128], xtl[:, par, k * 128:(k + 1) * 128])
                            for k in range(KD)])
                        if j % 4 == 3:
                            mm.then_inc(up_done, 1)
                if given(i, 1, MAXT):
                    first = pe.snap(pe.value_load(tile_expert[0:1, bass.ds(i - 1, 1)], min_val=0, max_val=E - 1) * WN)
                    wait(pe, y_ready, i - 2)
                    pe.wait_ge(h_lo, 2 * i)
                    q = 1 - par
                    products(nc, p2[:, q, 0:D], [
                        (hh[:, q, j * 128:(j + 1) * 128], hl[:, q, j * 128:(j + 1) * 128],
                         wfh[:, bass.ds(first + (W1N + j * D), D)], wfl[:, bass.ds(first + (W1N + j * D), D)])
                        for j in range(HC1)]).then_inc(down_done, 1)

            walk(pe, body)

        @block.scalar
        def _(act):
            def split_x(i, par):
                act.wait_ge(x_transposed, i + 1)
                wait(act, up_done, 2 * (i - 1))
                nc.scalar.activation(xth[:, par, :], px[:, 0:D], ACT.Copy).then_inc(x_hi, 1)

            split_x(0, 0)

            def body(i, par):
                if given(i, 0, MAXT - 2):
                    split_x(i + 1, 1 - par)
                if given(i, 0, MAXT - 1):
                    for c in range(2):
                        n = i * 2 + c
                        act.wait_ge(biased, n + 1)
                        wait(act, h_lo, n - 1)
                        nc.scalar.activation(h32[:, c, :], hb[:, c, :], ACT.Relu, scale=1.0 / WS
                                             ).then_inc(relu_done, 1)
                        act.wait_ge(relu_done, n + 1)
                        wait(act, down_done, i - 1)
                        nc.scalar.activation(hh[:, par, c * 512:(c + 1) * 512], h32[:, c, :], ACT.Copy
                                             ).then_inc(h_hi, 1)

            walk(act, body)

        @block.vector
        def _(dve):
            def split_x(i, par):
                dve.wait_ge(x_hi, i + 1)
                nc.vector.tensor_tensor(xtl[:, par, :], px[:, 0:D], xth[:, par, :], ALU.subtract).then_inc(x_lo, 1)

            split_x(0, 0)

            def body(i, par):
                if given(i, 0, MAXT - 2):
                    split_x(i + 1, 1 - par)
                if given(i, 0, MAXT - 1):
                    for c in range(2):
                        n = i * 2 + c
                        dve.wait_ge(up_done, n + 1)
                        wait(dve, relu_done, n - 1)
                        nc.vector.tensor_tensor(
                            hb[:, c, :].rearrange("p (j s) -> p j s", j=4),
                            p1[:, 2 * par + c, :].rearrange("p (j s) -> p j s", j=4),
                            tile_b1[:, bass.ds(i, 1), 4 * c:4 * c + 4].rearrange("p a j -> p (a j)")
                            .unsqueeze(2).to_broadcast([128, 4, 128]), ALU.add).then_inc(biased, 1)
                if given(i, 1, MAXT):
                    dve.wait_ge(down_done, i)
                    q = 1 - par
                    if given(i, 3, MAXT):
                        dve.wait_ge(y_outs[q], 8 * (i - 1 - q))
                    nc.vector.tensor_copy(y[:, q, :], p2[:, q, 0:D]).then_inc(y_ready, 1)
                if given(i, 0, MAXT - 1):
                    for c in range(2):
                        n = i * 2 + c
                        dve.wait_ge(h_hi, n + 1)
                        nc.vector.tensor_tensor(hl[:, par, c * 512:(c + 1) * 512], h32[:, c, :],
                                                hh[:, par, c * 512:(c + 1) * 512], ALU.subtract).then_inc(h_lo, 1)

            walk(dve, body)
            for t in range(B):
                dve.wait_ge(got[t % RT], 32 * (t // RT + 1))
                for i in range(2):
                    ins = nc.vector.scalar_tensor_tensor(out=x_res[:, t, :], in0=yt[:, t % RT, i, :],
                                                         scalar=own_gate[:, i, t:t + 1], in1=x_res[:, t, :],
                                                         op0=ALU.mult, op1=ALU.add)
                    if i == 0:
                        ins.then_inc(added1, 1)
                        dve.wait_ge(added1, t + 1)
                ins.then_inc(added, 1)

        @block.gpsimd
        def _(pool):
            def body(i, par):
                if given(i, 1, MAXT):
                    pool.wait_ge(y_ready, i)
                    nc.gpsimd.dma_start(yg[bass.ds((i - 1) * 128, 128), :], y[:, 1 - par, :]
                                        ).then_inc(y_outs[1 - par], 16)

            walk(pool, body)
            pool.wait_ge(y_outs[0], 16 * ((MAXT + 1) // 2))
            pool.wait_ge(y_outs[1], 16 * (MAXT // 2))
            for t in range(B):
                wait(pool, added, t - (RT - 1))
                for i in range(2):
                    nc.gpsimd.indirect_dma_start(yt[:, t % RT, i, :], None, yg,
                                                 bass.IndirectOffsetOnAxis(slot_idx[:, i, t:t + 1], 0)
                                                 ).then_inc(got[t % RT], 16)


def moe_phase(nc, A, x_res, xh, xl, ident32, tanh_g, xg, yg, out):
    with ExitStack() as ctx:
        sb, ps, sem = make_allocators(nc, ctx)
        own_gate = sb("own_gate", [S, 2, B])
        slot_idx = sb("slot_idx", [S, 2, B], U32)
        tile_expert = sb("tile_expert", [1, MAXT], I32)
        tile_b1 = sb("tile_b1", [128, MAXT, HC1])
        wT, b2 = sb("wT", [E + 1, 2, B, S], F16), sb("b2", [E + 1, 2, D], F16)
        wh, wl = sb("wh", [128, E, WN], F16), sb("wl", [128, E, WN], F16)
        with ExitStack() as c2:
            norm = c2.enter_context(nc.sbuf_tensor("norm", [S, B, D], F32))
            tile_hot = c2.enter_context(nc.sbuf_tensor("tile_hot", [128, MAXT, E], F32))
            stage = c2.enter_context(nc.sbuf_tensor("w_stage", [128, LB, CH], F32))
            arrived = [c2.enter_context(nc.semaphore(f"w_in{i}")) for i in range(LB)]
            with ExitStack() as c3:
                rms_w = c3.enter_context(nc.sbuf_tensor("rms_w", [S, D], F32))
                rw = c3.enter_context(nc.sbuf_tensor("router_w", [128, 2, KD, E], F16))
                norm_phase(nc, "n3", x_res, ident32, xh, xl, n_out=norm, rms_w=(A["L1_ffn_norm_weight"], rms_w),
                           weights=([(A["router_wT"], flat(rw[:, 0]), flat(rw[:, 1]))], KD * E))
                router_phase(nc, A, xh, xl, rw, own_gate, slot_idx, tile_expert, tile_hot, wT, b2, xg, stage, arrived,
                             ident32, tanh_g)
            shared_expert_phase(nc, A, x_res, xh, xl, norm, wh, wl, wT, b2, slot_idx, tile_hot, tile_b1, xg, stage,
                                arrived, tanh_g)
        routed_experts_phase(nc, x_res, wh, wl, own_gate, slot_idx, tile_expert, tile_b1, xg, yg, out, ident32)


def program(nc, A, out):
    with ExitStack() as ctx:
        sb, ps, sem = make_allocators(nc, ctx)
        x_res = sb("x_res", [S, B, D])
        ident32, ident16 = sb("ident32", [128, 128]), sb("ident16", [128, 128], F16)
        gates, tanh_g = sb("gates", [128, 4]), sb("tanh_g", [128, 4])
        xh, xl = sb("xh", [128, KD, T], F16), sb("xl", [128, KD, T], F16)
        xg = nc.dram_tensor("slots_in", (MAXT * 128, D), F32, kind="Internal").ap()
        yg = nc.dram_tensor("slots_out", (MAXT * 128, D), F32, kind="Internal").ap()
        x_in, g_in = sem("x_in"), sem("g_in")
        setup_phase(nc, A, x_res, ident32, ident16, gates, x_in, g_in)
        attention0_phase(nc, A, x_res, xh, xl, ident32, ident16, tanh_g, (x_in, g_in, gates, tanh_g))
        feed_forward0_phase(nc, A, x_res, xh, xl, ident32, tanh_g)
        attention1_phase(nc, A, x_res, xh, xl, ident32, ident16, tanh_g)
        clear_semaphores(nc)
        moe_phase(nc, A, x_res, xh, xl, ident32, tanh_g, xg, yg, out)


def lay_out(inputs, np):
    g = {k: np.ascontiguousarray(v) for k, v in inputs.items()}
    a = {
        "x": g["x"].reshape(T, D),
        "ctxT": g["ctx_1024"].reshape(B * NC, D).T.reshape(KD, 128, B * NC),
        "g_xattn": g["g_xattn"],
        "g_ffn": g["g_ffn"],
    }
    a["mask"] = g["mask_Bx1xSxS2_ff1"].reshape(B, S, NC)
    a["L1_qkv_bT"] = np.stack([g[f"L1_xattn_{n}_b"] for n in ("wq", "wk", "wv")]).reshape(3, KD, 128).transpose(2, 0, 1)
    a["w1"] = np.concatenate([g["L1_ffn_ew1"], g["L1_ffn_sw1"][None]])
    a["w2"] = np.concatenate([g["L1_ffn_ew2"], g["L1_ffn_sw2"][None]])
    a["b1T"] = np.concatenate([g["L1_ffn_eb1"], g["L1_ffn_sb1"][None]]).reshape(E + 1, HC1, 128).transpose(2, 0, 1)
    a["b2"] = np.concatenate([g["L1_ffn_eb2"], g["L1_ffn_sb2"][None]])
    a["router_wT"] = g["L1_ffn_router_w"].T.reshape(KD, 128, E).transpose(1, 0, 2)
    for n in ("L0_xattn_Wq", "L0_xattn_Wk", "L0_xattn_Wv", "L0_xattn_Wo", "L0_xattn_bo", "L0_ffn_w_gate",
              "L0_ffn_w_up", "L0_ffn_w_down", "L1_xattn_wq_w", "L1_xattn_wk_w", "L1_xattn_wv_w", "L1_xattn_wo_w",
              "L1_xattn_wo_b", "L1_ffn_norm_weight"):
        a[n] = g[n]
    return {k: np.ascontiguousarray(v) for k, v in a.items()}


def kernel(**inputs):
    import numpy as _np
    import concourse.bacc as _bacc
    from concourse import mybir as _mybir
    from concourse.bass_utils import run_bass_kernel_spmd as _run

    nc = _bacc.Bacc("TRN2", target_bir_lowering=False, num_devices=1)
    laid = lay_out(inputs, _np)
    arrays = {f"in_{n}": a for n, a in laid.items()}
    args = {n: nc.dram_tensor(f"in_{n}", a.shape, _mybir.dt.from_np(a.dtype), kind="ExternalInput").ap()
            for n, a in laid.items()}
    out = nc.dram_tensor("out_x", (B, S, D), F32, kind="ExternalOutput").ap()
    program(nc, args, out)
    r = _run(nc, [arrays], core_ids=[0])
    return r.results[0]["out_x"]
```
